# Optimizing a Trainium2 kernel written in Bass

```python
import numpy as np
import jax
import jax.numpy as jnp

def _softmax(x, axis=-1):
    return jax.nn.softmax(x, axis=axis)

def _gelu(x):
    return jax.nn.gelu(x, approximate=True)

def _silu(x):
    return jax.nn.silu(x)

def _sigmoid(x):
    return jax.nn.sigmoid(x)

def _layernorm(x, axis=-1, eps=1e-05):
    m = jnp.mean(x, axis=axis, keepdims=True)
    v = jnp.var(x, axis=axis, keepdims=True)
    return (x - m) / jnp.sqrt(v + eps)

def _scatter_add(tgt, idx, src, axis=0):
    return tgt.at[idx].add(src)

def _segment_sum(src, seg, n):
    return jax.ops.segment_sum(src, seg, n)
kernel_name = 'mk_audio_tower_d1_tok_aud1d768_r4_1e7425'

def setup_inputs(seed: int=0):
    np.random.seed(seed)
    _w = jnp.asarray

    def _rec_inputs():
        import jax
        import jax.numpy as jnp
        _rk = jax.random.key(seed)
        x = -6.41493e-05 + 1.00002 * jax.random.normal(jax.random.fold_in(_rk, 1), (32, 40000), jnp.float32)
        return x
    x = _rec_inputs()

    def _L0_tok_setup():
        import jax, jax.numpy as jnp
        import numpy as np
        import math
        SR = 4000
        FRAME_LEN = 100
        FRAME_STEP = 160
        N_FILTERS = 40
        N_MFCC = 13
        EMBED = 192
        BATCH = 64
        AUDIO_LEN = 40000
        N_FFT_BINS = FRAME_LEN // 2 + 1

        def _mel_filterbank():
            low_mel = 2595.0 * math.log10(1.0 + 0.0 / 700.0)
            high_mel = 2595.0 * math.log10(1.0 + SR // 2 / 700.0)
            mel_points = np.linspace(low_mel, high_mel, N_FILTERS + 2)
            hz_points = 700.0 * (10.0 ** (mel_points / 2595.0) - 1.0)
            bin_points = np.floor((FRAME_LEN + 1) * hz_points / SR)
            filt = np.zeros((N_FILTERS, N_FFT_BINS), dtype=np.float32)
            for i in range(1, N_FILTERS + 1):
                l, c, r = (bin_points[i - 1], bin_points[i], bin_points[i + 1])
                for j in range(int(l), int(c)):
                    filt[i - 1, j] = (j - l) / (c - l)
                for j in range(int(c), int(r)):
                    filt[i - 1, j] = (r - j) / (r - c)
            return jnp.asarray(filt)

        def _dct_matrix():
            k = np.arange(N_MFCC)[:, None]
            j = np.arange(N_FILTERS)[None, :]
            m = np.cos(np.pi * k * (2 * j + 1) / (2 * N_FILTERS)) * math.sqrt(2.0 / N_FILTERS)
            return jnp.asarray(m.astype(np.float32))
        key = jax.random.key(seed)
        kx, kw = jax.random.split(key)
        x = jax.random.normal(kx, (BATCH, AUDIO_LEN), dtype=jnp.float32)
        bound = 1.0 / math.sqrt(N_MFCC)
        w_proj = jax.random.uniform(kw, (N_MFCC, EMBED), minval=-bound, maxval=bound, dtype=jnp.float32)
        b_proj = jnp.zeros((EMBED,), dtype=jnp.float32)
        return {'x': x, 'mel_filters': _mel_filterbank(), 'dct': _dct_matrix(), 'w_proj': w_proj, 'b_proj': b_proj}
    _L0_tok_all = _L0_tok_setup()
    _L0_tok_in = {k: v for k, v in _L0_tok_all.items() if k in ('mel_filters', 'dct', 'w_proj', 'b_proj')}
    del _L0_tok_all

    def _L0_attn_setup():
        import jax, jax.numpy as jnp
        import numpy as np
        import math
        B, L, D = (2, 512, 192)
        H, DK = (8, 64)
        DV = D // H
        N_POS = 32
        DFF = 2 * D
        EPS = 1e-05

        def _rel_basis(l: int, n: int) -> jnp.ndarray:
            pos = jnp.arange(l)
            distance = pos[None, :] - pos[:, None]
            pow_rate = jnp.exp(jnp.log(jnp.float32((l + 1) / 2.0)) / (n // 2))
            center_widths = pow_rate ** jnp.arange(1, n // 2 + 1, dtype=jnp.float32)
            d = distance[:, :, None].astype(jnp.float32)
            unsigned = (jnp.abs(d) <= center_widths).astype(jnp.float32)
            signed = jnp.sign(d) * unsigned
            return jnp.concatenate([unsigned, signed], axis=-1)

        def _rmsnorm(x, w):
            norm = jnp.mean(x * x, axis=-1, keepdims=True)
            return x * jax.lax.rsqrt(norm + EPS) * w
        key = jax.random.key(seed)
        ks = jax.random.split(key, 12)
        s = 0.02
        return {'x': jax.random.normal(ks[0], (B, L, D), jnp.float32), 'norm1_w': jnp.ones((D,), jnp.float32), 'norm2_w': jnp.ones((D,), jnp.float32), 'wq': jax.random.normal(ks[1], (D, H * DK), jnp.float32) * s, 'wk': jax.random.normal(ks[2], (D, H * DK), jnp.float32) * s, 'wv': jax.random.normal(ks[3], (D, H * DV), jnp.float32) * s, 'wo': jax.random.normal(ks[4], (H * DV, D), jnp.float32) * s, 'bo': jnp.zeros((D,), jnp.float32), 'u_param': jax.random.normal(ks[5], (H, DK), jnp.float32) * s, 'v_param': jax.random.normal(ks[6], (H, DK), jnp.float32) * s, 'w_pos': jax.random.normal(ks[7], (H, DK, N_POS), jnp.float32) * s, 'w1': jax.random.normal(ks[8], (D, DFF), jnp.float32) * s, 'b1': jnp.zeros((DFF,), jnp.float32), 'w2': jax.random.normal(ks[9], (DFF, D), jnp.float32) * s, 'b2': jnp.zeros((D,), jnp.float32)}
    _L0_attn_all = _L0_attn_setup()
    _L0_attn_in = {k: v for k, v in _L0_attn_all.items() if k in ('norm1_w', 'norm2_w', 'wq', 'wk', 'wv', 'wo', 'bo', 'u_param', 'v_param', 'w_pos', 'w1', 'b1', 'w2', 'b2')}
    del _L0_attn_all

    def _L0_ffn_setup():
        import math
        import jax, jax.numpy as jnp
        import numpy as np
        B, L, D = (8, 1024, 192)
        E = 16
        TOP_K = 2
        F_EXP = 4 * D
        F_SH = F_EXP * 2 // 4
        key = jax.random.key(seed)
        ks = jax.random.split(key, 8)
        s = lambda fan_in: 1.0 / math.sqrt(fan_in)
        return {'hidden_states': jax.random.normal(ks[0], (B, L, D), jnp.float32), 'gate_weight': jax.random.uniform(ks[1], (E, D), jnp.float32, -s(D), s(D)), 'Wg': jax.random.uniform(ks[2], (E, F_EXP, D), jnp.float32, -s(D), s(D)), 'Wu': jax.random.uniform(ks[3], (E, F_EXP, D), jnp.float32, -s(D), s(D)), 'Wd': jax.random.uniform(ks[4], (E, D, F_EXP), jnp.float32, -s(F_EXP), s(F_EXP)), 'Ws_g': jax.random.uniform(ks[5], (F_SH, D), jnp.float32, -s(D), s(D)), 'Ws_u': jax.random.uniform(ks[6], (F_SH, D), jnp.float32, -s(D), s(D)), 'Ws_d': jax.random.uniform(ks[7], (D, F_SH), jnp.float32, -s(F_SH), s(F_SH))}
    _L0_ffn_all = _L0_ffn_setup()
    _L0_ffn_in = {k: v for k, v in _L0_ffn_all.items() if k in ('gate_weight', 'Wg', 'Wu', 'Wd', 'Ws_g', 'Ws_u', 'Ws_d')}
    del _L0_ffn_all
    return {'x': x, 'L0_tok_mel_filters': _L0_tok_in['mel_filters'], 'L0_tok_dct': _L0_tok_in['dct'], 'L0_tok_w_proj': _L0_tok_in['w_proj'], 'L0_tok_b_proj': _L0_tok_in['b_proj'], 'L0_attn_norm1_w': _L0_attn_in['norm1_w'], 'L0_attn_norm2_w': _L0_attn_in['norm2_w'], 'L0_attn_wq': _L0_attn_in['wq'], 'L0_attn_wk': _L0_attn_in['wk'], 'L0_attn_wv': _L0_attn_in['wv'], 'L0_attn_wo': _L0_attn_in['wo'], 'L0_attn_bo': _L0_attn_in['bo'], 'L0_attn_u_param': _L0_attn_in['u_param'], 'L0_attn_v_param': _L0_attn_in['v_param'], 'L0_attn_w_pos': _L0_attn_in['w_pos'], 'L0_attn_w1': _L0_attn_in['w1'], 'L0_attn_b1': _L0_attn_in['b1'], 'L0_attn_w2': _L0_attn_in['w2'], 'L0_attn_b2': _L0_attn_in['b2'], 'L0_ffn_gate_weight': _L0_ffn_in['gate_weight'], 'L0_ffn_Wg': _L0_ffn_in['Wg'], 'L0_ffn_Wu': _L0_ffn_in['Wu'], 'L0_ffn_Wd': _L0_ffn_in['Wd'], 'L0_ffn_Ws_g': _L0_ffn_in['Ws_g'], 'L0_ffn_Ws_u': _L0_ffn_in['Ws_u'], 'L0_ffn_Ws_d': _L0_ffn_in['Ws_d']}

def reference(x, L0_tok_mel_filters, L0_tok_dct, L0_tok_w_proj, L0_tok_b_proj, L0_attn_norm1_w, L0_attn_norm2_w, L0_attn_wq, L0_attn_wk, L0_attn_wv, L0_attn_wo, L0_attn_bo, L0_attn_u_param, L0_attn_v_param, L0_attn_w_pos, L0_attn_w1, L0_attn_b1, L0_attn_w2, L0_attn_b2, L0_ffn_gate_weight, L0_ffn_Wg, L0_ffn_Wu, L0_ffn_Wd, L0_ffn_Ws_g, L0_ffn_Ws_u, L0_ffn_Ws_d):
    import jax
    import jax.numpy as jnp

    def _L0_tok_ref(x, mel_filters, dct, w_proj, b_proj):
        import jax, jax.numpy as jnp
        import numpy as np
        import math
        SR = 4000
        FRAME_LEN = 100
        FRAME_STEP = 160
        N_FILTERS = 40
        N_MFCC = 13
        EMBED = 192
        BATCH = 64
        AUDIO_LEN = 40000
        N_FFT_BINS = FRAME_LEN // 2 + 1

        def _mel_filterbank():
            low_mel = 2595.0 * math.log10(1.0 + 0.0 / 700.0)
            high_mel = 2595.0 * math.log10(1.0 + SR // 2 / 700.0)
            mel_points = np.linspace(low_mel, high_mel, N_FILTERS + 2)
            hz_points = 700.0 * (10.0 ** (mel_points / 2595.0) - 1.0)
            bin_points = np.floor((FRAME_LEN + 1) * hz_points / SR)
            filt = np.zeros((N_FILTERS, N_FFT_BINS), dtype=np.float32)
            for i in range(1, N_FILTERS + 1):
                l, c, r = (bin_points[i - 1], bin_points[i], bin_points[i + 1])
                for j in range(int(l), int(c)):
                    filt[i - 1, j] = (j - l) / (c - l)
                for j in range(int(c), int(r)):
                    filt[i - 1, j] = (r - j) / (r - c)
            return jnp.asarray(filt)

        def _dct_matrix():
            k = np.arange(N_MFCC)[:, None]
            j = np.arange(N_FILTERS)[None, :]
            m = np.cos(np.pi * k * (2 * j + 1) / (2 * N_FILTERS)) * math.sqrt(2.0 / N_FILTERS)
            return jnp.asarray(m.astype(np.float32))
        B, T = x.shape
        n_frames = 1 + (T - FRAME_LEN) // FRAME_STEP
        idx = jnp.arange(n_frames)[:, None] * FRAME_STEP + jnp.arange(FRAME_LEN)[None, :]
        frames = x[:, idx]
        window = 0.54 - 0.46 * jnp.cos(2.0 * jnp.pi * jnp.arange(FRAME_LEN, dtype=jnp.float32) / (FRAME_LEN - 1))
        windowed = frames * window
        fft = jnp.fft.rfft(windowed, axis=-1)
        power = fft.real ** 2 + fft.imag ** 2
        mel_energies = jnp.einsum('bnf,mf->bnm', power, mel_filters)
        log_energies = jnp.log(mel_energies + 1e-06)
        mfcc = jnp.einsum('bnm,km->bnk', log_energies, dct)
        out = mfcc @ w_proj + b_proj
        return out

    def _L0_attn_ref(x, norm1_w, norm2_w, wq, wk, wv, wo, bo, u_param, v_param, w_pos, w1, b1, w2, b2):
        import jax, jax.numpy as jnp
        import numpy as np
        import math
        B, L, D = (2, 512, 192)
        H, DK = (8, 64)
        DV = D // H
        N_POS = 32
        DFF = 2 * D
        EPS = 1e-05

        def _rel_basis(l: int, n: int) -> jnp.ndarray:
            pos = jnp.arange(l)
            distance = pos[None, :] - pos[:, None]
            pow_rate = jnp.exp(jnp.log(jnp.float32((l + 1) / 2.0)) / (n // 2))
            center_widths = pow_rate ** jnp.arange(1, n // 2 + 1, dtype=jnp.float32)
            d = distance[:, :, None].astype(jnp.float32)
            unsigned = (jnp.abs(d) <= center_widths).astype(jnp.float32)
            signed = jnp.sign(d) * unsigned
            return jnp.concatenate([unsigned, signed], axis=-1)

        def _rmsnorm(x, w):
            norm = jnp.mean(x * x, axis=-1, keepdims=True)
            return x * jax.lax.rsqrt(norm + EPS) * w
        b, l, _ = x.shape
        skip = x
        h1 = _rmsnorm(x, norm1_w)
        q = (h1 @ wq).reshape(b, l, H, DK)
        k = (h1 @ wk).reshape(b, l, H, DK)
        v = (h1 @ wv).reshape(b, l, H, DV)
        basis = _rel_basis(l, N_POS)
        scale = 1.0 / math.sqrt(DK)
        qw = jnp.einsum('bihd,hdn->bihn', q, w_pos)
        qr = jnp.einsum('bihn,ijn->bhij', qw, basis)
        uk = jnp.einsum('hd,bjhd->bhj', u_param, k)[:, :, None, :]
        vw = jnp.einsum('hd,hdn->hn', v_param, w_pos)
        vr = jnp.einsum('hn,ijn->hij', vw, basis)[None]
        bias = (qr + uk + vr) * scale
        scores = jnp.einsum('bihd,bjhd->bhij', q, k) * scale + bias
        attn = jax.nn.softmax(scores, axis=-1)
        out = jnp.einsum('bhij,bjhd->bihd', attn, v)
        out = out.reshape(b, l, H * DV) @ wo + bo
        x = out + skip
        skip = x
        h2 = _rmsnorm(x, norm2_w)
        h2 = jax.nn.gelu(h2 @ w1 + b1, approximate=False) @ w2 + b2
        return h2 + skip

    def _L0_ffn_ref(hidden_states, gate_weight, Wg, Wu, Wd, Ws_g, Ws_u, Ws_d):
        import math
        import jax, jax.numpy as jnp
        import numpy as np
        B, L, D = (8, 1024, 192)
        E = 16
        TOP_K = 2
        F_EXP = 4 * D
        F_SH = F_EXP * 2 // 4
        b, l, d = hidden_states.shape
        n = b * l
        x = hidden_states.reshape(n, d)
        scores = jax.nn.sigmoid(x @ gate_weight.T)
        capacity = math.ceil(n / E * TOP_K)
        topk_score, topk_ids = jax.lax.top_k(scores.T, capacity)
        xg = x[topk_ids]
        gate = jax.nn.silu(jnp.einsum('ecd,efd->ecf', xg, Wg))
        up = jnp.einsum('ecd,efd->ecf', xg, Wu)
        out = jnp.einsum('ecf,edf->ecd', gate * up, Wd)
        out = out * topk_score[..., None]
        y = jnp.zeros((n, d), x.dtype).at[topk_ids.reshape(-1)].add(out.reshape(-1, d))
        y = y.reshape(b, l, d)
        shared = jax.nn.silu(hidden_states @ Ws_g.T) * (hidden_states @ Ws_u.T) @ Ws_d.T
        return y + shared
    h = _L0_tok_ref(x, L0_tok_mel_filters, L0_tok_dct, L0_tok_w_proj, L0_tok_b_proj)
    h = h + _L0_attn_ref(_layernorm(h, axis=-1), L0_attn_norm1_w, L0_attn_norm2_w, L0_attn_wq, L0_attn_wk, L0_attn_wv, L0_attn_wo, L0_attn_bo, L0_attn_u_param, L0_attn_v_param, L0_attn_w_pos, L0_attn_w1, L0_attn_b1, L0_attn_w2, L0_attn_b2)
    h = h + _L0_ffn_ref(_layernorm(h, axis=-1), L0_ffn_gate_weight, L0_ffn_Wg, L0_ffn_Wu, L0_ffn_Wd, L0_ffn_Ws_g, L0_ffn_Ws_u, L0_ffn_Ws_d)
    return h

_drawn_inputs = setup_inputs


def setup_inputs(seed=0):
    import zlib

    import numpy as np

    out = dict(_drawn_inputs(seed))
    spreads = {'L0_tok_b_proj': (0.0, 0.332),
     'L0_attn_norm1_w': (1.0, 0.6),
     'L0_attn_norm2_w': (1.0, 0.6),
     'L0_attn_bo': (0.0, 0.406),
     'L0_attn_b1': (0.0, 0.8),
     'L0_attn_b2': (0.0, 0.367)}
    factors = {'L0_attn_wq': 8.0,
     'L0_attn_wk': 8.0,
     'L0_attn_wv': 3.367,
     'L0_attn_wo': 3.312,
     'L0_attn_u_param': 8.0,
     'L0_attn_v_param': 8.0,
     'L0_attn_w_pos': 8.0,
     'L0_attn_w1': 5.381,
     'L0_attn_w2': 4.87,
     'L0_ffn_gate_weight': 3.531,
     'L0_ffn_Wg': 3.28,
     'L0_ffn_Wu': 3.108,
     'L0_ffn_Wd': 3.126,
     'L0_ffn_Ws_g': 2.682,
     'L0_ffn_Ws_u': 2.952}
    for name, (base, spread) in spreads.items():
        noise = np.random.default_rng([zlib.crc32(name.encode()), seed]).standard_normal(out[name].shape)
        drawn = base * np.exp(spread * noise) if base else spread * noise
        out[name] = jnp.asarray(drawn.astype(out[name].dtype))
    for name, factor in factors.items():
        out[name] = (out[name] * factor).astype(out[name].dtype)
    return out
```

```python
import math
from contextlib import ExitStack

import numpy as np
import concourse.bass as bass
from concourse import mybir

F32 = mybir.dt.float32
ALU = mybir.AluOpType
ACT = mybir.ActivationFunctionType
AX_X = mybir.AxisListType.X

BATCH, AUDIO = 32, 40000
FRAME_LEN, FRAME_STEP = 100, 160
FRAMES = 1 + (AUDIO - FRAME_LEN) // FRAME_STEP
BINS = FRAME_LEN // 2 + 1
MELS, MFCC, D = 40, 13, 192
HEADS, DK = 8, 64
DV = D // HEADS
N_POS = 32
DFF = 2 * D
EPS = 1e-5
TOKENS = BATCH * FRAMES
EXPERTS, TOP_K = 16, 2
CAPACITY = math.ceil(TOKENS / EXPERTS * TOP_K)
F_EXP = 4 * D
F_SH = F_EXP // 2

TP = 125
NT = FRAMES // TP
KD = 96
NK = D // KD
PAIRS = HEADS // 2
RANGE = 125
ND = 2 * RANGE + 1
PITCH = 2 * FRAMES - 1
SLOTS = HEADS + 2
SCALE = 1.0 / math.sqrt(DK)
SROW = D + EXPERTS


EXP_LN = "natural_log_exp_and_others"


def dft_table():
    n = np.arange(FRAME_LEN, dtype=np.float64)
    window = 0.54 - 0.46 * np.cos(2.0 * np.pi * n / (FRAME_LEN - 1))
    angle = 2.0 * np.pi * np.outer(n, np.arange(BINS)) / FRAME_LEN
    return (np.concatenate([np.cos(angle), np.sin(angle)], 1) * window[:, None]).astype(np.float32)


def basis_table():
    half = N_POS // 2
    rate = np.exp(np.log(np.float32((FRAMES + 1) / 2.0)) / np.float32(half)).astype(np.float32)
    widths = rate ** np.arange(1, half + 1, dtype=np.float32)
    assert widths[-1] < RANGE + 1
    dist = np.arange(-RANGE, RANGE + 1).astype(np.float32)
    inside = (np.abs(dist)[None, :] <= widths[:, None]).astype(np.float32)
    return np.concatenate([inside, np.sign(dist)[None, :] * inside], 0)


def apart(eng, ready, *waits):
    waits = [(s, v if isinstance(v, int) else eng.to_reg(v)) for s, v in waits]
    eng.wait_ge(*ready)
    for s, v in waits:
        if not isinstance(v, int) or v > 0:
            eng.wait_ge(s, v)


def tower(nc, w, hx_d, bias_d, h1_d, xs_d, xnT_d, scT_d, sem, n_batch=BATCH):
    ctx = ExitStack()

    def sb(name, shape, dt=F32):
        return ctx.enter_context(nc.sbuf_tensor("sb_" + name, shape, dt))

    def pb(name, shape):
        return ctx.enter_context(nc.psum_tensor("ps_" + name, shape, F32))

    with ctx:
        ident = sb("ident", [128, 128])
        dft = sb("dft", [FRAME_LEN, 2 * BINS])
        mel = sb("mel", [2 * BINS, MELS])
        dct = sb("dct", [MELS, MFCC])
        wproj = sb("wproj", [MFCC + 1, D])
        wq = sb("wq", [KD, NK, HEADS * DK])
        wk = sb("wk", [KD, NK, HEADS * DK])
        wv = sb("wv", [KD, NK, D])
        wo = sb("wo", [KD, NK, D])
        w1 = sb("w1", [KD, NK, DFF])
        w2 = sb("w2", [128, DFF // 128, D])
        gate = sb("gate", [KD, NK, EXPERTS])
        n1w = sb("n1w", [KD, NK])
        n2w = sb("n2w", [KD, NK])
        b1 = sb("b1", [128, DFF // 128])
        ucol = sb("ucol", [128, PAIRS])
        vcol = sb("vcol", [128, PAIRS])
        wpos = sb("wpos", [N_POS, HEADS * DK])
        basis = sb("basis", [N_POS, ND])
        bb = sb("bb", [TP, NT, 2 * D])
        tiny = sb("tiny", [MELS, 1])
        power = sb("power", [TP, 2 * NT])
        zeros = sb("zeros", [TP, PITCH])
        wbz = sb("wbz", [128, HEADS, ND])
        frames = sb("frames", [FRAME_LEN, FRAMES])
        sq = sb("sq", [2 * BINS, FRAMES])
        logmel = sb("logmel", [MELS, FRAMES])
        mfcc = sb("mfcc", [MFCC + 1, FRAMES])
        hx = sb("hx", [TP, NT, 2 * D])
        t_stats = sb("t_stats", [TP, NT, 6])
        t_mv = sb("t_mv", [TP, NT, 2])
        t_inv = sb("t_inv", [TP, NT])
        t_v = sb("t_v", [TP, 2 * NT])
        t_y = sb("t_y", [TP, 2 * NT])
        h1n = sb("h1n", [TP, NT, D])
        h1T = sb("h1T", [KD, NK, FRAMES])
        qu = sb("qu", [128, PAIRS, FRAMES])
        qv = sb("qv", [128, PAIRS, FRAMES])
        kz = sb("kz", [128, HEADS, FRAMES])
        vz = sb("vz", [TP, NT, HEADS, KD])
        rsb = sb("rsb", [TP, 2, NT, ND])
        bsk = sb("bsk", [TP, 4, NT, FRAMES])
        ssb = sb("ssb", [TP, 2, NT, FRAMES])
        prob = sb("prob", [TP, 2, NT, FRAMES])
        mx = sb("mx", [TP, 2, NT])
        rs = sb("rs", [TP, 2, NT])
        rinv = sb("rinv", [TP, 2, NT])
        ptsb = sb("ptsb", [TP, 2, NT, FRAMES])
        otsb = sb("otsb", [KD, NK, FRAMES])
        hxl = sb("hxl", [TP, NT, 2 * D])
        x1 = sb("x1", [TP, NT, D])
        xb = sb("xb", [TP, NT, D])
        junk = sb("junk", [TP, D])
        ss = sb("ss", [TP, NT])
        c_v = sb("c_v", [TP, NT])
        c_y = sb("c_y", [TP, NT])
        h2n = sb("h2n", [TP, NT, D])
        h2T = sb("h2T", [KD, NK, FRAMES])
        gT = sb("gT", [128, DFF // 128, FRAMES])
        h1 = sb("h1", [TP, NT, D])
        c_stats = sb("c_stats", [TP, NT, 6])
        c_mv = sb("c_mv", [TP, NT, 2])
        d_v = sb("d_v", [TP, NT])
        d_y = sb("d_y", [TP, NT])
        xs = sb("xs", [TP, NT, SROW])
        xnT = sb("xnT", [KD, NK, FRAMES])
        sige = sb("sige", [TP, NT, EXPERTS])
        scT = sb("scT", [EXPERTS, FRAMES])
        sps = [pb(f"sps{i}", [TP, NT, FRAMES]) for i in range(2)]
        ptps = pb("ptps", [TP, NT, FRAMES])
        otps = pb("otps", [KD, NK, FRAMES])
        qps = [pb(f"qps{i}", [128, 512]) for i in range(2)]
        tps = pb("tps", [128, 512])
        cps = pb("cps", [128, 512])

        w_ld = sem("w_ld")
        READY = (w_ld, W_LOADS)
        z_set = sem("z_set")
        zero_st = sem("zero_st")
        wb_mm = sem("wb_mm")
        wb_ev = sem("wb_ev")
        fr_ld = sem("fr_ld")
        t_mm = sem("t_mm")
        t_ev = sem("t_ev")
        t_ch = sem("t_ch")
        hx_st = sem("hx_st")
        q_mm = sem("q_mm")
        q_ev = [sem(f"q_ev{i}") for i in range(2)]
        r_st = [sem(f"r_st{i}") for i in range(2)]
        bsk_ld = [sem(f"bsk_ld{i}") for i in range(4)]
        s_mm = sem("s_mm")
        s_add = sem("s_add")
        p_exp = sem("p_exp")
        r_inv = sem("r_inv")
        p_nrm = sem("p_nrm")
        pt_mm = sem("pt_mm")
        pt_ev = sem("pt_ev")
        pv_mm = sem("pv_mm")
        ot_ev = sem("ot_ev")
        hxl_ld = sem("hxl_ld")
        c_hb = sem("c_hb")
        c_mm = sem("c_mm")
        c_ev = sem("c_ev")
        c_ch = sem("c_ch")
        c_xb = sem("c_xb")
        d_ch = sem("d_ch")
        c_sg = sem("c_sg")
        c_st = sem("c_st")

        T_USES, C_USES, Q_USES = 5, 8, 14
        T_CHAIN, C_CHAIN, D_CHAIN = 13, 6, 8
        QK_SLOT = {1: 0, 3: 1, 5: 2, 7: 3}
        R_SLOT = {s: s - 2 for s in range(2, 10)}
        QK_USE = [0, 3, 6, 9]
        R_USE = [1, 2, 4, 5, 7, 8, 10, 11]
        V_USE = [12, 13]

        def wait(eng, s, value):
            if not isinstance(value, int) or value > 0:
                eng.wait_ge(s, value)

        def q_freed(eng, b, use):
            wait(eng, q_ev[use % 2], 2 * (Q_USES // 2 * b + use // 2))

        def q_evacuated(eng, b, use):
            wait(eng, q_ev[use % 2], 2 * (Q_USES // 2 * b + use // 2 + 1))

        def rounds(eng, body):
            last = n_batch - 1

            def at(i):
                return [(i - j) if 0 <= i - j <= last else None for j in range(4)]

            head = min(3, n_batch + 3)
            for i in range(head):
                body(*at(i))
            if n_batch > 3:
                with eng.Fori(3, n_batch) as i:
                    body(i, i - 1, i - 2, i - 3)
            for i in range(max(head, n_batch), n_batch + 3):
                body(*at(i))

        def bank2(ps, n, rows):
            return ps[0:rows, 0:2 * n].rearrange("p (t n) -> p t n", t=2)

        block = ctx.enter_context(nc.Block())

        @block.sync
        def _(sp):
            loads = [
                (ident[:], w["ident"]), (dft[:], w["dft"]), (mel[0:BINS], w["melT"]),
                (mel[BINS:2 * BINS], w["melT"]), (dct[:], w["dctT"]),
                (wproj[0:MFCC], w["w_proj"]), (wproj[MFCC:MFCC + 1], w["b_proj"]),
                (wq[:], w["wq"].rearrange("(k p) n -> p k n", p=KD)),
                (wk[:], w["wk"].rearrange("(k p) n -> p k n", p=KD)),
                (wv[:], w["wv"].rearrange("(k p) n -> p k n", p=KD)),
                (wo[:], w["wo"].rearrange("(k p) n -> p k n", p=KD)),
                (w1[:], w["w1"].rearrange("(k p) n -> p k n", p=KD)),
                (w2[:], w["w2"].rearrange("(k p) n -> p k n", p=128)),
                (gate[:], w["gateT"].rearrange("(k p) n -> p k n", p=KD)),
                (n1w[:], w["n1w"]), (n2w[:], w["n2w"]), (b1[:], w["b1"]),
                (ucol[:], w["u"]), (vcol[:], w["v"]), (wpos[:], w["w_posT"]), (basis[:], w["basis"]),
            ]
            for t in range(NT):
                loads += [(bb[:, t, 0:D], w["b2"].partition_broadcast(TP)),
                          (bb[:, t, D:2 * D], w["bo"].partition_broadcast(TP))]
            for dst, src in loads:
                sp.dma_start(dst, src).then_inc(w_ld, 16)
            sp.wait_ge(z_set, 1)
            for h in range(HEADS):
                for t in range(NT):
                    sp.dma_start(bias_d[h, t * TP:(t + 1) * TP, :], zeros[:]).then_inc(zero_st, 16)

            def body(bt, bq, bb_, bc):
                for s in range(SLOTS):
                    if bt is not None and s == 0:
                        wait(sp, t_mm, T_USES * bt - 4)
                        sp.dma_start(frames[:], w["frames"][:, bass.ds(bt * FRAMES, FRAMES)]).then_inc(fr_ld, 16)
                    if bt is not None and s == 7:
                        wait(sp, t_ch, T_CHAIN * bt + 11)
                        sp.dma_start(hx_d[bass.ds(bt * FRAMES, FRAMES), :].rearrange("(t p) n -> p t n", p=TP), hx[:]).then_inc(hx_st, 16)
                    if bb_ is not None and s + 2 < HEADS:
                        load_bias(bb_, s + 2)
                    if bq is not None and s in R_SLOT:
                        h = R_SLOT[s]
                        q_evacuated(sp, bq, R_USE[h])
                        wait(sp, bsk_ld[h % 4], 16 * (2 * (bq - 1) + h // 4 + 1))
                        if isinstance(bq, int) and bq == 0 and h == 0:
                            sp.wait_ge(zero_st, 16 * HEADS * NT)
                        dst = bias_d[h, :, FRAMES - 1 - RANGE:FRAMES + RANGE].rearrange("(t p) n -> p t n", p=TP)
                        sp.dma_start(dst, rsb[:, h % 2]).then_inc(r_st[h % 2], 16)
                    if bq is not None and s >= 8:
                        load_bias(bq, s - 8)
                    if bc is not None and s == 9:
                        sl = bass.ds(bc * FRAMES, FRAMES)
                        wait(sp, c_ev, C_USES * bc + 8)
                        sp.dma_start(h1_d[sl, :].rearrange("(t p) n -> p t n", p=TP), h1[:]).then_inc(c_st, 16)
                        sp.dma_start(xnT_d[:, sl].rearrange("(k p) n -> p k n", p=KD), xnT[:]).then_inc(c_st, 16)
                        sp.dma_start(xs_d[sl, :].rearrange("(t p) n -> p t n", p=TP), xs[:]).then_inc(c_st, 16)
                        sp.dma_start(scT_d[:, sl], scT[:]).then_inc(c_st, 16)
                    if bb_ is not None and s == 9:
                        apart(sp, READY, (hx_st, 16 * (bb_ + 1)), (c_xb, bb_))
                        sp.dma_start(hxl[:], hx_d[bass.ds(bb_ * FRAMES, FRAMES), :].rearrange("(t p) n -> p t n", p=TP)).then_inc(hxl_ld, 16)

            def load_bias(b, h):
                wait(sp, r_st[h % 2], 16 * (4 * b + h // 2 + 1))
                wait(sp, s_add, 2 * (HEADS * b + h - 4) + 2)
                base = bias_d[h, 0:1, FRAMES - 1:FRAMES]
                src = bass.AP(base.tensor, base.offset, [[PITCH - 1, TP], [(PITCH - 1) * TP, NT], [1, FRAMES]])
                sp.dma_start(bsk[:, h % 4], src).then_inc(bsk_ld[h % 4], 16)

            rounds(sp, body)
            sp.wait_ge(c_st, 64 * n_batch)
            sp.wait_ge(hx_st, 16 * n_batch)

        @block.gpsimd
        def _(pool):
            g = nc.gpsimd
            g.memset(zeros[:], 0.0).then_inc(z_set, 1)
            g.memset(mfcc[:], 1.0).then_inc(z_set, 1)
            g.memset(kz[:], 0.0).then_inc(z_set, 1)
            g.memset(vz[:], 0.0).then_inc(z_set, 1)
            g.memset(wbz[:], 0.0).then_inc(z_set, 1)
            g.memset(tiny[:], 1e-6).then_inc(z_set, 1)
            g.memset(power[:], -0.5).then_inc(z_set, 1)
            pool.wait_ge(w_ld, W_LOADS)
            pool.wait_ge(z_set, 7)

            def body(bt, bq, bb_, bc):
                for s in range(SLOTS):
                    if bc is not None and s == 0:
                        pool.wait_ge(hxl_ld, 16 * (bc + 1))
                        g.tensor_tensor(hxl[:], hxl[:], bb[:], ALU.add).then_inc(c_hb, 1)
                    if bt is not None and s == 4:
                        pool.wait_ge(t_ch, T_CHAIN * bt + 8)
                        g.tensor_tensor(t_y[:], t_v[:], power[:], ALU.pow).then_inc(t_ch, 1)
                    if bc is not None and s == 1:
                        pool.wait_ge(c_ch, C_CHAIN * bc + 3)
                        g.tensor_tensor(c_y[:], c_v[:], power[:, 0:NT], ALU.pow).then_inc(c_ch, 1)
                        g.tensor_tensor(xb[:], x1[:], hxl[:, :, 0:D], ALU.add).then_inc(c_xb, 1)
                    if bc is not None and s == 5:
                        pool.wait_ge(d_ch, D_CHAIN * bc + 5)
                        g.tensor_tensor(d_y[:], d_v[:], power[:, 0:NT], ALU.pow).then_inc(d_ch, 1)

            rounds(pool, body)

        @block.scalar
        def _(act):
            a = nc.scalar
            a.preload_act_table_set(EXP_LN)
            act.wait_ge(w_ld, W_LOADS)
            act.wait_ge(z_set, 7)

            def body(bt, bq, bb_, bc):
                for s in range(SLOTS):
                    if bb_ is not None and s < HEADS:
                        n = HEADS * bb_ + s
                        for t in range(NT):
                            act.wait_ge(s_add, 2 * n + t + 1)
                            if t == 0:
                                wait(act, pt_mm, n - 1)
                            a.activation(prob[:, s % 2, t], ssb[:, s % 2, t], ACT.Exp, bias=mx[:, s % 2, t:t + 1],
                                         scale=-1.0, accum_out=rs[:, s % 2, t:t + 1]).then_inc(p_exp, 1)
                    if bt is not None and s == 1:
                        act.wait_ge(t_mm, T_USES * bt + 1)
                        a.activation(sq[:], tps[0:2 * BINS, 0:FRAMES], ACT.Square).then_inc(t_ev, 1)
                    if bt is not None and s == 2:
                        act.wait_ge(t_mm, T_USES * bt + 2)
                        a.activation(logmel[:], tps[0:MELS, 0:FRAMES], ACT.Ln, bias=tiny[:, 0:1]).then_inc(t_ev, 1)
                    if bt is not None and s == 3:
                        act.wait_ge(t_mm, T_USES * bt + 3)
                        a.activation(mfcc[0:MFCC], tps[0:MFCC, 0:FRAMES], ACT.Copy).then_inc(t_ev, 1)
                    if bt is not None and s == 4:
                        act.wait_ge(t_mm, T_USES * bt + 4)
                        wait(act, hx_st, 16 * bt)
                        a.activation(hx[:, :, 0:D], bank2(tps, D, TP), ACT.Copy).then_inc(t_ev, 1)
                    if bq is not None and s in R_SLOT:
                        h = R_SLOT[s]
                        act.wait_ge(q_mm, Q_USES * bq + R_USE[h] + 1)
                        wait(act, r_st[h % 2], 16 * (4 * bq + h // 2))
                        a.activation(rsb[:, h % 2], bank2(qps[R_USE[h] % 2], ND, TP), ACT.Copy).then_inc(q_ev[R_USE[h] % 2], 2)
                    if bq is not None and s in QK_SLOT:
                        p = QK_SLOT[s]
                        act.wait_ge(q_mm, Q_USES * bq + QK_USE[p] + 1)
                        ps = bank2(qps[QK_USE[p] % 2], FRAMES, 128)
                        wait(act, s_mm, HEADS * (bq - 1) + 2 * p + 2)
                        a.activation(qu[:, p], ps[:, 0], ACT.Identity, bias=ucol[:, p:p + 1])
                        a.activation(qv[:, p], ps[:, 0], ACT.Identity, bias=vcol[:, p:p + 1])
                        a.activation(kz[0:64, 2 * p], ps[0:64, 1], ACT.Copy)
                        a.activation(kz[64:128, 2 * p + 1], ps[64:128, 1], ACT.Copy).then_inc(q_ev[QK_USE[p] % 2], 2)
                    if bc is not None and s == 0:
                        b0 = C_CHAIN * bc
                        act.wait_ge(c_ev, C_USES * bc + 1)
                        a.activation(junk[:], x1[:, 0], ACT.Square, accum_out=ss[:, 0:1]).then_inc(c_ch, 1)
                        act.wait_ge(c_ch, b0 + 1)
                        a.activation(junk[:], x1[:, 1], ACT.Square, accum_out=ss[:, 1:2]).then_inc(c_ch, 1)
                    if bc is not None and s == 3:
                        for use, ms in ((3, (0, 1)), (4, (2,))):
                            act.wait_ge(c_mm, C_USES * bc + use)
                            ps = bank2(cps, FRAMES, 128)
                            for m in ms:
                                ins = a.activation(gT[:, m], ps[:, m % 2], ACT.Gelu, bias=b1[:, m:m + 1])
                            ins.then_inc(c_ev, 1)
                        a.preload_act_table_set(EXP_LN)
                    if bc is not None and s == 7:
                        act.wait_ge(c_mm, C_USES * bc + 7)
                        a.activation(sige[:], cps[0:TP, 0:NT * EXPERTS].rearrange("p (t n) -> p t n", t=NT), ACT.Exp, scale=-1.0).then_inc(c_ev, 1)

            rounds(act, body)

        @block.vector
        def _(dve):
            v = nc.vector
            dve.wait_ge(w_ld, W_LOADS)
            dve.wait_ge(z_set, 7)
            for p in range(PAIRS):
                dve.wait_ge(wb_mm, p + 1)
                for i in range(2):
                    v.tensor_copy(wbz[64 * i:64 * i + 64, 2 * p + i], qps[p % 2][64 * i:64 * i + 64, 0:ND]).then_inc(wb_ev, 1)

            def body(bt, bq, bb_, bc):
                for s in range(SLOTS):
                    if bb_ is not None and s < HEADS:
                        n = HEADS * bb_ + s
                        apart(dve, READY, (s_mm, n + 1), (bsk_ld[s % 4], 16 * (2 * bb_ + s // 4 + 1)),
                              (p_exp, 2 * (n - 1)))
                        for t in range(NT):
                            v.tensor_tensor_reduce(out=ssb[:, s % 2, t], in0=sps[s % 2][:, t], in1=bsk[:, s % 4, t],
                                                   scale=-SCALE, scalar=3.0e38, op0=ALU.add, op1=ALU.min,
                                                   accum_out=mx[:, s % 2, t:t + 1]).then_inc(s_add, 1)
                        dve.wait_ge(p_exp, 2 * n + 2)
                        v.reciprocal(rinv[:, s % 2], rs[:, s % 2]).then_inc(r_inv, 1)
                        dve.wait_ge(r_inv, n + 1)
                        for t in range(NT):
                            v.tensor_scalar(prob[:, s % 2, t], prob[:, s % 2, t], rinv[:, s % 2, t:t + 1], None, ALU.mult).then_inc(p_nrm, 1)
                    if bq is not None and s == 9:
                        for t in range(NT):
                            dve.wait_ge(q_mm, Q_USES * bq + V_USE[t] + 1)
                            if t == 0:
                                wait(dve, pv_mm, HEADS * bq)
                            for i in range(NK):
                                base = vz[:, t, i * 4, 0:DV]
                                dst = bass.AP(base.tensor, base.offset, [base.ap[0], [KD + DV, 4], [1, DV]])
                                src = qps[V_USE[t] % 2][0:TP, i * KD:(i + 1) * KD].rearrange("p (h n) -> p h n", h=4)
                                v.tensor_copy(dst, src).then_inc(q_ev[V_USE[t] % 2], 1)
                    if bt is not None and s == 4:
                        b0 = T_CHAIN * bt
                        dve.wait_ge(t_ev, T_USES * bt + 4)
                        for t in range(NT):
                            v.bn_stats(t_stats[:, t], hx[:, t, 0:D]).then_inc(t_ch, 1)
                        apart(dve, READY, (t_ch, b0 + 2))
                        for t in range(NT):
                            v.bn_aggr(t_mv[:, t], t_stats[:, t]).then_inc(t_ch, 1)
                        dve.wait_ge(t_ch, b0 + 4)
                        v.tensor_scalar(t_v[:, 0:NT], t_mv[:, :, 1], EPS, None, ALU.add).then_inc(t_ch, 1)
                        dve.wait_ge(t_ch, b0 + 5)
                        v.reciprocal(t_inv[:], t_v[:, 0:NT]).then_inc(t_ch, 1)
                        dve.wait_ge(t_ch, b0 + 6)
                        v.tensor_tensor(t_inv[:], t_inv[:], t_mv[:, :, 1], ALU.mult).then_inc(t_ch, 1)
                        dve.wait_ge(t_ch, b0 + 7)
                        v.tensor_scalar(t_v[:, NT:2 * NT], t_inv[:], EPS, None, ALU.add).then_inc(t_ch, 1)
                    if bt is not None and s == 9:
                        dve.wait_ge(t_mm, T_USES * bt + 5)
                        if bq is not None:
                            dve.wait_ge(q_mm, Q_USES * (bq + 1))
                        ps = bank2(tps, FRAMES, KD)
                        v.tensor_scalar(h1T[:, 0], ps[:, 0], n1w[:, 0:1], None, ALU.mult)
                        v.tensor_scalar(h1T[:, 1], ps[:, 1], n1w[:, 1:2], None, ALU.mult).then_inc(t_ev, 1)
                    if bb_ is not None and s == 9:
                        dve.wait_ge(pv_mm, HEADS * (bb_ + 1))
                        wait(dve, c_mm, C_USES * (bb_ - 1) + 1)
                        v.tensor_copy(otsb[:], otps[:]).then_inc(ot_ev, 1)
                    if bc is not None and s == 0:
                        dve.wait_ge(c_mm, C_USES * bc + 1)
                        dve.wait_ge(c_hb, bc + 1)
                        v.tensor_tensor(x1[:], bank2(cps, D, TP), hxl[:, :, D:2 * D], ALU.add).then_inc(c_ev, 1)
                    if bc is not None and s == 1:
                        dve.wait_ge(c_ch, C_CHAIN * bc + 2)
                        v.tensor_scalar(c_v[:], ss[:], 1.0 / D, EPS, ALU.mult, ALU.add).then_inc(c_ch, 1)
                        dve.wait_ge(c_ch, C_CHAIN * bc + 4)
                        for t in range(NT):
                            v.tensor_scalar(h2n[:, t], x1[:, t], c_y[:, t:t + 1], None, ALU.mult).then_inc(c_ch, 1)
                    if bc is not None and s == 2:
                        dve.wait_ge(c_mm, C_USES * bc + 2)
                        ps = bank2(cps, FRAMES, KD)
                        v.tensor_scalar(h2T[:, 0], ps[:, 0], n2w[:, 0:1], None, ALU.mult)
                        v.tensor_scalar(h2T[:, 1], ps[:, 1], n2w[:, 1:2], None, ALU.mult).then_inc(c_ev, 1)
                    if bc is not None and s == 4:
                        b0 = D_CHAIN * bc
                        dve.wait_ge(c_mm, C_USES * bc + 5)
                        dve.wait_ge(c_xb, bc + 1)
                        wait(dve, c_st, 64 * bc)
                        v.tensor_tensor(h1[:], bank2(cps, D, TP), xb[:], ALU.add).then_inc(c_ev, 1)
                        dve.wait_ge(c_ev, C_USES * bc + 5)
                        for t in range(NT):
                            v.bn_stats(c_stats[:, t], h1[:, t]).then_inc(d_ch, 1)
                        apart(dve, READY, (d_ch, b0 + 2))
                        for t in range(NT):
                            v.bn_aggr(c_mv[:, t], c_stats[:, t]).then_inc(d_ch, 1)
                        dve.wait_ge(d_ch, b0 + 4)
                        v.tensor_scalar(d_v[:], c_mv[:, :, 1], EPS, None, ALU.add).then_inc(d_ch, 1)
                    if bc is not None and s == 5:
                        b0 = D_CHAIN * bc
                        wait(dve, c_st, 64 * bc)
                        dve.wait_ge(d_ch, b0 + 6)
                        for t in range(NT):
                            v.tensor_scalar(xs[:, t, 0:D], h1[:, t], c_mv[:, t, 0:1], d_y[:, t:t + 1], ALU.subtract, ALU.mult).then_inc(d_ch, 1)
                    if bt is not None and s == 5:
                        b0 = T_CHAIN * bt
                        wait(dve, hx_st, 16 * bt)
                        dve.wait_ge(t_ch, b0 + 9)
                        for t in range(NT):
                            v.tensor_scalar(hx[:, t, D:2 * D], hx[:, t, 0:D], t_mv[:, t, 0:1], t_y[:, t:t + 1], ALU.subtract, ALU.mult).then_inc(t_ch, 1)
                        for t in range(NT):
                            dve.wait_ge(t_ch, b0 + 10 + t)
                            v.tensor_scalar(h1n[:, t], hx[:, t, D:2 * D], t_y[:, NT + t:NT + t + 1], None, ALU.mult).then_inc(t_ch, 1)
                    if bc is not None and s == 6:
                        dve.wait_ge(c_mm, C_USES * bc + 6)
                        v.tensor_copy(xnT[:], bank2(cps, FRAMES, KD)).then_inc(c_ev, 1)
                    if bc is not None and s == 7:
                        dve.wait_ge(c_ev, C_USES * bc + 7)
                        v.tensor_scalar(sige[:], sige[:], 1.0, None, ALU.add).then_inc(c_sg, 1)
                        dve.wait_ge(c_sg, 2 * bc + 1)
                        v.reciprocal(xs[:, :, D:SROW], sige[:]).then_inc(c_sg, 1)
                    if bc is not None and s == 8:
                        dve.wait_ge(c_mm, C_USES * bc + 8)
                        v.tensor_copy(scT[:], cps[0:EXPERTS, 0:FRAMES]).then_inc(c_ev, 1)
                    if bb_ is not None and 1 <= s <= HEADS:
                        n = HEADS * bb_ + s - 1
                        dve.wait_ge(pt_mm, n + 1)
                        wait(dve, pv_mm, n - 1)
                        v.tensor_copy(ptsb[:, (s - 1) % 2], ptps[:]).then_inc(pt_ev, 1)

            rounds(dve, body)

        @block.tensor
        def _(pe):
            m = nc.tensor.matmul
            pe.wait_ge(w_ld, W_LOADS)
            for p in range(PAIRS):
                if p >= 2:
                    pe.wait_ge(wb_ev, 2 * (p - 1))
                m(qps[p % 2][:, 0:ND], wpos[:, p * 128:(p + 1) * 128], basis[:], start=True, stop=True).then_inc(wb_mm, 1)
            pe.wait_ge(wb_ev, 2 * PAIRS)
            pe.wait_ge(z_set, 7)

            def transposes(ps, src, s):
                for k in range(NK):
                    for t in range(NT):
                        ins = nc.tensor.transpose(ps[:, k, t * TP:(t + 1) * TP], src[:, t, k * KD:(k + 1) * KD], ident[0:TP, 0:TP])
                ins.then_inc(s, 1)

            def natural(ps, lhsT, rhs, s):
                nk = rhs.shape[1]
                for t in range(NT):
                    for k in range(nk):
                        ins = m(ps[:, t], lhsT[:, k, t * TP:(t + 1) * TP], rhs[:, k], start=k == 0, stop=k == nk - 1)
                ins.then_inc(s, 1)

            def body(bt, bq, bb_, bc):
                for s in range(SLOTS):
                    if bb_ is not None and s < HEADS:
                        n = HEADS * bb_ + s
                        if s % 2 == 0:
                            q_evacuated(pe, bb_, QK_USE[s // 2])
                        wait(pe, s_add, 2 * (n - 1))
                        for t in range(NT):
                            ins = m(sps[s % 2][:, t], qu[:, s // 2, t * TP:(t + 1) * TP], kz[:, s], start=True, stop=True)
                        ins.then_inc(s_mm, 1)
                    if bt is not None and 1 <= s <= 4:
                        apart(pe, READY, (t_ev, T_USES * bt + s - 1))
                        if s == 1:
                            pe.wait_ge(fr_ld, 16 * (bt + 1))
                            m(tps[0:2 * BINS, 0:FRAMES], dft[:], frames[:], start=True, stop=True).then_inc(t_mm, 1)
                        if s == 2:
                            m(tps[0:MELS, 0:FRAMES], mel[:], sq[:], start=True, stop=True).then_inc(t_mm, 1)
                        if s == 3:
                            m(tps[0:MFCC, 0:FRAMES], dct[:], logmel[:], start=True, stop=True).then_inc(t_mm, 1)
                        if s == 4:
                            ps = bank2(tps, D, TP)
                            for t in range(NT):
                                ins = m(ps[:, t], mfcc[:, t * TP:(t + 1) * TP], wproj[:], start=True, stop=True)
                            ins.then_inc(t_mm, 1)
                    if bq is not None and s in R_SLOT:
                        h = R_SLOT[s]
                        q_freed(pe, bq, R_USE[h])
                        if h % 2 == 0:
                            q_evacuated(pe, bq, QK_USE[h // 2])
                        ps = bank2(qps[R_USE[h] % 2], ND, TP)
                        for t in range(NT):
                            ins = m(ps[:, t], qv[:, h // 2, t * TP:(t + 1) * TP], wbz[:, h], start=True, stop=True)
                        ins.then_inc(q_mm, 1)
                    if bq is not None and s in QK_SLOT:
                        p = QK_SLOT[s]
                        q_freed(pe, bq, QK_USE[p])
                        if p == 0:
                            pe.wait_ge(t_ev, T_USES * (bq + 1))
                        ps = bank2(qps[QK_USE[p] % 2], FRAMES, 128)
                        for i, wt in enumerate((wq, wk)):
                            for k in range(NK):
                                ins = m(ps[:, i], wt[:, k, p * 128:(p + 1) * 128], h1T[:, k], start=k == 0, stop=k == NK - 1)
                        ins.then_inc(q_mm, 1)
                    if bc is not None and s == 0:
                        wait(pe, c_ev, C_USES * bc)
                        pe.wait_ge(ot_ev, bc + 1)
                        natural(bank2(cps, D, TP), otsb, wo, c_mm)
                    if bc is not None and s == 2:
                        pe.wait_ge(c_ch, C_CHAIN * bc + C_CHAIN)
                        pe.wait_ge(c_ev, C_USES * bc + 1)
                        transposes(bank2(cps, FRAMES, KD), h2n, c_mm)
                    if bc is not None and s == 3:
                        pe.wait_ge(c_ev, C_USES * bc + 2)
                        ps = bank2(cps, FRAMES, 128)
                        for j in range(2):
                            for k in range(NK):
                                ins = m(ps[:, j], w1[:, k, j * 128:(j + 1) * 128], h2T[:, k], start=k == 0, stop=k == NK - 1)
                        ins.then_inc(c_mm, 1)
                    if bc is not None and s == 4:
                        pe.wait_ge(c_ev, C_USES * bc + 4)
                        natural(bank2(cps, D, TP), gT, w2, c_mm)
                    if bc is not None and s == 6:
                        pe.wait_ge(d_ch, D_CHAIN * bc + D_CHAIN)
                        pe.wait_ge(c_ev, C_USES * bc + 5)
                        transposes(bank2(cps, FRAMES, KD), xs[:, :, 0:D], c_mm)
                    if bc is not None and s == 7:
                        pe.wait_ge(c_ev, C_USES * bc + 6)
                        natural(cps[0:TP, 0:NT * EXPERTS].rearrange("p (t n) -> p t n", t=NT), xnT, gate, c_mm)
                    if bc is not None and s == 8:
                        pe.wait_ge(c_sg, 2 * bc + 2)
                        for t in range(NT):
                            ins = nc.tensor.transpose(cps[0:EXPERTS, t * TP:(t + 1) * TP], xs[:, t, D:SROW], ident[0:TP, 0:TP])
                        ins.then_inc(c_mm, 1)
                    if bb_ is not None and 1 <= s <= HEADS:
                        n = HEADS * bb_ + s - 1
                        pe.wait_ge(p_nrm, 2 * n + 2)
                        wait(pe, pt_ev, n)
                        for j in range(NT):
                            for t in range(NT):
                                ins = nc.tensor.transpose(ptps[:, j, t * TP:(t + 1) * TP], prob[:, (s - 1) % 2, t, j * TP:(j + 1) * TP], ident[0:TP, 0:TP])
                        ins.then_inc(pt_mm, 1)
                    if bb_ is not None and s >= 2:
                        h = s - 2
                        n = HEADS * bb_ + h
                        if h == 0:
                            q_evacuated(pe, bb_, V_USE[0])
                            q_evacuated(pe, bb_, V_USE[1])
                            wait(pe, ot_ev, bb_)
                        pe.wait_ge(pt_ev, n + 1)
                        for j in range(NT):
                            ins = m(otps[:, h // 4], vz[:, j, h], ptsb[:, h % 2, j], start=h % 4 == 0 and j == 0, stop=h % 4 == 3 and j == NT - 1)
                        ins.then_inc(pv_mm, 1)
                    if bq is not None and s == 9:
                        for t in range(NT):
                            q_freed(pe, bq, V_USE[t])
                            for k in range(NK):
                                ins = m(qps[V_USE[t] % 2][0:TP, 0:D], h1T[:, k, t * TP:(t + 1) * TP], wv[:, k], start=k == 0, stop=k == NK - 1)
                            ins.then_inc(q_mm, 1)
                    if bt is not None and s == 9:
                        pe.wait_ge(t_ch, T_CHAIN * bt + T_CHAIN)
                        pe.wait_ge(t_ev, T_USES * bt + 4)
                        transposes(bank2(tps, FRAMES, KD), h1n, t_mm)
                    if bc is not None and s == 3:
                        pe.wait_ge(c_ev, C_USES * bc + 3)
                        ps = bank2(cps, FRAMES, 128)
                        for k in range(NK):
                            ins = m(ps[:, 0], w1[:, k, 256:384], h2T[:, k], start=k == 0, stop=k == NK - 1)
                        ins.then_inc(c_mm, 1)

            rounds(pe, body)


W_LOADS = 16 * (21 + 2 * NT)

BF16 = mybir.dt.bfloat16
I32 = mybir.dt.int32
U32 = mybir.dt.uint32

CHUNK = 500
CHUNKS = TOKENS // CHUNK
CT = CHUNK // TP
MS = F_SH // 128
SPLIT = 128 // EXPERTS
SPAN = TOKENS // SPLIT
BLOCKS = SPAN // TP
SCORE_BITS = 30
LO = 32


def expert_blocks():
    p = np.arange(128)
    return (p[:, None] // SPLIT == p[None, :] // SPLIT).astype(np.float32)


def expert_before():
    p = np.arange(128)
    return expert_blocks() * (p[:, None] < p[None, :]).astype(np.float32)


def shared_and_route(nc, w, h1_d, xnT_d, scT_d, out_d, hi_all, lo_all, sem):
    ctx = ExitStack()

    def sb(name, shape, dt=F32):
        return ctx.enter_context(nc.sbuf_tensor("sh_" + name, shape, dt))

    def pb(name, shape):
        return ctx.enter_context(nc.psum_tensor("shp_" + name, shape, F32))

    with ctx:
        ident = sb("ident", [128, 128])
        wg = sb("wg", [KD, NK, F_SH])
        wu = sb("wu", [KD, NK, F_SH])
        wd = sb("wd", [128, MS, D])
        blocks = sb("blocks", [128, 128])
        before = sb("before", [128, 128])
        xT = sb("xT", [KD, 2, NK, CHUNK])
        res = sb("res", [TP, 2, CT, D])
        sg = sb("sg", [128, 2, CHUNK])
        hT = sb("hT", [128, MS, CHUNK])
        y = sb("y", [TP, 2, CT, D])
        sc = sb("sc", [128, SPAN])
        hit = sb("hit", [128, SPAN])
        eq = sb("eq", [128, SPAN])
        run = sb("run", [128, SPAN])
        zero = sb("zero", [128, SPAN])
        thr = sb("thr", [128, 1], I32)
        bit = sb("bit", [128, 1], I32)
        cand = sb("cand", [128, 1], I32)
        take = sb("take", [128, 1], I32)
        cnt = sb("cnt", [128, 1])
        need = sb("need", [128, 1])
        off = sb("off", [128, 1])
        posi = sb("posi", [TP, BLOCKS, 128], I32)
        gps = [pb(f"g{i}", [128, CHUNK]) for i in range(2)]
        ups = [pb(f"u{i}", [128, CHUNK]) for i in range(2)]
        dps = [pb(f"d{i}", [TP, 2, D]) for i in range(2)]
        kps = pb("k", [128, 1])
        pps = pb("p", [TP, BLOCKS // 2, 128])

        w_ld = sem("sh_w_ld")
        sc_ld = sem("sh_sc_ld")
        ini = sem("sh_ini")
        x_ld = [sem(f"sh_x_ld{i}") for i in range(2)]
        gu_mm = sem("sh_gu_mm")
        g_ev = sem("sh_g_ev")
        h_ev = sem("sh_h_ev")
        d_mm = sem("sh_d_mm")
        y_ev = sem("sh_y_ev")
        y_st = [sem(f"sh_y_st{i}") for i in range(2)]
        k_cnt = sem("sh_k_cnt")
        k_mm = sem("sh_k_mm")
        k_ch = sem("sh_k_ch")
        r_ch = sem("sh_r_ch")
        r_mm = sem("sh_r_mm")
        K_CHAIN = 3

        def wait(eng, s, value):
            if not isinstance(value, int) or value > 0:
                eng.wait_ge(s, value)

        def chunks(eng, body):
            for i in range(2):
                body(i, i)
            with eng.Fori(1, CHUNKS // 2) as j:
                for i in range(2):
                    body(2 * j + i, i)

        block = ctx.enter_context(nc.Block())

        @block.sync
        def _(sp):
            sp.dma_start(sc[:], scT_d.rearrange("e (c n) -> (e c) n", n=SPAN)).then_inc(sc_ld, 16)
            for dst, src in ((wg[:], w["WsgT"].rearrange("(k p) n -> p k n", p=KD)),
                             (wu[:], w["WsuT"].rearrange("(k p) n -> p k n", p=KD)),
                             (wd[:], w["WsdT"].rearrange("(k p) n -> p k n", p=128)),
                             (ident[:], w["ident"]), (blocks[:], w["blocks"]), (before[:], w["before"])):
                sp.dma_start(dst, src).then_inc(w_ld, 16)

            def body(c, par):
                wait(sp, y_ev, 2 * (c - 1))
                sp.dma_start(xT[:, par], xnT_d[:, bass.ds(c * CHUNK, CHUNK)].rearrange("(k p) n -> p k n", p=KD)).then_inc(x_ld[par], 16)
                sp.dma_start(res[:, par], h1_d[bass.ds(c * CHUNK, CHUNK), :].rearrange("(t p) n -> p t n", p=TP)).then_inc(x_ld[par], 16)

            chunks(sp, body)

        @block.scalar
        def _(act):
            a = nc.scalar

            def body(c, par):
                for m in range(MS):
                    n = MS * c + m
                    act.wait_ge(gu_mm, 2 * n + 1)
                    wait(act, h_ev, n - 1)
                    a.activation(sg[:, (MS * par + m) % 2], gps[(MS * par + m) % 2][:], ACT.Silu).then_inc(g_ev, 1)
                act.wait_ge(y_ev, 2 * c + 2)
                act.dma_start(out_d[bass.ds(c * CHUNK, CHUNK), :].rearrange("(t p) n -> p t n", p=TP), y[:, par]).then_inc(y_st[par], 16)

            chunks(act, body)
            for i in range(2):
                act.wait_ge(y_st[i], 16 * (CHUNKS // 2))

        @block.vector
        def _(dve):
            v = nc.vector
            v.memset(thr[:], 0).then_inc(ini, 1)
            v.memset(bit[:], 1 << (SCORE_BITS - 1)).then_inc(ini, 1)
            v.memset(zero[:], 0.0).then_inc(ini, 1)
            dve.wait_ge(ini, 3)
            dve.wait_ge(sc_ld, 16)

            def count(k):
                wait(dve, k_ch, K_CHAIN * k)
                v.tensor_tensor(cand[:], thr[:], bit[:], ALU.bitwise_or).then_inc(k_ch, 1)
                dve.wait_ge(k_ch, K_CHAIN * k + 1)
                v.tensor_scalar(hit[:], sc[:], cand[:].bitcast(F32), 0.0, ALU.is_ge, ALU.add, accum_out=cnt[:]).then_inc(k_cnt, 1)

            def update(k):
                dve.wait_ge(k_mm, k + 1)
                v.tensor_scalar(take[:], kps[:], float(CAPACITY), None, ALU.is_ge).then_inc(k_ch, 1)
                dve.wait_ge(k_ch, K_CHAIN * k + 2)
                v.tensor_single_scalar(bit[:], bit[:], 1, ALU.logical_shift_right)
                v.copy_predicated(thr[:], take[:], cand[:]).then_inc(k_ch, 1)

            def gated(c, par, m):
                n = MS * c + m
                dve.wait_ge(gu_mm, 2 * n + 2)
                dve.wait_ge(g_ev, n + 1)
                wait(dve, d_mm, 2 * c)
                v.tensor_tensor(hT[:, m], sg[:, (MS * par + m) % 2], ups[(MS * par + m) % 2][:], ALU.mult).then_inc(h_ev, 1)

            def body(c, par):
                count(2 * c)
                gated(c, par, 0)
                update(2 * c)
                count(2 * c + 1)
                gated(c, par, 1)
                gated(c, par, 2)
                update(2 * c + 1)
                dve.wait_ge(x_ld[par], 32 * ((c - par) // 2 + 1) if isinstance(c, int) else 16 * (c - par) + 32)
                wait(dve, y_st[par], 16 * (c // 2) if isinstance(c, int) else 8 * (c - par))
                for i in range(2):
                    dve.wait_ge(d_mm, 2 * c + i + 1)
                    v.tensor_tensor(y[:, par, 2 * i:2 * i + 2], dps[i][:], res[:, par, 2 * i:2 * i + 2], ALU.add).then_inc(y_ev, 1)

            assert 2 * CHUNKS >= SCORE_BITS
            chunks(dve, body)

            step = [0]

            def then(ins):
                step[0] += 1
                ins.then_inc(r_ch, 1)
                dve.wait_ge(r_ch, step[0])

            dve.wait_ge(k_ch, K_CHAIN * 2 * CHUNKS)
            t = thr[:].bitcast(F32)
            then(v.tensor_scalar(hit[:], sc[:], t, 0.0, ALU.is_gt, ALU.add, accum_out=cnt[:]))
            then(v.tensor_scalar(eq[:], sc[:], t, None, ALU.is_equal))
            then(v.tensor_tensor_scan(run[:], eq[:], zero[:], 0.0, ALU.add, ALU.add))
            dve.wait_ge(r_mm, 1)
            then(v.tensor_scalar(need[:], kps[:], -1.0, float(CAPACITY), ALU.mult, ALU.add))
            dve.wait_ge(r_mm, 2)
            then(v.tensor_tensor(need[:], need[:], kps[:], ALU.subtract))
            then(v.scalar_tensor_tensor(out=eq[:], in0=run[:], scalar=need[:], in1=eq[:], op0=ALU.is_le, op1=ALU.mult))
            then(v.tensor_tensor(hit[:], hit[:], eq[:], ALU.add))
            then(v.tensor_tensor_scan(run[:], hit[:], zero[:], 0.0, ALU.add, ALU.add))
            dve.wait_ge(r_mm, 3)
            then(v.tensor_copy(off[:], kps[:]))
            then(v.scalar_tensor_tensor(out=run[:], in0=run[:], scalar=off[:], in1=hit[:], op0=ALU.add, op1=ALU.mult))
            then(v.tensor_scalar(run[:], run[:], -1.0, None, ALU.add))
            half = BLOCKS // 2
            for i in range(2):
                dve.wait_ge(r_mm, 4 + i)
                then(v.tensor_copy(posi[:, i * half:(i + 1) * half], pps[:]))
            then(v.tensor_single_scalar(hi_all[:], posi[:], 5, ALU.arith_shift_right))
            then(v.tensor_single_scalar(lo_all[:], posi[:], LO - 1, ALU.bitwise_and))

        @block.tensor
        def _(pe):
            m_ = nc.tensor.matmul
            pe.wait_ge(w_ld, 96)

            def tally(k):
                pe.wait_ge(k_cnt, k + 1)
                m_(kps[:], blocks[:], cnt[:], start=True, stop=True).then_inc(k_mm, 1)

            def body(c, par):
                pe.wait_ge(x_ld[par], 32 * ((c - par) // 2 + 1) if isinstance(c, int) else 16 * (c - par) + 32)
                for m in range(MS):
                    n = MS * c + m
                    b = (MS * par + m) % 2
                    for ps, wt, s in ((gps[b], wg, g_ev), (ups[b], wu, h_ev)):
                        wait(pe, s, n - 1)
                        for k in range(NK):
                            ins = m_(ps[:], wt[:, k, m * 128:(m + 1) * 128], xT[:, par, k], start=k == 0, stop=k == NK - 1)
                        ins.then_inc(gu_mm, 1)
                    if m == 0:
                        tally(2 * c)
                tally(2 * c + 1)
                pe.wait_ge(h_ev, MS * (c + 1))
                for i in range(2):
                    wait(pe, y_ev, 2 * (c - 1) + i + 1)
                    for t in range(2):
                        for m in range(MS):
                            ins = m_(dps[i][:, t], hT[:, m, (2 * i + t) * TP:(2 * i + t + 1) * TP], wd[:, m], start=m == 0, stop=m == MS - 1)
                    ins.then_inc(d_mm, 1)

            chunks(pe, body)
            pe.wait_ge(r_ch, 1)
            m_(kps[:], blocks[:], cnt[:], start=True, stop=True).then_inc(r_mm, 1)
            pe.wait_ge(r_ch, 4)
            m_(kps[:], before[:], run[:, SPAN - 1:SPAN], start=True, stop=True).then_inc(r_mm, 1)
            pe.wait_ge(r_ch, 8)
            m_(kps[:], before[:], run[:, SPAN - 1:SPAN], start=True, stop=True).then_inc(r_mm, 1)
            for i in range(2):
                pe.wait_ge(r_ch, 11 + i)
                for j in range(BLOCKS // 2):
                    b = i * (BLOCKS // 2) + j
                    ins = nc.tensor.transpose(pps[:, j], run[:, b * TP:(b + 1) * TP], ident[:])
                ins.then_inc(r_mm, 1)


def experts(nc, w, xs_d, idx_d, out_d, hi_all, lo_all, sem, n_exp=EXPERTS):
    ctx = ExitStack()

    def sb(name, shape, dt=F32):
        return ctx.enter_context(nc.sbuf_tensor("ex_" + name, shape, dt))

    def pb(name, shape):
        return ctx.enter_context(nc.psum_tensor("exp_" + name, shape, F32))

    CAP_T = CAPACITY // TP
    ME = F_EXP // 128
    HALF = CAPACITY // 2
    HT = HALF // TP

    with ctx:
        ident = sb("ident", [128, 128])
        iota = sb("iota", [TP, LO])
        row = sb("row", [TP, 1])
        tile = sb("tile", [TP, BLOCKS * SPLIT])
        wg = sb("wg", [KD, NK, F_EXP])
        wu = sb("wu", [KD, NK, F_EXP])
        wd = sb("wd", [128, ME, D])
        one_hi = sb("one_hi", [TP, BLOCKS, SPLIT, LO], BF16)
        one_lo = sb("one_lo", [TP, BLOCKS, SPLIT, LO], BF16)
        val = sb("val", [TP, BLOCKS * SPLIT, 2, LO], BF16)
        lst = sb("lst", [LO, LO])
        lsti = sb("lsti", [LO, LO], U32)
        idxg = sb("idxg", [TP, CAP_T], U32)
        idxs = sb("idxs", [TP, CAP_T], U32)
        xg = sb("xg", [TP, CAP_T, SROW])
        gsc = sb("gsc", [TP, CAP_T])
        xgT = sb("xgT", [KD, NK, CAPACITY])
        sg = sb("sg", [128, 2, HALF])
        hT = sb("hT", [128, ME, CAPACITY])
        y = sb("y", [TP, CAP_T, D])
        gps = [pb(f"g{i}", [128, HALF]) for i in range(2)]
        ups = [pb(f"u{i}", [128, HALF]) for i in range(2)]
        dps = [pb(f"d{i}", [TP, 2, D]) for i in range(2)]
        tps = pb("t", [KD, HT, TP])
        lps = pb("l", [LO, 2 * LO])

        c_ld = sem("ex_c_ld")
        wgu_ld = sem("ex_wgu_ld")
        wd_ld = sem("ex_wd_ld")
        hot = sem("ex_hot")
        l_mm = sem("ex_l_mm")
        l_ev = sem("ex_l_ev")
        l_st = sem("ex_l_st")
        ig_ld = sem("ex_ig_ld")
        is_ld = sem("ex_is_ld")
        gat = sem("ex_gat")
        t_mm = sem("ex_t_mm")
        t_ev = sem("ex_t_ev")
        sc_ev = sem("ex_sc_ev")
        gu_mm = sem("ex_gu_mm")
        g_ev = sem("ex_g_ev")
        h_ev = sem("ex_h_ev")
        d_mm = sem("ex_d_mm")
        y_ev = sem("ex_y_ev")
        sca = sem("ex_sca")
        UNITS = 2 * ME
        TR = NK * 2
        DN = CAP_T // 2
        HOT = 4

        def wait(eng, s, value):
            if not isinstance(value, int) or value > 0:
                eng.wait_ge(s, value)

        def turns(eng, body):
            body(0, True, True)
            with eng.Fori(1, n_exp - 2) as e:
                body(e, True, True)
            body(n_exp - 2, True, False)
            body(n_exp - 1, False, False)

        block = ctx.enter_context(nc.Block())

        @block.sync
        def _(sp):
            for dst, src in ((ident[:], w["ident"]), (iota[:], w["iota"]), (row[:], w["row"]), (tile[:], w["tile"])):
                sp.dma_start(dst, src).then_inc(c_ld, 16)

            def load_gu(e):
                wait(sp, gu_mm, 2 * UNITS * e)
                for dst, src in ((wg, w["WgT"]), (wu, w["WuT"])):
                    sp.dma_start(dst[:], src[bass.ds(e, 1)].rearrange("a (k p) n -> p (a k) n", p=KD)).then_inc(wgu_ld, 16)

            def load_d(e):
                wait(sp, d_mm, DN * e)
                sp.dma_start(wd[:], w["WdT"][bass.ds(e, 1)].rearrange("a (k p) n -> p (a k) n", p=128)).then_inc(wd_ld, 16)

            def store_list(e):
                wait(sp, l_ev, 2 * e + 2)
                sp.dma_start(idx_d[bass.ds(e, 1), :].rearrange("a (p n) -> p (a n)", n=LO), lsti[:]).then_inc(l_st, 16)

            def load_idx(dst, s, e):
                wait(sp, l_st, 16 * (e + 1))
                sp.dma_start(dst[:], idx_d[bass.ds(e, 1), 0:CAPACITY].rearrange("a (p t) -> p (a t)", t=CAP_T)).then_inc(s, 16)

            load_gu(0)
            load_d(0)
            store_list(0)
            load_idx(idxg, ig_ld, 0)
            store_list(1)

            def body(e, more, lists):
                wait(sp, sca, 16 * CAP_T * e)
                load_idx(idxs, is_ld, e)
                if more:
                    wait(sp, gat, 16 * CAP_T * (e + 1))
                    load_idx(idxg, ig_ld, e + 1)
                if lists:
                    store_list(e + 2)
                if more:
                    load_gu(e + 1)
                    load_d(e + 1)

            turns(sp, body)

        @block.gpsimd
        def _(pool):
            g = nc.gpsimd
            last = pool.to_reg(TOKENS - 1)

            def gather(e):
                apart(pool, (c_ld, 64), (ig_ld, 16 * (e + 1)), (t_mm, TR * e), (sc_ev, e))
                for t in range(CAP_T):
                    g.indirect_dma_start(xg[:, t], None, xs_d[:, :], bass.IndirectOffsetOnAxis(idxg[:, t:t + 1], 0),
                                         bounds_check=last).then_inc(gat, 16)

            gather(0)

            def body(e, more, lists):
                if more:
                    gather(e + 1)
                for t in range(CAP_T):
                    apart(pool, (c_ld, 64), *[(is_ld, 16 * (e + 1))] * (t == 0), *[(y_ev, DN * e + t // 2 + 1)] * (t % 2 == 0),
                               (sca, 16 * (CAP_T * e + t)))
                    g.indirect_dma_start(out_d[:, :], bass.IndirectOffsetOnAxis(idxs[:, t:t + 1], 0), y[:, t], None,
                                         bounds_check=last, compute_op=ALU.add).then_inc(sca, 16)

            turns(pool, body)
            pool.wait_ge(sca, 16 * CAP_T * n_exp)

        @block.scalar
        def _(act):
            a = nc.scalar

            def body(e, more, lists):
                for n in range(UNITS):
                    act.wait_ge(gu_mm, 2 * (UNITS * e + n) + 1)
                    wait(act, h_ev, UNITS * e + n - 1)
                    a.activation(sg[:, n % 2], gps[n % 2][:], ACT.Silu).then_inc(g_ev, 1)

            turns(act, body)

        @block.vector
        def _(dve):
            v = nc.vector
            dve.wait_ge(c_ld, 64)

            def one_hots(e):
                shape = [TP, BLOCKS, SPLIT, LO]
                wait(dve, l_mm, e)
                own = bass.ds(e * SPLIT, SPLIT)
                io = iota[:].rearrange("p (a b n) -> p a b n", a=1, b=1).to_broadcast(shape)
                v.tensor_tensor(one_hi[:], hi_all[:, :, own].rearrange("p a (b n) -> p a b n", n=1).to_broadcast(shape), io, ALU.is_equal).then_inc(hot, 1)
                v.tensor_tensor(one_lo[:], lo_all[:, :, own].rearrange("p a (b n) -> p a b n", n=1).to_broadcast(shape), io, ALU.is_equal).then_inc(hot, 1)
                dve.wait_ge(hot, HOT * e + 2)
                flat = one_lo[:].rearrange("p a b n -> p (a b) n")
                v.tensor_scalar(val[:, :, 0], flat, row[:, 0:1], None, ALU.mult).then_inc(hot, 1)
                v.tensor_tensor(val[:, :, 1], flat, tile[:].rearrange("p (a n) -> p a n", n=1).to_broadcast([TP, BLOCKS * SPLIT, LO]), ALU.mult).then_inc(hot, 1)

            def list_out(e):
                dve.wait_ge(l_mm, e + 1)
                wait(dve, l_st, 16 * e)
                v.tensor_copy(lst[:], lps[:, 0:LO]).then_inc(l_ev, 1)
                dve.wait_ge(l_ev, 2 * e + 1)
                v.scalar_tensor_tensor(out=lsti[:], in0=lps[:, LO:2 * LO], scalar=float(TP), in1=lst[:], op0=ALU.mult, op1=ALU.add).then_inc(l_ev, 1)

            def rows_in(e, j):
                dve.wait_ge(t_mm, TR * e + j + 1)
                k, half = j % NK, j // NK
                v.tensor_copy(xgT[:, k, half * HALF:(half + 1) * HALF].rearrange("p (t n) -> p t n", n=TP), tps[:]).then_inc(t_ev, 1)

            def scores_in(e):
                dve.wait_ge(gat, 16 * CAP_T * (e + 1))
                wait(dve, y_ev, DN * e)
                v.tensor_copy(gsc[:], xg[:, :, bass.ds(D + e, 1)].rearrange("p t n -> p (t n)")).then_inc(sc_ev, 1)

            one_hots(0)
            list_out(0)
            one_hots(1)
            list_out(1)
            for j in range(TR):
                rows_in(0, j)
            scores_in(0)

            def body(e, more, lists):
                for n in range(UNITS):
                    dve.wait_ge(gu_mm, 2 * (UNITS * e + n) + 2)
                    dve.wait_ge(g_ev, UNITS * e + n + 1)
                    wait(dve, d_mm, DN * e)
                    m, half = n % ME, n // ME
                    v.tensor_tensor(hT[:, m, half * HALF:(half + 1) * HALF], sg[:, n % 2], ups[n % 2][:], ALU.mult).then_inc(h_ev, 1)
                    if lists and n == 2:
                        one_hots(e + 2)
                for j in range(DN):
                    if more:
                        rows_in(e + 1, j)
                    if j == 0:
                        dve.wait_ge(sc_ev, e + 1)
                        wait(dve, sca, 16 * CAP_T * e)
                    dve.wait_ge(d_mm, DN * e + j + 1)
                    for i in range(2):
                        t = 2 * j + i
                        ins = v.tensor_scalar(y[:, t], dps[j % 2][:, i], gsc[:, t:t + 1], None, ALU.mult)
                    ins.then_inc(y_ev, 1)
                if more:
                    dve.wait_ge(y_ev, DN * (e + 1))
                    scores_in(e + 1)
                if lists:
                    list_out(e + 2)

            turns(dve, body)

        @block.tensor
        def _(pe):
            m_ = nc.tensor.matmul
            pe.wait_ge(c_ld, 64)

            def list_mm(e):
                pe.wait_ge(hot, HOT * (e + 1))
                wait(pe, l_ev, 2 * e)
                for b in range(BLOCKS):
                    for c in range(SPLIT):
                        n = b * SPLIT + c
                        ins = m_(lps[:], one_hi[:, b, c], val[:, n].rearrange("p a n -> p (a n)"), start=n == 0, stop=n == BLOCKS * SPLIT - 1)
                ins.then_inc(l_mm, 1)

            def rows_T(e, j):
                k, half = j % NK, j // NK
                if j == 0:
                    pe.wait_ge(gat, 16 * CAP_T * (e + 1))
                wait(pe, t_ev, TR * e + j)
                for t in range(HT):
                    ins = nc.tensor.transpose(tps[:, t], xg[:, half * HT + t, k * KD:(k + 1) * KD], ident[0:TP, 0:TP])
                ins.then_inc(t_mm, 1)

            list_mm(0)
            list_mm(1)
            for j in range(TR):
                rows_T(0, j)

            def body(e, more, lists):
                pe.wait_ge(wgu_ld, 32 * (e + 1))
                pe.wait_ge(t_ev, TR * (e + 1))
                for n in range(UNITS):
                    m, half = n % ME, n // ME
                    for ps, wt, s in ((gps, wg, g_ev), (ups, wu, h_ev)):
                        wait(pe, s, UNITS * e + n - 1)
                        for k in range(NK):
                            ins = m_(ps[n % 2][:], wt[:, k, m * 128:(m + 1) * 128], xgT[:, k, half * HALF:(half + 1) * HALF], start=k == 0, stop=k == NK - 1)
                        ins.then_inc(gu_mm, 1)
                pe.wait_ge(wd_ld, 16 * (e + 1))
                for j in range(DN):
                    if more:
                        rows_T(e + 1, j)
                    if j == 0:
                        pe.wait_ge(h_ev, UNITS * (e + 1))
                    wait(pe, y_ev, DN * e + j - 1)
                    for i in range(2):
                        t = 2 * j + i
                        for m in range(ME):
                            ins = m_(dps[j % 2][:, i], hT[:, m, t * TP:(t + 1) * TP], wd[:, m], start=m == 0, stop=m == ME - 1)
                    ins.then_inc(d_mm, 1)
                if lists:
                    list_mm(e + 2)

            turns(pe, body)


def audio_tower(nc, w, out_d):
    def scratch(name, shape, dt=F32):
        return nc.dram_tensor(name, shape, dt, kind="Internal").ap()

    hx_d = scratch("hx_d", (TOKENS, 2 * D))
    bias_d = scratch("bias_d", (HEADS, FRAMES, PITCH))
    h1_d = scratch("h1_d", (TOKENS, D))
    xs_d = scratch("xs_d", (TOKENS, SROW))
    xnT_d = scratch("xnT_d", (D, TOKENS))
    scT_d = scratch("scT_d", (EXPERTS, TOKENS))
    idx_d = scratch("idx_d", (EXPERTS, LO * LO), U32)
    with ExitStack() as ctx:
        def sem(name):
            return ctx.enter_context(nc.semaphore(name))

        tower(nc, w, hx_d, bias_d, h1_d, xs_d, xnT_d, scT_d, sem)
        hi_all = ctx.enter_context(nc.sbuf_tensor("hi_all", [TP, BLOCKS, 128], I32))
        lo_all = ctx.enter_context(nc.sbuf_tensor("lo_all", [TP, BLOCKS, 128], I32))
        shared_and_route(nc, w, h1_d, xnT_d, scT_d, out_d, hi_all, lo_all, sem)
        experts(nc, w, xs_d, idx_d, out_d, hi_all, lo_all, sem)


def constants():
    block, part = np.divmod(np.arange(BLOCKS * SPLIT), SPLIT)
    return {
        "ident": np.eye(128, dtype=np.float32), "dft": dft_table(), "basis": basis_table(),
        "blocks": expert_blocks(), "before": expert_before(),
        "iota": np.tile(np.arange(LO, dtype=np.float32), (TP, 1)),
        "row": np.arange(TP, dtype=np.float32)[:, None],
        "tile": np.tile((part * BLOCKS + block).astype(np.float32), (TP, 1)),
    }


def layout(i):
    a, f, t = "L0_attn_", "L0_ffn_", "L0_tok_"
    framed = i["x"][:, :FRAMES * FRAME_STEP].reshape(BATCH, FRAMES, FRAME_STEP)[:, :, :FRAME_LEN]
    return {
        "frames": framed.transpose(2, 0, 1).reshape(FRAME_LEN, TOKENS),
        "melT": i[t + "mel_filters"].T, "dctT": i[t + "dct"].T,
        "w_proj": i[t + "w_proj"], "b_proj": i[t + "b_proj"].reshape(1, D),
        "wq": i[a + "wq"], "wk": i[a + "wk"], "wv": i[a + "wv"], "wo": i[a + "wo"],
        "w1": i[a + "w1"], "w2": i[a + "w2"], "b2": i[a + "b2"], "bo": i[a + "bo"],
        "n1w": i[a + "norm1_w"].reshape(NK, KD).T, "n2w": i[a + "norm2_w"].reshape(NK, KD).T,
        "b1": i[a + "b1"].reshape(DFF // 128, 128).T,
        "u": i[a + "u_param"].reshape(PAIRS, 128).T, "v": i[a + "v_param"].reshape(PAIRS, 128).T,
        "w_posT": i[a + "w_pos"].transpose(2, 0, 1).reshape(N_POS, HEADS * DK),
        "gateT": i[f + "gate_weight"].T,
        "WsgT": i[f + "Ws_g"].T, "WsuT": i[f + "Ws_u"].T, "WsdT": i[f + "Ws_d"].T,
        "WgT": i[f + "Wg"].transpose(0, 2, 1), "WuT": i[f + "Wu"].transpose(0, 2, 1),
        "WdT": i[f + "Wd"].transpose(0, 2, 1),
    }


def kernel(**inputs):
    import concourse.bacc as bacc
    from concourse.bass_utils import run_bass_kernel_spmd

    nc = bacc.Bacc("TRN2", target_bir_lowering=False, num_devices=1)
    arrays = {k: np.ascontiguousarray(v) for k, v in {**layout(inputs), **constants()}.items()}
    w = {k: nc.dram_tensor(k, v.shape, mybir.dt.from_np(v.dtype), kind="ExternalInput").ap() for k, v in arrays.items()}
    out_d = nc.dram_tensor("out", (TOKENS, D), F32, kind="ExternalOutput").ap()
    audio_tower(nc, w, out_d)
    r = run_bass_kernel_spmd(nc, [arrays], core_ids=[0])
    return r.results[0]["out"].reshape(BATCH, FRAMES, D)
```

```python
import math
from contextlib import ExitStack

import numpy as np
import concourse.bass as bass
from concourse import mybir

F32 = mybir.dt.float32
ALU = mybir.AluOpType
ACT = mybir.ActivationFunctionType
AX_X = mybir.AxisListType.X

BATCH, AUDIO = 32, 40000
FRAME_LEN, FRAME_STEP = 100, 160
FRAMES = 1 + (AUDIO - FRAME_LEN) // FRAME_STEP
BINS = FRAME_LEN // 2 + 1
MELS, MFCC, D = 40, 13, 192
HEADS, DK = 8, 64
DV = D // HEADS
N_POS = 32
DFF = 2 * D
EPS = 1e-5
TOKENS = BATCH * FRAMES
EXPERTS, TOP_K = 16, 2
CAPACITY = math.ceil(TOKENS / EXPERTS * TOP_K)
F_EXP = 4 * D
F_SH = F_EXP // 2

TP = 125
NT = FRAMES // TP
KD = 96
NK = D // KD
PAIRS = HEADS // 2
RANGE = 125
ND = 2 * RANGE + 1
PITCH = 2 * FRAMES - 1
SLOTS = HEADS
SCALE = 1.0 / math.sqrt(DK)
SROW = 2 * 128 + EXPERTS


EXP_SET = "exp_and_others"


def dft_table():
    n = np.arange(FRAME_LEN, dtype=np.float64)
    window = 0.54 - 0.46 * np.cos(2.0 * np.pi * n / (FRAME_LEN - 1))
    angle = 2.0 * np.pi * np.outer(n, np.arange(BINS)) / FRAME_LEN
    return (np.concatenate([np.cos(angle), np.sin(angle)], 1) * window[:, None]).astype(np.float32)


def basis_table():
    half = N_POS // 2
    rate = np.exp(np.log(np.float32((FRAMES + 1) / 2.0)) / np.float32(half)).astype(np.float32)
    widths = rate ** np.arange(1, half + 1, dtype=np.float32)
    assert widths[-1] < RANGE + 1
    dist = np.arange(-RANGE, RANGE + 1).astype(np.float32)
    inside = (np.abs(dist)[None, :] <= widths[:, None]).astype(np.float32)
    return np.concatenate([inside, np.sign(dist)[None, :] * inside], 0)


def apart(eng, ready, *waits):
    waits = [(s, v if isinstance(v, int) else eng.to_reg(v)) for s, v in waits]
    eng.wait_ge(*ready)
    for s, v in waits:
        if not isinstance(v, int) or v > 0:
            eng.wait_ge(s, v)


def tower(nc, w, hx_d, bias_d, h1_d, xs_d, xnT_d, scT_d, sem, n_batch=BATCH):
    ctx = ExitStack()

    def sb(name, shape, dt=F32):
        return ctx.enter_context(nc.sbuf_tensor("sb_" + name, shape, dt))

    def pb(name, shape):
        return ctx.enter_context(nc.psum_tensor("ps_" + name, shape, F32))

    with ctx:
        ident = sb("ident", [128, 128])
        dft = sb("dft", [FRAME_LEN, 2 * BINS])
        mel = sb("mel", [2 * BINS, MELS])
        dct = sb("dct", [MELS, MFCC])
        wproj = sb("wproj", [MFCC + 1, D])
        wq = sb("wq", [KD, NK, HEADS * DK])
        wk = sb("wk", [KD, NK, HEADS * DK])
        wv = sb("wv", [KD, NK, D])
        wo = sb("wo", [KD, NK, D])
        w1 = sb("w1", [KD, NK, DFF])
        w2 = sb("w2", [128, DFF // 128, D])
        gate = sb("gate", [KD, NK, EXPERTS])
        n1w = sb("n1w", [KD, NK])
        n2w = sb("n2w", [KD, NK])
        b1 = sb("b1", [128, DFF // 128])
        ucol = sb("ucol", [128, PAIRS])
        vcol = sb("vcol", [128, PAIRS])
        wpos = sb("wpos", [N_POS, HEADS * DK])
        basis = sb("basis", [N_POS, ND])
        bb = sb("bb", [TP, NT, 2 * D])
        tiny = sb("tiny", [MELS, 1])
        power = sb("power", [TP, 2 * NT])
        zeros = sb("zeros", [TP, PITCH])
        wbz = sb("wbz", [128, HEADS, ND])
        frames = sb("frames", [FRAME_LEN, FRAMES])
        sq = sb("sq", [2 * BINS, FRAMES])
        logmel = sb("logmel", [MELS, FRAMES])
        mfcc = sb("mfcc", [MFCC + 1, FRAMES])
        hx = sb("hx", [TP, NT, 2 * D])
        t_stats = sb("t_stats", [TP, NT, 6])
        t_mv = sb("t_mv", [TP, NT, 2])
        t_inv = sb("t_inv", [TP, NT])
        t_v = sb("t_v", [TP, 2 * NT])
        t_y = sb("t_y", [TP, 2 * NT])
        h1n = sb("h1n", [TP, NT, D])
        h1T = sb("h1T", [KD, NK, FRAMES])
        qu = sb("qu", [128, PAIRS, FRAMES])
        qv = sb("qv", [128, PAIRS, FRAMES])
        kz = sb("kz", [128, HEADS, FRAMES])
        vz = sb("vz", [TP, NT, HEADS, KD])
        vtmp = sb("vtmp", [TP, NT, D])
        rsb = sb("rsb", [TP, 2, NT, ND])
        bsk = sb("bsk", [TP, 4, NT, FRAMES])
        ssb = sb("ssb", [TP, 2, NT, FRAMES])
        prob = sb("prob", [TP, 2, NT, FRAMES])
        mx = sb("mx", [TP, 2, NT])
        rs = sb("rs", [TP, 2, NT])
        rinv = sb("rinv", [TP, 2, NT])
        ptsb = sb("ptsb", [TP, 2, NT, FRAMES])
        otsb = sb("otsb", [KD, NK, FRAMES])
        hxl = sb("hxl", [TP, NT, 2 * D])
        x1 = sb("x1", [TP, NT, D])
        xb = sb("xb", [TP, NT, D])
        junk = sb("junk", [TP, D])
        ss = sb("ss", [TP, NT])
        c_v = sb("c_v", [TP, NT])
        c_y = sb("c_y", [TP, NT])
        h2n = sb("h2n", [TP, NT, D])
        h2T = sb("h2T", [KD, NK, FRAMES])
        gT = sb("gT", [128, DFF // 128, FRAMES])
        h1 = sb("h1", [TP, NT, D])
        c_stats = sb("c_stats", [TP, NT, 6])
        c_mv = sb("c_mv", [TP, NT, 2])
        d_v = sb("d_v", [TP, NT])
        d_y = sb("d_y", [TP, NT])
        xs = sb("xs", [TP, NT, SROW])
        xnT = sb("xnT", [KD, NK, FRAMES])
        sige = sb("sige", [TP, NT, EXPERTS])
        scT = sb("scT", [EXPERTS, FRAMES])
        sps = [pb(f"sps{i}", [TP, NT, FRAMES]) for i in range(2)]
        ptps = pb("ptps", [TP, NT, FRAMES])
        otps = pb("otps", [KD, NK, FRAMES])
        qps = [pb(f"qps{i}", [128, 512]) for i in range(2)]
        tps = pb("tps", [128, 512])
        cps = pb("cps", [128, 512])

        w_ld = sem("w_ld")
        READY = (w_ld, W_LOADS)
        z_set = sem("z_set")
        zero_st = sem("zero_st")
        wb_mm = sem("wb_mm")
        wb_ev = sem("wb_ev")
        fr_ld = sem("fr_ld")
        t_mm = sem("t_mm")
        t_ev = sem("t_ev")
        t_ch = sem("t_ch")
        hx_st = sem("hx_st")
        q_mm = sem("q_mm")
        q_ev = [sem(f"q_ev{i}") for i in range(2)]
        r_st = [sem(f"r_st{i}") for i in range(2)]
        bsk_ld = [sem(f"bsk_ld{i}") for i in range(4)]
        s_mm = sem("s_mm")
        s_add = sem("s_add")
        p_exp = sem("p_exp")
        r_inv = sem("r_inv")
        p_nrm = sem("p_nrm")
        pt_mm = sem("pt_mm")
        pt_ev = sem("pt_ev")
        pv_mm = sem("pv_mm")
        ot_ev = sem("ot_ev")
        hxl_ld = sem("hxl_ld")
        c_hb = sem("c_hb")
        c_mm = sem("c_mm")
        c_ev = sem("c_ev")
        c_ch = sem("c_ch")
        c_xb = sem("c_xb")
        d_ch = sem("d_ch")
        c_sg = sem("c_sg")
        x_dup = sem("x_dup")
        d_mm = sem("d_mm")
        d_ev = sem("d_ev")
        vz_in = sem("vz_in")
        c_st = sem("c_st")
        scT_st = sem("scT_st")

        T_USES, C_USES, D_USES, Q_USES = 5, 5, 3, 14
        T_CHAIN, C_CHAIN, D_CHAIN = 13, 6, 8
        QK_SLOT = {0: 0, 2: 1, 4: 2, 6: 3}
        T_SLOT = {1: 0, 2: 1, 4: 2, 5: 3}
        QK_USE = [0, 3, 8, 11]
        R_USE = [1, 2, 4, 5, 9, 10, 12, 13]
        V_USE = [6, 7]

        def wait(eng, s, value):
            if not isinstance(value, int) or value > 0:
                eng.wait_ge(s, value)

        def q_freed(eng, b, use):
            wait(eng, q_ev[use % 2], 2 * (Q_USES // 2 * b + use // 2))

        def q_count(b, use):
            return 2 * (Q_USES // 2 * b + use // 2 + 1)

        def q_evacuated(eng, b, use):
            wait(eng, q_ev[use % 2], q_count(b, use))

        def rounds(eng, body):
            last = n_batch - 1

            def at(i):
                return [(i - j) if 0 <= i - j <= last else None for j in range(5)]

            head = min(4, n_batch + 4)
            for i in range(head):
                body(*at(i))
            if n_batch > 4:
                with eng.Fori(4, n_batch) as i:
                    body(i, i - 1, i - 2, i - 3, i - 4)
            for i in range(max(head, n_batch), n_batch + 4):
                body(*at(i))

        def bank2(ps, n, rows):
            return ps[0:rows, 0:2 * n].rearrange("p (t n) -> p t n", t=2)

        block = ctx.enter_context(nc.Block())

        @block.sync
        def _(sp):
            loads = [
                (ident[:], w["ident"]), (dft[:], w["dft"]), (mel[0:BINS], w["melT"]),
                (mel[BINS:2 * BINS], w["melT"]), (dct[:], w["dctT"]),
                (wproj[0:MFCC], w["w_proj"]), (wproj[MFCC:MFCC + 1], w["b_proj"]),
                (wq[:], w["wq"].rearrange("(k p) n -> p k n", p=KD)),
                (wk[:], w["wk"].rearrange("(k p) n -> p k n", p=KD)),
                (wv[:], w["wv"].rearrange("(k p) n -> p k n", p=KD)),
                (wo[:], w["wo"].rearrange("(k p) n -> p k n", p=KD)),
                (w1[:], w["w1"].rearrange("(k p) n -> p k n", p=KD)),
                (w2[:], w["w2"].rearrange("(k p) n -> p k n", p=128)),
                (gate[:], w["gateT"].rearrange("(k p) n -> p k n", p=KD)),
                (n1w[:], w["n1w"]), (n2w[:], w["n2w"]), (b1[:], w["b1"]),
                (ucol[:], w["u"]), (vcol[:], w["v"]), (wpos[:], w["w_posT"]), (basis[:], w["basis"]),
            ]
            for t in range(NT):
                loads += [(bb[:, t, 0:D], w["b2"].partition_broadcast(TP)),
                          (bb[:, t, D:2 * D], w["bo"].partition_broadcast(TP))]
            for dst, src in loads:
                sp.dma_start(dst, src).then_inc(w_ld, 16)
            sp.wait_ge(z_set, 1)
            for h in range(HEADS):
                for t in range(NT):
                    sp.dma_start(bias_d[h, t * TP:(t + 1) * TP, :], zeros[:]).then_inc(zero_st, 16)

            def body(bt, bq, bb_, bc, bd):
                for s in range(SLOTS):
                    if bt is not None and s == 0:
                        wait(sp, t_mm, T_USES * bt - 4)
                        sp.dma_start(frames[:], w["frames"][:, bass.ds(bt * FRAMES, FRAMES)]).then_inc(fr_ld, 16)
                    if bb_ is not None and s + 2 < HEADS:
                        load_bias(bb_, s + 2)
                    if bq is not None and s % 2 == 1:
                        for h in (s - 1, s):
                            q_evacuated(sp, bq, R_USE[h])
                            wait(sp, bsk_ld[h % 4], 16 * (2 * (bq - 1) + h // 4 + 1))
                            if isinstance(bq, int) and bq == 0 and h == 0:
                                sp.wait_ge(zero_st, 16 * HEADS * NT)
                            dst = bias_d[h, :, FRAMES - 1 - RANGE:FRAMES + RANGE].rearrange("(t p) n -> p t n", p=TP)
                            sp.dma_start(dst, rsb[:, h % 2]).then_inc(r_st[h % 2], 16)
                    if bd is not None and s == 5:
                        sl = bass.ds(bd * FRAMES, FRAMES)
                        apart(sp, READY, (d_ev, D_USES * bd + 2), (c_sg, 2 * bd + 2), (x_dup, bd + 1))
                        sp.dma_start(h1_d[sl, :].rearrange("(t p) n -> p t n", p=TP), h1[:]).then_inc(c_st, 16)
                        sp.dma_start(xnT_d[:, sl].rearrange("(k p) n -> p k n", p=KD), xnT[:]).then_inc(c_st, 16)
                        sp.dma_start(xs_d[sl, :].rearrange("(t p) n -> p t n", p=TP), xs[:]).then_inc(c_st, 16)
                    if bb_ is not None and s == 5:
                        apart(sp, READY, (hx_st, 16 * (bb_ + 1)), (c_xb, bb_))
                        sp.dma_start(hxl[:], hx_d[bass.ds(bb_ * FRAMES, FRAMES), :].rearrange("(t p) n -> p t n", p=TP)).then_inc(hxl_ld, 16)
                    if bq is not None and s >= 6:
                        load_bias(bq, s - 6)
                    if bt is not None and s == 7:
                        wait(sp, t_ch, T_CHAIN * bt + 11)
                        sp.dma_start(hx_d[bass.ds(bt * FRAMES, FRAMES), :].rearrange("(t p) n -> p t n", p=TP), hx[:]).then_inc(hx_st, 16)

            def load_bias(b, h):
                wait(sp, r_st[h % 2], 16 * (4 * b + h // 2 + 1))
                wait(sp, s_add, 2 * (HEADS * b + h - 4) + 2)
                base = bias_d[h, 0:1, FRAMES - 1:FRAMES]
                src = bass.AP(base.tensor, base.offset, [[PITCH - 1, TP], [(PITCH - 1) * TP, NT], [1, FRAMES]])
                sp.dma_start(bsk[:, h % 4], src).then_inc(bsk_ld[h % 4], 16)

            rounds(sp, body)
            sp.wait_ge(c_st, 48 * n_batch)
            sp.wait_ge(hx_st, 16 * n_batch)

        @block.gpsimd
        def _(pool):
            g = nc.gpsimd
            g.memset(zeros[:], 0.0).then_inc(z_set, 1)
            g.memset(mfcc[:], 1.0).then_inc(z_set, 1)
            g.memset(kz[:], 0.0).then_inc(z_set, 1)
            g.memset(vz[:], 0.0).then_inc(z_set, 1)
            g.memset(wbz[:], 0.0).then_inc(z_set, 1)
            g.memset(tiny[:], 1e-6).then_inc(z_set, 1)
            g.memset(power[:], -0.5).then_inc(z_set, 1)
            pool.wait_ge(w_ld, W_LOADS)
            pool.wait_ge(z_set, 7)

            def vz_copy(b, i):
                base = vz[:, 0, i * 4, 0:DV]
                dst = bass.AP(base.tensor, base.offset, [base.ap[0], [HEADS * KD, NT], [KD + DV, 4], [1, DV]])
                apart(pool, READY, (q_ev[0], q_count(b, V_USE[0])), (q_ev[1], q_count(b, V_USE[1])),
                      (pv_mm, HEADS * (b - 1) + 4 * i + 4))
                g.tensor_copy(dst, vtmp[:, :, i * KD:(i + 1) * KD].rearrange("p t (h n) -> p t h n", h=4)).then_inc(vz_in, 1)

            def body(bt, bq, bb_, bc, bd):
                for s in range(SLOTS):
                    if bb_ is not None and s == 1:
                        vz_copy(bb_, 1)
                    if bc is not None and s == 1:
                        pool.wait_ge(hxl_ld, 16 * (bc + 1))
                        g.tensor_tensor(hxl[:], hxl[:], bb[:], ALU.add).then_inc(c_hb, 1)
                    if bc is not None and s == 3:
                        pool.wait_ge(c_ch, C_CHAIN * bc + 3)
                        g.tensor_tensor(c_y[:], c_v[:], power[:, 0:NT], ALU.pow).then_inc(c_ch, 1)
                        g.tensor_tensor(xb[:], x1[:], hxl[:, :, 0:D], ALU.add).then_inc(c_xb, 1)
                    if bd is not None and s == 0:
                        pool.wait_ge(d_ch, D_CHAIN * bd + 5)
                        g.tensor_tensor(d_y[:], d_v[:], power[:, 0:NT], ALU.pow).then_inc(d_ch, 1)
                        apart(pool, READY, (d_ch, D_CHAIN * bd + D_CHAIN))
                        g.tensor_copy(xs[:, :, D:256], xs[:, :, 128:D]).then_inc(x_dup, 1)
                    if bq is not None and s == 5:
                        vz_copy(bq, 0)
                    if bd is not None and s == 6:
                        pool.wait_ge(d_ev, D_USES * bd + 3)
                        g.dma_start(scT_d[:, bass.ds(bd * FRAMES, FRAMES)], scT[:]).then_inc(scT_st, 16)
                    if bt is not None and s == 5:
                        pool.wait_ge(t_ch, T_CHAIN * bt + 8)
                        g.tensor_tensor(t_y[:], t_v[:], power[:], ALU.pow).then_inc(t_ch, 1)

            rounds(pool, body)
            pool.wait_ge(scT_st, 16 * n_batch)

        @block.scalar
        def _(act):
            a = nc.scalar
            a.preload_act_table_set(EXP_SET)
            act.wait_ge(w_ld, W_LOADS)
            act.wait_ge(z_set, 7)

            def body(bt, bq, bb_, bc, bd):
                for s in range(SLOTS):
                    if bq is not None and s - 1 in QK_SLOT:
                        p = QK_SLOT[s - 1]
                        act.wait_ge(q_mm, Q_USES * bq + QK_USE[p] + 1)
                        ps = bank2(qps[QK_USE[p] % 2], FRAMES, 128)
                        wait(act, s_mm, HEADS * (bq - 1) + 2 * p + 2)
                        a.activation(qu[:, p], ps[:, 0], ACT.Identity, bias=ucol[:, p:p + 1])
                        a.activation(qv[:, p], ps[:, 0], ACT.Identity, bias=vcol[:, p:p + 1])
                        a.activation(kz[0:64, 2 * p], ps[0:64, 1], ACT.Copy)
                        a.activation(kz[64:128, 2 * p + 1], ps[64:128, 1], ACT.Copy).then_inc(q_ev[QK_USE[p] % 2], 2)
                    if bb_ is not None and s < HEADS:
                        n = HEADS * bb_ + s
                        for t in range(NT):
                            act.wait_ge(s_add, 2 * n + t + 1)
                            if t == 0:
                                wait(act, pt_mm, n - 1)
                            a.activation(prob[:, s % 2, t], ssb[:, s % 2, t], ACT.Exp, bias=mx[:, s % 2, t:t + 1],
                                         scale=-1.0, accum_out=rs[:, s % 2, t:t + 1]).then_inc(p_exp, 1)
                    if bc is not None and s == 2:
                        b0 = C_CHAIN * bc
                        act.wait_ge(c_ev, C_USES * bc + 1)
                        a.activation(junk[:], x1[:, 0], ACT.Square, accum_out=ss[:, 0:1]).then_inc(c_ch, 1)
                        act.wait_ge(c_ch, b0 + 1)
                        a.activation(junk[:], x1[:, 1], ACT.Square, accum_out=ss[:, 1:2]).then_inc(c_ch, 1)
                    if bd is not None and s == 3:
                        act.wait_ge(d_mm, D_USES * bd + 2)
                        a.activation(sige[:], cps[0:TP, 0:NT * EXPERTS].rearrange("p (t n) -> p t n", t=NT), ACT.Exp, scale=-1.0).then_inc(d_ev, 1)
                    if bc is not None and s == 5:
                        act.wait_ge(c_mm, C_USES * bc + 3)
                        ps = bank2(cps, FRAMES, 128)
                        a.activation(gT[:, 0], ps[:, 0], ACT.Gelu, bias=b1[:, 0:1])
                        a.activation(gT[:, 1], ps[:, 1], ACT.Gelu, bias=b1[:, 1:2]).then_inc(c_ev, 1)
                    if bt is not None and s == 1:
                        act.wait_ge(t_mm, T_USES * bt + 1)
                        a.activation(sq[:], tps[0:2 * BINS, 0:FRAMES], ACT.Square).then_inc(t_ev, 1)
                    if bt is not None and s == 4:
                        act.wait_ge(t_mm, T_USES * bt + 3)
                        a.activation(mfcc[0:MFCC], tps[0:MFCC, 0:FRAMES], ACT.Copy).then_inc(t_ev, 1)
                    if bt is not None and s == 5:
                        act.wait_ge(t_mm, T_USES * bt + 4)
                        wait(act, hx_st, 16 * bt)
                        a.activation(hx[:, :, 0:D], bank2(tps, D, TP), ACT.Copy).then_inc(t_ev, 1)
                    if bq is not None and s % 2 == 1:
                        for h in (s - 1, s):
                            act.wait_ge(q_mm, Q_USES * bq + R_USE[h] + 1)
                            wait(act, r_st[h % 2], 16 * (4 * bq + h // 2))
                            a.activation(rsb[:, h % 2], bank2(qps[R_USE[h] % 2], ND, TP), ACT.Copy).then_inc(q_ev[R_USE[h] % 2], 2)
                    if bc is not None and s == 5:
                        act.wait_ge(c_mm, C_USES * bc + 4)
                        a.activation(gT[:, 2], bank2(cps, FRAMES, 128)[:, 0], ACT.Gelu, bias=b1[:, 2:3]).then_inc(c_ev, 1)
                        a.preload_act_table_set(EXP_SET)
                    if bq is not None and s == 3:
                        for t in range(NT):
                            act.wait_ge(q_mm, Q_USES * bq + V_USE[t] + 1)
                            if t == 0:
                                wait(act, vz_in, 2 * bq)
                            a.activation(vtmp[:, t], qps[V_USE[t] % 2][0:TP, 0:D], ACT.Copy).then_inc(q_ev[V_USE[t] % 2], 2)
                    if bt is not None and s == 3:
                        act.wait_ge(t_mm, T_USES * bt + 2)
                        a.activation(logmel[:], tps[0:MELS, 0:FRAMES], ACT.Ln, bias=tiny[:, 0:1]).then_inc(t_ev, 1)
                        a.preload_act_table_set(EXP_SET)

            rounds(act, body)

        @block.vector
        def _(dve):
            v = nc.vector
            dve.wait_ge(w_ld, W_LOADS)
            dve.wait_ge(z_set, 7)
            for p in range(PAIRS):
                dve.wait_ge(wb_mm, p + 1)
                for i in range(2):
                    v.tensor_copy(wbz[64 * i:64 * i + 64, 2 * p + i], qps[p % 2][64 * i:64 * i + 64, 0:ND]).then_inc(wb_ev, 1)

            def pt_copy(b, h):
                if b is not None:
                    n = HEADS * b + h
                    dve.wait_ge(pt_mm, n + 1)
                    wait(dve, pv_mm, n - 1)
                    v.tensor_copy(ptsb[:, h % 2], ptps[:]).then_inc(pt_ev, 1)

            def body(bt, bq, bb_, bc, bd):
                for s in range(SLOTS):
                    if bb_ is not None and s < HEADS:
                        n = HEADS * bb_ + s
                        apart(dve, READY, (s_mm, n + 1), (bsk_ld[s % 4], 16 * (2 * bb_ + s // 4 + 1)),
                              (p_exp, 2 * (n - 1)))
                        for t in range(NT):
                            v.tensor_tensor_reduce(out=ssb[:, s % 2, t], in0=sps[s % 2][:, t], in1=bsk[:, s % 4, t],
                                                   scale=-SCALE, scalar=3.0e38, op0=ALU.add, op1=ALU.min,
                                                   accum_out=mx[:, s % 2, t:t + 1]).then_inc(s_add, 1)
                    if s == 0:
                        pt_copy(bc, HEADS - 1)
                    if s > 0:
                        pt_copy(bb_, s - 1)
                    if bc is not None and s == 1:
                        dve.wait_ge(pv_mm, HEADS * (bc + 1))
                        wait(dve, c_mm, C_USES * (bc - 1) + 1)
                        v.tensor_copy(otsb[:], otps[:]).then_inc(ot_ev, 1)
                    if bb_ is not None and s < HEADS:
                        n = HEADS * bb_ + s
                        dve.wait_ge(p_exp, 2 * n + 2)
                        v.reciprocal(rinv[:, s % 2], rs[:, s % 2]).then_inc(r_inv, 1)
                        dve.wait_ge(r_inv, n + 1)
                        for t in range(NT):
                            v.tensor_scalar(prob[:, s % 2, t], prob[:, s % 2, t], rinv[:, s % 2, t:t + 1], None, ALU.mult).then_inc(p_nrm, 1)
                    if bc is not None and s == 2:
                        dve.wait_ge(c_mm, C_USES * bc + 1)
                        dve.wait_ge(c_hb, bc + 1)
                        v.tensor_tensor(x1[:], bank2(cps, D, TP), hxl[:, :, D:2 * D], ALU.add).then_inc(c_ev, 1)
                    if bc is not None and s == 4:
                        dve.wait_ge(c_mm, C_USES * bc + 2)
                        ps = bank2(cps, FRAMES, KD)
                        v.tensor_scalar(h2T[:, 0], ps[:, 0], n2w[:, 0:1], None, ALU.mult)
                        v.tensor_scalar(h2T[:, 1], ps[:, 1], n2w[:, 1:2], None, ALU.mult).then_inc(c_ev, 1)
                    if bd is not None and s == 1:
                        dve.wait_ge(d_mm, D_USES * bd + 1)
                        wait(dve, c_st, 48 * bd)
                        v.tensor_copy(xnT[:], bank2(cps, FRAMES, KD)).then_inc(d_ev, 1)
                    if bc is not None and s == 3:
                        dve.wait_ge(c_ch, C_CHAIN * bc + 2)
                        v.tensor_scalar(c_v[:], ss[:], 1.0 / D, EPS, ALU.mult, ALU.add).then_inc(c_ch, 1)
                        dve.wait_ge(c_ch, C_CHAIN * bc + 4)
                        for t in range(NT):
                            v.tensor_scalar(h2n[:, t], x1[:, t], c_y[:, t:t + 1], None, ALU.mult).then_inc(c_ch, 1)
                    if bd is not None and s == 3:
                        dve.wait_ge(d_ev, D_USES * bd + 2)
                        v.tensor_scalar(sige[:], sige[:], 1.0, None, ALU.add).then_inc(c_sg, 1)
                        dve.wait_ge(c_sg, 2 * bd + 1)
                        v.reciprocal(xs[:, :, 256:SROW], sige[:]).then_inc(c_sg, 1)
                    if bd is not None and s == 6:
                        dve.wait_ge(d_mm, D_USES * bd + 3)
                        wait(dve, scT_st, 16 * bd)
                        v.tensor_copy(scT[:], tps[0:EXPERTS, 0:FRAMES]).then_inc(d_ev, 1)
                    if bd is not None and s == 0:
                        b0 = D_CHAIN * bd
                        wait(dve, c_st, 48 * bd)
                        dve.wait_ge(d_ch, b0 + 6)
                        for t in range(NT):
                            v.tensor_scalar(xs[:, t, 0:D], h1[:, t], c_mv[:, t, 0:1], d_y[:, t:t + 1], ALU.subtract, ALU.mult).then_inc(d_ch, 1)
                    if bt is not None and s == 5:
                        b0 = T_CHAIN * bt
                        dve.wait_ge(t_ev, T_USES * bt + 4)
                        for t in range(NT):
                            v.bn_stats(t_stats[:, t], hx[:, t, 0:D]).then_inc(t_ch, 1)
                        apart(dve, READY, (t_ch, b0 + 2))
                        for t in range(NT):
                            v.bn_aggr(t_mv[:, t], t_stats[:, t]).then_inc(t_ch, 1)
                        dve.wait_ge(t_ch, b0 + 4)
                        v.tensor_scalar(t_v[:, 0:NT], t_mv[:, :, 1], EPS, None, ALU.add).then_inc(t_ch, 1)
                        dve.wait_ge(t_ch, b0 + 5)
                        v.reciprocal(t_inv[:], t_v[:, 0:NT]).then_inc(t_ch, 1)
                        dve.wait_ge(t_ch, b0 + 6)
                        v.tensor_tensor(t_inv[:], t_inv[:], t_mv[:, :, 1], ALU.mult).then_inc(t_ch, 1)
                        dve.wait_ge(t_ch, b0 + 7)
                        v.tensor_scalar(t_v[:, NT:2 * NT], t_inv[:], EPS, None, ALU.add).then_inc(t_ch, 1)
                    if bt is not None and s == 6:
                        b0 = T_CHAIN * bt
                        wait(dve, hx_st, 16 * bt)
                        dve.wait_ge(t_ch, b0 + 9)
                        for t in range(NT):
                            v.tensor_scalar(hx[:, t, D:2 * D], hx[:, t, 0:D], t_mv[:, t, 0:1], t_y[:, t:t + 1], ALU.subtract, ALU.mult).then_inc(t_ch, 1)
                        for t in range(NT):
                            dve.wait_ge(t_ch, b0 + 10 + t)
                            v.tensor_scalar(h1n[:, t], hx[:, t, D:2 * D], t_y[:, NT + t:NT + t + 1], None, ALU.mult).then_inc(t_ch, 1)
                    if bc is not None and s == 7:
                        b0 = D_CHAIN * bc
                        dve.wait_ge(c_mm, C_USES * bc + 5)
                        dve.wait_ge(c_xb, bc + 1)
                        wait(dve, c_st, 48 * bc)
                        v.tensor_tensor(h1[:], bank2(cps, D, TP), xb[:], ALU.add).then_inc(c_ev, 1)
                        dve.wait_ge(c_ev, C_USES * bc + 5)
                        for t in range(NT):
                            v.bn_stats(c_stats[:, t], h1[:, t]).then_inc(d_ch, 1)
                        apart(dve, READY, (d_ch, b0 + 2))
                        for t in range(NT):
                            v.bn_aggr(c_mv[:, t], c_stats[:, t]).then_inc(d_ch, 1)
                        dve.wait_ge(d_ch, b0 + 4)
                        v.tensor_scalar(d_v[:], c_mv[:, :, 1], EPS, None, ALU.add).then_inc(d_ch, 1)
                    if bt is not None and s == 7:
                        dve.wait_ge(t_mm, T_USES * bt + 5)
                        if bq is not None:
                            dve.wait_ge(q_mm, Q_USES * (bq + 1))
                        ps = bank2(tps, FRAMES, KD)
                        v.tensor_scalar(h1T[:, 0], ps[:, 0], n1w[:, 0:1], None, ALU.mult)
                        v.tensor_scalar(h1T[:, 1], ps[:, 1], n1w[:, 1:2], None, ALU.mult).then_inc(t_ev, 1)

            rounds(dve, body)

        @block.tensor
        def _(pe):
            m = nc.tensor.matmul
            pe.wait_ge(w_ld, W_LOADS)
            for p in range(PAIRS):
                if p >= 2:
                    pe.wait_ge(wb_ev, 2 * (p - 1))
                m(qps[p % 2][:, 0:ND], wpos[:, p * 128:(p + 1) * 128], basis[:], start=True, stop=True).then_inc(wb_mm, 1)
            pe.wait_ge(wb_ev, 2 * PAIRS)
            pe.wait_ge(z_set, 7)

            def transposes(ps, src, s):
                for k in range(NK):
                    for t in range(NT):
                        ins = nc.tensor.transpose(ps[:, k, t * TP:(t + 1) * TP], src[:, t, k * KD:(k + 1) * KD], ident[0:TP, 0:TP])
                ins.then_inc(s, 1)

            def natural(ps, lhsT, rhs, s):
                nk = rhs.shape[1]
                for t in range(NT):
                    for k in range(nk):
                        ins = m(ps[:, t], lhsT[:, k, t * TP:(t + 1) * TP], rhs[:, k], start=k == 0, stop=k == nk - 1)
                ins.then_inc(s, 1)

            def probs_T(b, h):
                if b is not None:
                    n = HEADS * b + h
                    pe.wait_ge(p_nrm, 2 * n + 2)
                    wait(pe, pt_ev, n)
                    for j in range(NT):
                        for t in range(NT):
                            ins = nc.tensor.transpose(ptps[:, j, t * TP:(t + 1) * TP], prob[:, h % 2, t, j * TP:(j + 1) * TP], ident[0:TP, 0:TP])
                    ins.then_inc(pt_mm, 1)

            def values(b, h):
                if b is not None:
                    n = HEADS * b + h
                    if h % 4 == 0:
                        pe.wait_ge(vz_in, 2 * b + 1 + h // 4)
                    if h == 0:
                        wait(pe, ot_ev, b)
                    pe.wait_ge(pt_ev, n + 1)
                    for j in range(NT):
                        ins = m(otps[:, h // 4], vz[:, j, h], ptsb[:, h % 2, j], start=h % 4 == 0 and j == 0, stop=h % 4 == 3 and j == NT - 1)
                    ins.then_inc(pv_mm, 1)

            def body(bt, bq, bb_, bc, bd):
                for s in range(SLOTS):
                    if bb_ is not None and s < HEADS:
                        n = HEADS * bb_ + s
                        if s % 2 == 0:
                            q_evacuated(pe, bb_, QK_USE[s // 2])
                        wait(pe, s_add, 2 * (n - 1))
                        for t in range(NT):
                            ins = m(sps[s % 2][:, t], qu[:, s // 2, t * TP:(t + 1) * TP], kz[:, s], start=True, stop=True)
                        ins.then_inc(s_mm, 1)
                    if s == 0:
                        probs_T(bc, HEADS - 1)
                    if s > 0:
                        probs_T(bb_, s - 1)
                    if bd is not None and s == 1:
                        pe.wait_ge(d_ch, D_CHAIN * bd + D_CHAIN)
                        pe.wait_ge(c_ev, C_USES * bd + 5)
                        transposes(bank2(cps, FRAMES, KD), xs[:, :, 0:D], d_mm)
                    if bc is not None and s == 2:
                        if bd is not None:
                            pe.wait_ge(d_ev, D_USES * bd + 1)
                        pe.wait_ge(ot_ev, bc + 1)
                        natural(bank2(cps, D, TP), otsb, wo, c_mm)
                    if bd is not None and s == 3:
                        pe.wait_ge(d_ev, D_USES * bd + 1)
                        if bc is not None:
                            pe.wait_ge(c_ev, C_USES * bc + 1)
                        natural(cps[0:TP, 0:NT * EXPERTS].rearrange("p (t n) -> p t n", t=NT), xnT, gate, d_mm)
                    if bc is not None and s == 4:
                        if bd is not None:
                            pe.wait_ge(d_ev, D_USES * bd + 2)
                        pe.wait_ge(c_ch, C_CHAIN * bc + C_CHAIN)
                        pe.wait_ge(c_ev, C_USES * bc + 1)
                        transposes(bank2(cps, FRAMES, KD), h2n, c_mm)
                    if bd is not None and s == 6:
                        pe.wait_ge(c_sg, 2 * bd + 2)
                        if bt is not None:
                            pe.wait_ge(t_ev, T_USES * bt + 4)
                        for t in range(NT):
                            ins = nc.tensor.transpose(tps[0:EXPERTS, t * TP:(t + 1) * TP], xs[:, t, 256:SROW], ident[0:TP, 0:TP])
                        ins.then_inc(d_mm, 1)
                    if bc is not None and s == 5:
                        pe.wait_ge(c_ev, C_USES * bc + 2)
                        ps = bank2(cps, FRAMES, 128)
                        for j in range(2):
                            for k in range(NK):
                                ins = m(ps[:, j], w1[:, k, j * 128:(j + 1) * 128], h2T[:, k], start=k == 0, stop=k == NK - 1)
                        ins.then_inc(c_mm, 1)
                    if bc is not None and s == 7:
                        pe.wait_ge(c_ev, C_USES * bc + 4)
                        natural(bank2(cps, D, TP), gT, w2, c_mm)
                    if bt is not None and s in T_SLOT:
                        apart(pe, READY, (t_ev, T_USES * bt + T_SLOT[s]))
                        if T_SLOT[s] == 0:
                            pe.wait_ge(fr_ld, 16 * (bt + 1))
                            m(tps[0:2 * BINS, 0:FRAMES], dft[:], frames[:], start=True, stop=True).then_inc(t_mm, 1)
                        if T_SLOT[s] == 1:
                            m(tps[0:MELS, 0:FRAMES], mel[:], sq[:], start=True, stop=True).then_inc(t_mm, 1)
                        if T_SLOT[s] == 2:
                            m(tps[0:MFCC, 0:FRAMES], dct[:], logmel[:], start=True, stop=True).then_inc(t_mm, 1)
                        if T_SLOT[s] == 3:
                            ps = bank2(tps, D, TP)
                            for t in range(NT):
                                ins = m(ps[:, t], mfcc[:, t * TP:(t + 1) * TP], wproj[:], start=True, stop=True)
                            ins.then_inc(t_mm, 1)
                    if bq is not None and s in QK_SLOT:
                        p = QK_SLOT[s]
                        q_freed(pe, bq, QK_USE[p])
                        if p == 0:
                            pe.wait_ge(t_ev, T_USES * (bq + 1))
                        ps = bank2(qps[QK_USE[p] % 2], FRAMES, 128)
                        for i, wt in enumerate((wq, wk)):
                            for k in range(NK):
                                ins = m(ps[:, i], wt[:, k, p * 128:(p + 1) * 128], h1T[:, k], start=k == 0, stop=k == NK - 1)
                        ins.then_inc(q_mm, 1)
                    if bq is not None and s % 2 == 1:
                        for h in (s - 1, s):
                            q_freed(pe, bq, R_USE[h])
                            if h % 2 == 0:
                                q_evacuated(pe, bq, QK_USE[h // 2])
                            ps = bank2(qps[R_USE[h] % 2], ND, TP)
                            for t in range(NT):
                                ins = m(ps[:, t], qv[:, h // 2, t * TP:(t + 1) * TP], wbz[:, h], start=True, stop=True)
                            ins.then_inc(q_mm, 1)
                    if bc is not None and s == 5:
                        pe.wait_ge(c_ev, C_USES * bc + 3)
                        ps = bank2(cps, FRAMES, 128)
                        for k in range(NK):
                            ins = m(ps[:, 0], w1[:, k, 256:384], h2T[:, k], start=k == 0, stop=k == NK - 1)
                        ins.then_inc(c_mm, 1)
                    if bq is not None and s == 3:
                        for t in range(NT):
                            q_freed(pe, bq, V_USE[t])
                            for k in range(NK):
                                ins = m(qps[V_USE[t] % 2][0:TP, 0:D], h1T[:, k, t * TP:(t + 1) * TP], wv[:, k], start=k == 0, stop=k == NK - 1)
                            ins.then_inc(q_mm, 1)
                    if s == 0:
                        values(bc, HEADS - 1)
                    if s > 0:
                        values(bb_, s - 1)
                    if bt is not None and s == 7:
                        pe.wait_ge(t_ch, T_CHAIN * bt + T_CHAIN)
                        if bd is not None:
                            pe.wait_ge(d_ev, D_USES * bd + 3)
                        pe.wait_ge(t_ev, T_USES * bt + 4)
                        transposes(bank2(tps, FRAMES, KD), h1n, t_mm)

            rounds(pe, body)


W_LOADS = 16 * (21 + 2 * NT)

BF16 = mybir.dt.bfloat16
F32R = mybir.dt.float32r
I32 = mybir.dt.int32
U32 = mybir.dt.uint32

CHUNK = 500
CHUNKS = TOKENS // CHUNK
CT = CHUNK // TP
MS = F_SH // 128
SPLIT = 128 // EXPERTS
SPAN = TOKENS // SPLIT
BLOCKS = SPAN // TP
SCORE_BITS = 30
LO = 32


def expert_blocks():
    p = np.arange(128)
    return (p[:, None] // SPLIT == p[None, :] // SPLIT).astype(np.float32)


def expert_before():
    p = np.arange(128)
    return expert_blocks() * (p[:, None] < p[None, :]).astype(np.float32)


def shared_and_route(nc, w, h1_d, xnT_d, scT_d, out_d, hi_all, lo_all, sem):
    ctx = ExitStack()

    def sb(name, shape, dt=F32):
        return ctx.enter_context(nc.sbuf_tensor("sh_" + name, shape, dt))

    def pb(name, shape):
        return ctx.enter_context(nc.psum_tensor("shp_" + name, shape, F32))

    with ctx:
        ident = sb("ident", [128, 128])
        wg = sb("wg", [KD, NK, F_SH])
        wu = sb("wu", [KD, NK, F_SH])
        wd = sb("wd", [128, MS, D])
        blocks = sb("blocks", [128, 128])
        before = sb("before", [128, 128])
        xT = sb("xT", [KD, 2, NK, CHUNK])
        res = sb("res", [TP, 2, CT, D])
        sg = sb("sg", [128, 2, CHUNK])
        hT = sb("hT", [128, MS, CHUNK])
        y = sb("y", [TP, 2, CT, D])
        sc = sb("sc", [128, SPAN])
        hit = sb("hit", [128, SPAN])
        eq = sb("eq", [128, SPAN])
        run = sb("run", [128, SPAN])
        zero = sb("zero", [128, SPAN])
        thr = sb("thr", [128, 1], I32)
        bit = sb("bit", [128, 1], I32)
        cand = sb("cand", [128, 1], I32)
        take = sb("take", [128, 1], I32)
        cnt = sb("cnt", [128, 1])
        need = sb("need", [128, 1])
        off = sb("off", [128, 1])
        posi = sb("posi", [TP, BLOCKS, 128], I32)
        gps = [pb(f"g{i}", [128, CHUNK]) for i in range(2)]
        ups = [pb(f"u{i}", [128, CHUNK]) for i in range(2)]
        dps = [pb(f"d{i}", [TP, 2, D]) for i in range(2)]
        kps = pb("k", [128, 1])
        pps = pb("p", [TP, BLOCKS // 2, 128])

        w_ld = sem("sh_w_ld")
        sc_ld = sem("sh_sc_ld")
        ini = sem("sh_ini")
        x_ld = [sem(f"sh_x_ld{i}") for i in range(2)]
        gu_mm = sem("sh_gu_mm")
        g_ev = sem("sh_g_ev")
        h_ev = sem("sh_h_ev")
        d_mm = sem("sh_d_mm")
        y_ev = sem("sh_y_ev")
        y_st = [sem(f"sh_y_st{i}") for i in range(2)]
        k_cnt = sem("sh_k_cnt")
        k_mm = sem("sh_k_mm")
        k_ch = sem("sh_k_ch")
        r_ch = sem("sh_r_ch")
        r_mm = sem("sh_r_mm")
        K_CHAIN = 3

        def wait(eng, s, value):
            if not isinstance(value, int) or value > 0:
                eng.wait_ge(s, value)

        def chunks(eng, body):
            for i in range(2):
                body(i, i)
            with eng.Fori(1, CHUNKS // 2) as j:
                for i in range(2):
                    body(2 * j + i, i)

        block = ctx.enter_context(nc.Block())

        @block.sync
        def _(sp):
            sp.dma_start(sc[:], scT_d.rearrange("e (c n) -> (e c) n", n=SPAN)).then_inc(sc_ld, 16)
            for dst, src in ((wg[:], w["WsgT"].rearrange("(k p) n -> p k n", p=KD)),
                             (wu[:], w["WsuT"].rearrange("(k p) n -> p k n", p=KD)),
                             (wd[:], w["WsdT"].rearrange("(k p) n -> p k n", p=128)),
                             (ident[:], w["ident"]), (blocks[:], w["blocks"]), (before[:], w["before"])):
                sp.dma_start(dst, src).then_inc(w_ld, 16)

            def body(c, par):
                wait(sp, y_ev, 2 * (c - 1))
                sp.dma_start(xT[:, par], xnT_d[:, bass.ds(c * CHUNK, CHUNK)].rearrange("(k p) n -> p k n", p=KD)).then_inc(x_ld[par], 16)
                sp.dma_start(res[:, par], h1_d[bass.ds(c * CHUNK, CHUNK), :].rearrange("(t p) n -> p t n", p=TP)).then_inc(x_ld[par], 16)

            chunks(sp, body)

        @block.scalar
        def _(act):
            a = nc.scalar

            def body(c, par):
                for m in range(MS):
                    n = MS * c + m
                    act.wait_ge(gu_mm, 2 * n + 1)
                    wait(act, h_ev, n - 1)
                    a.activation(sg[:, (MS * par + m) % 2], gps[(MS * par + m) % 2][:], ACT.Silu).then_inc(g_ev, 1)
                act.wait_ge(y_ev, 2 * c + 2)
                act.dma_start(out_d[bass.ds(c * CHUNK, CHUNK), :].rearrange("(t p) n -> p t n", p=TP), y[:, par]).then_inc(y_st[par], 16)

            chunks(act, body)
            for i in range(2):
                act.wait_ge(y_st[i], 16 * (CHUNKS // 2))

        @block.vector
        def _(dve):
            v = nc.vector
            v.memset(thr[:], 0).then_inc(ini, 1)
            v.memset(bit[:], 1 << (SCORE_BITS - 1)).then_inc(ini, 1)
            v.memset(zero[:], 0.0).then_inc(ini, 1)
            dve.wait_ge(ini, 3)
            dve.wait_ge(sc_ld, 16)

            def count(k):
                wait(dve, k_ch, K_CHAIN * k)
                v.tensor_tensor(cand[:], thr[:], bit[:], ALU.bitwise_or).then_inc(k_ch, 1)
                dve.wait_ge(k_ch, K_CHAIN * k + 1)
                v.tensor_scalar(hit[:], sc[:], cand[:].bitcast(F32), 0.0, ALU.is_ge, ALU.add, accum_out=cnt[:]).then_inc(k_cnt, 1)

            def update(k):
                dve.wait_ge(k_mm, k + 1)
                v.tensor_scalar(take[:], kps[:], float(CAPACITY), None, ALU.is_ge).then_inc(k_ch, 1)
                dve.wait_ge(k_ch, K_CHAIN * k + 2)
                v.tensor_single_scalar(bit[:], bit[:], 1, ALU.logical_shift_right)
                v.copy_predicated(thr[:], take[:], cand[:]).then_inc(k_ch, 1)

            def gated(c, par, m):
                n = MS * c + m
                dve.wait_ge(gu_mm, 2 * n + 2)
                dve.wait_ge(g_ev, n + 1)
                wait(dve, d_mm, 2 * c)
                v.tensor_tensor(hT[:, m], sg[:, (MS * par + m) % 2], ups[(MS * par + m) % 2][:], ALU.mult).then_inc(h_ev, 1)

            def body(c, par):
                count(2 * c)
                gated(c, par, 0)
                update(2 * c)
                count(2 * c + 1)
                gated(c, par, 1)
                gated(c, par, 2)
                update(2 * c + 1)
                dve.wait_ge(x_ld[par], 32 * ((c - par) // 2 + 1) if isinstance(c, int) else 16 * (c - par) + 32)
                wait(dve, y_st[par], 16 * (c // 2) if isinstance(c, int) else 8 * (c - par))
                for i in range(2):
                    dve.wait_ge(d_mm, 2 * c + i + 1)
                    v.tensor_tensor(y[:, par, 2 * i:2 * i + 2], dps[i][:], res[:, par, 2 * i:2 * i + 2], ALU.add).then_inc(y_ev, 1)

            assert 2 * CHUNKS >= SCORE_BITS
            chunks(dve, body)

            step = [0]

            def then(ins):
                step[0] += 1
                ins.then_inc(r_ch, 1)
                dve.wait_ge(r_ch, step[0])

            dve.wait_ge(k_ch, K_CHAIN * 2 * CHUNKS)
            t = thr[:].bitcast(F32)
            then(v.tensor_scalar(hit[:], sc[:], t, 0.0, ALU.is_gt, ALU.add, accum_out=cnt[:]))
            then(v.tensor_scalar(eq[:], sc[:], t, None, ALU.is_equal))
            then(v.tensor_tensor_scan(run[:], eq[:], zero[:], 0.0, ALU.add, ALU.add))
            dve.wait_ge(r_mm, 1)
            then(v.tensor_scalar(need[:], kps[:], -1.0, float(CAPACITY), ALU.mult, ALU.add))
            dve.wait_ge(r_mm, 2)
            then(v.tensor_tensor(need[:], need[:], kps[:], ALU.subtract))
            then(v.scalar_tensor_tensor(out=eq[:], in0=run[:], scalar=need[:], in1=eq[:], op0=ALU.is_le, op1=ALU.mult))
            then(v.tensor_tensor(hit[:], hit[:], eq[:], ALU.add))
            then(v.tensor_tensor_scan(run[:], hit[:], zero[:], 0.0, ALU.add, ALU.add))
            dve.wait_ge(r_mm, 3)
            then(v.tensor_copy(off[:], kps[:]))
            then(v.scalar_tensor_tensor(out=run[:], in0=run[:], scalar=off[:], in1=hit[:], op0=ALU.add, op1=ALU.mult))
            then(v.tensor_scalar(run[:], run[:], -1.0, None, ALU.add))
            half = BLOCKS // 2
            for i in range(2):
                dve.wait_ge(r_mm, 4 + i)
                then(v.tensor_copy(posi[:, i * half:(i + 1) * half], pps[:]))
            then(v.tensor_single_scalar(hi_all[:], posi[:], 5, ALU.arith_shift_right))
            then(v.tensor_single_scalar(lo_all[:], posi[:], LO - 1, ALU.bitwise_and))

        @block.tensor
        def _(pe):
            m_ = nc.tensor.matmul
            pe.wait_ge(w_ld, 96)

            def tally(k):
                pe.wait_ge(k_cnt, k + 1)
                m_(kps[:], blocks[:], cnt[:], start=True, stop=True).then_inc(k_mm, 1)

            def body(c, par):
                pe.wait_ge(x_ld[par], 32 * ((c - par) // 2 + 1) if isinstance(c, int) else 16 * (c - par) + 32)
                for m in range(MS):
                    n = MS * c + m
                    b = (MS * par + m) % 2
                    for ps, wt, s in ((gps[b], wg, g_ev), (ups[b], wu, h_ev)):
                        wait(pe, s, n - 1)
                        for k in range(NK):
                            ins = m_(ps[:], wt[:, k, m * 128:(m + 1) * 128], xT[:, par, k], start=k == 0, stop=k == NK - 1)
                        ins.then_inc(gu_mm, 1)
                    if m == 0:
                        tally(2 * c)
                tally(2 * c + 1)
                pe.wait_ge(h_ev, MS * (c + 1))
                for i in range(2):
                    wait(pe, y_ev, 2 * (c - 1) + i + 1)
                    for t in range(2):
                        for m in range(MS):
                            ins = m_(dps[i][:, t], hT[:, m, (2 * i + t) * TP:(2 * i + t + 1) * TP], wd[:, m], start=m == 0, stop=m == MS - 1)
                    ins.then_inc(d_mm, 1)

            chunks(pe, body)
            pe.wait_ge(r_ch, 1)
            m_(kps[:], blocks[:], cnt[:], start=True, stop=True).then_inc(r_mm, 1)
            pe.wait_ge(r_ch, 4)
            m_(kps[:], before[:], run[:, SPAN - 1:SPAN], start=True, stop=True).then_inc(r_mm, 1)
            pe.wait_ge(r_ch, 8)
            m_(kps[:], before[:], run[:, SPAN - 1:SPAN], start=True, stop=True).then_inc(r_mm, 1)
            for i in range(2):
                pe.wait_ge(r_ch, 11 + i)
                for j in range(BLOCKS // 2):
                    b = i * (BLOCKS // 2) + j
                    ins = nc.tensor.transpose(pps[:, j], run[:, b * TP:(b + 1) * TP], ident[:])
                ins.then_inc(r_mm, 1)


def experts(nc, w, xs_d, idx_d, out_d, hi_all, lo_all, sem, n_exp=EXPERTS):
    ctx = ExitStack()

    def sb(name, shape, dt=F32):
        return ctx.enter_context(nc.sbuf_tensor("ex_" + name, shape, dt))

    def pb(name, shape):
        return ctx.enter_context(nc.psum_tensor("exp_" + name, shape, F32))

    CAP_T = CAPACITY // TP
    ME = F_EXP // 128
    HALF = CAPACITY // 2
    HT = HALF // TP

    with ctx:
        ident = sb("ident", [128, 128])
        iota = sb("iota", [TP, LO])
        row = sb("row", [TP, 1])
        tile = sb("tile", [TP, BLOCKS * SPLIT])
        wraw = sb("wraw", [128, 2, 2, F_EXP])
        wsp = sb("wsp", [128, 2, 3, F_EXP], F32R)
        wd = sb("wd", [128, ME, D])
        one_hi = sb("one_hi", [TP, BLOCKS, SPLIT, LO], BF16)
        one_lo = sb("one_lo", [TP, BLOCKS, SPLIT, LO], BF16)
        val = sb("val", [TP, BLOCKS * SPLIT, 2, LO], BF16)
        lst = sb("lst", [LO, LO])
        lsti = sb("lsti", [LO, LO], U32)
        idxg = sb("idxg", [TP, CAP_T], U32)
        idxs = sb("idxs", [TP, CAP_T], U32)
        xg = sb("xg", [TP, CAP_T, SROW])
        gsc = sb("gsc", [TP, CAP_T])
        xsp = sb("xsp", [128, 2, 2, CAPACITY], F32R)
        sg = sb("sg", [128, 2, HALF])
        hT = sb("hT", [128, ME, CAPACITY])
        y = sb("y", [TP, CAP_T, D])
        gps = [pb(f"g{i}", [128, HALF]) for i in range(2)]
        ups = [pb(f"u{i}", [128, HALF]) for i in range(2)]
        dps = [pb(f"d{i}", [TP, 2, D]) for i in range(2)]
        tps = pb("t", [128, HT, TP])
        lps = pb("l", [LO, 2 * LO])

        c_ld = sem("ex_c_ld")
        wgu_ld = sem("ex_wgu_ld")
        w_hi = sem("ex_w_hi")
        w_lo = sem("ex_w_lo")
        t_hi = sem("ex_t_hi")
        wd_ld = sem("ex_wd_ld")
        hot = sem("ex_hot")
        l_mm = sem("ex_l_mm")
        l_ev = sem("ex_l_ev")
        l_st = sem("ex_l_st")
        ig_ld = sem("ex_ig_ld")
        is_ld = sem("ex_is_ld")
        gat = sem("ex_gat")
        t_mm = sem("ex_t_mm")
        t_ev = sem("ex_t_ev")
        sc_ev = sem("ex_sc_ev")
        gu_mm = sem("ex_gu_mm")
        g_ev = sem("ex_g_ev")
        h_ev = sem("ex_h_ev")
        d_mm = sem("ex_d_mm")
        y_ev = sem("ex_y_ev")
        sca = sem("ex_sca")
        UNITS = 2 * ME
        TR = 2 * 2
        WSP = 2 * 2
        DN = CAP_T // 2
        HOT = 4

        def wait(eng, s, value):
            if not isinstance(value, int) or value > 0:
                eng.wait_ge(s, value)

        def turns(eng, body):
            body(0, True, True)
            with eng.Fori(1, n_exp - 2) as e:
                body(e, True, True)
            body(n_exp - 2, True, False)
            body(n_exp - 1, False, False)

        block = ctx.enter_context(nc.Block())

        @block.sync
        def _(sp):
            for dst, src in ((ident[:], w["ident"]), (iota[:], w["iota"]), (row[:], w["row"]), (tile[:], w["tile"])):
                sp.dma_start(dst, src).then_inc(c_ld, 16)

            def load_gu(e):
                wait(sp, w_lo, WSP * e)
                for i, src in enumerate((w["WgT"], w["WuT"])):
                    one = src[bass.ds(e, 1)].rearrange("a d n -> d (a n)")
                    sp.dma_start(wraw[:, i, 0], one[0:128]).then_inc(wgu_ld, 16)
                    for half in range(2):
                        sp.dma_start(wraw[half * 64:half * 64 + 64, i, 1], one[128:D]).then_inc(wgu_ld, 16)

            def load_d(e):
                wait(sp, d_mm, DN * e)
                sp.dma_start(wd[:], w["WdT"][bass.ds(e, 1)].rearrange("a (k p) n -> p (a k) n", p=128)).then_inc(wd_ld, 16)

            def store_list(e):
                wait(sp, l_ev, 2 * e + 2)
                sp.dma_start(idx_d[bass.ds(e, 1), :].rearrange("a (p n) -> p (a n)", n=LO), lsti[:]).then_inc(l_st, 16)

            def load_idx(dst, s, e):
                wait(sp, l_st, 16 * (e + 1))
                sp.dma_start(dst[:], idx_d[bass.ds(e, 1), 0:CAPACITY].rearrange("a (p t) -> p (a t)", t=CAP_T)).then_inc(s, 16)

            load_gu(0)
            load_d(0)
            store_list(0)
            load_idx(idxg, ig_ld, 0)
            store_list(1)

            def body(e, more, lists):
                wait(sp, sca, 16 * CAP_T * e)
                load_idx(idxs, is_ld, e)
                if more:
                    load_gu(e + 1)
                if more:
                    wait(sp, gat, 16 * CAP_T * (e + 1))
                    load_idx(idxg, ig_ld, e + 1)
                if lists:
                    store_list(e + 2)
                if more:
                    load_d(e + 1)

            turns(sp, body)

        @block.gpsimd
        def _(pool):
            g = nc.gpsimd
            last = pool.to_reg(TOKENS - 1)

            def gather(e):
                apart(pool, (c_ld, 64), (ig_ld, 16 * (e + 1)), (t_mm, TR * e), (sc_ev, e))
                for t in range(CAP_T):
                    g.indirect_dma_start(xg[:, t], None, xs_d[:, :], bass.IndirectOffsetOnAxis(idxg[:, t:t + 1], 0),
                                         bounds_check=last).then_inc(gat, 16)

            gather(0)

            def body(e, more, lists):
                if more:
                    gather(e + 1)
                for t in range(CAP_T):
                    apart(pool, (c_ld, 64), *[(is_ld, 16 * (e + 1))] * (t == 0), *[(y_ev, DN * e + t // 2 + 1)] * (t % 2 == 0),
                               (sca, 16 * (CAP_T * e + t)))
                    g.indirect_dma_start(out_d[:, :], bass.IndirectOffsetOnAxis(idxs[:, t:t + 1], 0), y[:, t], None,
                                         bounds_check=last, compute_op=ALU.add).then_inc(sca, 16)

            turns(pool, body)
            pool.wait_ge(sca, 16 * CAP_T * n_exp)

        @block.scalar
        def _(act):
            a = nc.scalar

            def weights_high(e):
                act.wait_ge(wgu_ld, 96 * (e + 1))
                wait(act, gu_mm, 2 * UNITS * e)
                for i in range(2):
                    a.activation(wsp[:, i, 0], wraw[:, i, 0], ACT.Copy).then_inc(w_hi, 1)
                    a.activation(wsp[:, i, 2], wraw[:, i, 1], ACT.Copy).then_inc(w_hi, 1)

            def rows_high(e, j):
                act.wait_ge(t_mm, TR * e + j + 1)
                k, half = j % 2, j // 2
                a.activation(xsp[:, 0, k, half * HALF:(half + 1) * HALF], tps[:].rearrange("p t n -> p (t n)"), ACT.Copy).then_inc(t_hi, 1)

            weights_high(0)
            for j in range(TR):
                rows_high(0, j)

            def body(e, more, lists):
                for n in range(UNITS):
                    act.wait_ge(gu_mm, 2 * (UNITS * e + n) + 1)
                    wait(act, h_ev, UNITS * e + n - 1)
                    a.activation(sg[:, n % 2], gps[n % 2][:], ACT.Silu).then_inc(g_ev, 1)
                if more:
                    for j in range(TR):
                        rows_high(e + 1, j)
                        if j == 0:
                            weights_high(e + 1)

            turns(act, body)

        @block.vector
        def _(dve):
            v = nc.vector
            dve.wait_ge(c_ld, 64)

            def one_hots(e, step):
                shape = [TP, BLOCKS, SPLIT, LO]
                own = bass.ds(e * SPLIT, SPLIT)
                io = iota[:].rearrange("p (a b n) -> p a b n", a=1, b=1).to_broadcast(shape)
                flat = one_lo[:].rearrange("p a b n -> p (a b) n")
                if step == 0:
                    wait(dve, l_mm, e)
                    v.tensor_tensor(one_hi[:], hi_all[:, :, own].rearrange("p a (b n) -> p a b n", n=1).to_broadcast(shape), io, ALU.is_equal).then_inc(hot, 1)
                if step == 1:
                    v.tensor_tensor(one_lo[:], lo_all[:, :, own].rearrange("p a (b n) -> p a b n", n=1).to_broadcast(shape), io, ALU.is_equal).then_inc(hot, 1)
                if step == 2:
                    dve.wait_ge(hot, HOT * e + 2)
                    v.tensor_scalar(val[:, :, 0], flat, row[:, 0:1], None, ALU.mult).then_inc(hot, 1)
                if step == 3:
                    v.tensor_tensor(val[:, :, 1], flat, tile[:].rearrange("p (a n) -> p a n", n=1).to_broadcast([TP, BLOCKS * SPLIT, LO]), ALU.mult).then_inc(hot, 1)

            def list_out(e):
                dve.wait_ge(l_mm, e + 1)
                wait(dve, l_st, 16 * e)
                v.tensor_copy(lst[:], lps[:, 0:LO]).then_inc(l_ev, 1)
                dve.wait_ge(l_ev, 2 * e + 1)
                v.scalar_tensor_tensor(out=lsti[:], in0=lps[:, LO:2 * LO], scalar=float(TP), in1=lst[:], op0=ALU.mult, op1=ALU.add).then_inc(l_ev, 1)

            def rows_in(e, j):
                dve.wait_ge(t_mm, TR * e + j + 1)
                k, half = j % 2, j // 2
                dve.wait_ge(t_hi, TR * e + j + 1)
                part = slice(half * HALF, (half + 1) * HALF)
                v.tensor_tensor(xsp[:, 1, k, part], tps[:].rearrange("p t n -> p (t n)"), xsp[:, 0, k, part].bitcast(F32), ALU.subtract).then_inc(t_ev, 1)

            def weights_low(e, j):
                i, k = j // 2, j % 2
                dve.wait_ge(w_hi, WSP * e + j + 1)
                half = slice(0, 128) if k == 0 else slice(64, 128)
                v.tensor_tensor(wsp[half, i, 1 + k], wraw[half, i, k], wsp[half, i, 2 * k].bitcast(F32), ALU.subtract).then_inc(w_lo, 1)

            def scores_in(e):
                dve.wait_ge(gat, 16 * CAP_T * (e + 1))
                wait(dve, y_ev, DN * e)
                v.tensor_copy(gsc[:], xg[:, :, bass.ds(2 * 128 + e, 1)].rearrange("p t n -> p (t n)")).then_inc(sc_ev, 1)

            for step in range(HOT):
                one_hots(0, step)
            list_out(0)
            for step in range(HOT):
                one_hots(1, step)
            list_out(1)
            for j in range(TR):
                weights_low(0, j)
                rows_in(0, j)
            scores_in(0)

            def body(e, more, lists):
                for n in range(UNITS):
                    dve.wait_ge(gu_mm, 2 * (UNITS * e + n) + 2)
                    dve.wait_ge(g_ev, UNITS * e + n + 1)
                    wait(dve, d_mm, DN * e)
                    m, half = n % ME, n // ME
                    v.tensor_tensor(hT[:, m, half * HALF:(half + 1) * HALF], sg[:, n % 2], ups[n % 2][:], ALU.mult).then_inc(h_ev, 1)
                    if lists and n >= UNITS - 2 * HOT and n % 2 == 0:
                        one_hots(e + 2, (n - UNITS + 2 * HOT) // 2)
                for j in range(DN):
                    if more:
                        rows_in(e + 1, j)
                        weights_low(e + 1, j)
                    if j == 0:
                        dve.wait_ge(sc_ev, e + 1)
                        wait(dve, sca, 16 * CAP_T * e)
                    dve.wait_ge(d_mm, DN * e + j + 1)
                    for i in range(2):
                        t = 2 * j + i
                        ins = v.tensor_scalar(y[:, t], dps[j % 2][:, i], gsc[:, t:t + 1], None, ALU.mult)
                    ins.then_inc(y_ev, 1)
                if more:
                    dve.wait_ge(y_ev, DN * (e + 1))
                    scores_in(e + 1)
                if lists:
                    list_out(e + 2)

            turns(dve, body)

        @block.tensor
        def _(pe):
            m_ = nc.tensor.matmul
            pe.wait_ge(c_ld, 64)

            def list_mm(e):
                pe.wait_ge(hot, HOT * (e + 1))
                wait(pe, l_ev, 2 * e)
                for b in range(BLOCKS):
                    for c in range(SPLIT):
                        n = b * SPLIT + c
                        ins = m_(lps[:], one_hi[:, b, c], val[:, n].rearrange("p a n -> p (a n)"), start=n == 0, stop=n == BLOCKS * SPLIT - 1)
                ins.then_inc(l_mm, 1)

            def rows_T(e, j):
                k, half = j % 2, j // 2
                if j == 0:
                    pe.wait_ge(gat, 16 * CAP_T * (e + 1))
                wait(pe, t_ev, TR * e + j)
                for t in range(HT):
                    ins = nc.tensor.transpose(tps[:, t], xg[:, half * HT + t, k * 128:(k + 1) * 128], ident[0:TP, 0:TP])
                ins.then_inc(t_mm, 1)

            list_mm(0)
            list_mm(1)
            for j in range(TR):
                rows_T(0, j)

            def body(e, more, lists):
                pe.wait_ge(w_lo, WSP * (e + 1))
                pe.wait_ge(t_ev, TR * (e + 1))
                for n in range(UNITS):
                    m, half = n % ME, n // ME
                    for i, (ps, s) in enumerate(((gps, g_ev), (ups, h_ev))):
                        wait(pe, s, UNITS * e + n - 1)
                        for k, (wk, xp, xk) in enumerate(((0, 0, 0), (1, 0, 0), (0, 1, 0), (2, 0, 1), (2, 1, 1))):
                            ins = m_(ps[n % 2][:], wsp[:, i, wk, m * 128:(m + 1) * 128], xsp[:, xp, xk, half * HALF:(half + 1) * HALF], start=k == 0, stop=k == 4)
                        ins.then_inc(gu_mm, 1)
                pe.wait_ge(wd_ld, 16 * (e + 1))
                for j in range(DN):
                    if more:
                        rows_T(e + 1, j)
                    if j == 0:
                        pe.wait_ge(h_ev, UNITS * (e + 1))
                    wait(pe, y_ev, DN * e + j - 1)
                    for i in range(2):
                        t = 2 * j + i
                        for m in range(ME):
                            ins = m_(dps[j % 2][:, i], hT[:, m, t * TP:(t + 1) * TP], wd[:, m], start=m == 0, stop=m == ME - 1)
                    ins.then_inc(d_mm, 1)
                if lists:
                    list_mm(e + 2)

            turns(pe, body)


def audio_tower(nc, w, out_d):
    def scratch(name, shape, dt=F32):
        return nc.dram_tensor(name, shape, dt, kind="Internal").ap()

    hx_d = scratch("hx_d", (TOKENS, 2 * D))
    bias_d = scratch("bias_d", (HEADS, FRAMES, PITCH))
    h1_d = scratch("h1_d", (TOKENS, D))
    xs_d = scratch("xs_d", (TOKENS, SROW))
    xnT_d = scratch("xnT_d", (D, TOKENS))
    scT_d = scratch("scT_d", (EXPERTS, TOKENS))
    idx_d = scratch("idx_d", (EXPERTS, LO * LO), U32)
    with ExitStack() as ctx:
        def sem(name):
            return ctx.enter_context(nc.semaphore(name))

        tower(nc, w, hx_d, bias_d, h1_d, xs_d, xnT_d, scT_d, sem)
        hi_all = ctx.enter_context(nc.sbuf_tensor("hi_all", [TP, BLOCKS, 128], I32))
        lo_all = ctx.enter_context(nc.sbuf_tensor("lo_all", [TP, BLOCKS, 128], I32))
        shared_and_route(nc, w, h1_d, xnT_d, scT_d, out_d, hi_all, lo_all, sem)
        experts(nc, w, xs_d, idx_d, out_d, hi_all, lo_all, sem)


def constants():
    block, part = np.divmod(np.arange(BLOCKS * SPLIT), SPLIT)
    return {
        "ident": np.eye(128, dtype=np.float32), "dft": dft_table(), "basis": basis_table(),
        "blocks": expert_blocks(), "before": expert_before(),
        "iota": np.tile(np.arange(LO, dtype=np.float32), (TP, 1)),
        "row": np.arange(TP, dtype=np.float32)[:, None],
        "tile": np.tile((part * BLOCKS + block).astype(np.float32), (TP, 1)),
    }


def layout(i):
    a, f, t = "L0_attn_", "L0_ffn_", "L0_tok_"
    framed = i["x"][:, :FRAMES * FRAME_STEP].reshape(BATCH, FRAMES, FRAME_STEP)[:, :, :FRAME_LEN]
    return {
        "frames": framed.transpose(2, 0, 1).reshape(FRAME_LEN, TOKENS),
        "melT": i[t + "mel_filters"].T, "dctT": i[t + "dct"].T,
        "w_proj": i[t + "w_proj"], "b_proj": i[t + "b_proj"].reshape(1, D),
        "wq": i[a + "wq"], "wk": i[a + "wk"], "wv": i[a + "wv"], "wo": i[a + "wo"],
        "w1": i[a + "w1"], "w2": i[a + "w2"], "b2": i[a + "b2"], "bo": i[a + "bo"],
        "n1w": i[a + "norm1_w"].reshape(NK, KD).T, "n2w": i[a + "norm2_w"].reshape(NK, KD).T,
        "b1": i[a + "b1"].reshape(DFF // 128, 128).T,
        "u": i[a + "u_param"].reshape(PAIRS, 128).T, "v": i[a + "v_param"].reshape(PAIRS, 128).T,
        "w_posT": i[a + "w_pos"].transpose(2, 0, 1).reshape(N_POS, HEADS * DK),
        "gateT": i[f + "gate_weight"].T,
        "WsgT": i[f + "Ws_g"].T, "WsuT": i[f + "Ws_u"].T, "WsdT": i[f + "Ws_d"].T,
        "WgT": i[f + "Wg"].transpose(0, 2, 1), "WuT": i[f + "Wu"].transpose(0, 2, 1),
        "WdT": i[f + "Wd"].transpose(0, 2, 1),
    }


def kernel(**inputs):
    import concourse.bacc as bacc
    from concourse.bass_utils import run_bass_kernel_spmd

    nc = bacc.Bacc("TRN2", target_bir_lowering=False, num_devices=1)
    arrays = {k: np.ascontiguousarray(v) for k, v in {**layout(inputs), **constants()}.items()}
    w = {k: nc.dram_tensor(k, v.shape, mybir.dt.from_np(v.dtype), kind="ExternalInput").ap() for k, v in arrays.items()}
    out_d = nc.dram_tensor("out", (TOKENS, D), F32, kind="ExternalOutput").ap()
    audio_tower(nc, w, out_d)
    r = run_bass_kernel_spmd(nc, [arrays], core_ids=[0])
    return r.results[0]["out"].reshape(BATCH, FRAMES, D)
```

```python
import math
from contextlib import ExitStack

import numpy as np
import concourse.bass as bass
from concourse import mybir

F32 = mybir.dt.float32
F32R = mybir.dt.float32r
ALU = mybir.AluOpType
ACT = mybir.ActivationFunctionType
AX_X = mybir.AxisListType.X

BATCH, AUDIO = 32, 40000
FRAME_LEN, FRAME_STEP = 100, 160
FRAMES = 1 + (AUDIO - FRAME_LEN) // FRAME_STEP
BINS = FRAME_LEN // 2 + 1
MELS, MFCC, D = 40, 13, 192
HEADS, DK = 8, 64
DV = D // HEADS
N_POS = 32
DFF = 2 * D
EPS = 1e-5
TOKENS = BATCH * FRAMES
EXPERTS, TOP_K = 16, 2
CAPACITY = math.ceil(TOKENS / EXPERTS * TOP_K)
F_EXP = 4 * D
F_SH = F_EXP // 2

TP = 125
NT = FRAMES // TP
KD = 96
NK = D // KD
PAIRS = HEADS // 2
RANGE = 125
ND = 2 * RANGE + 1
NDE = ND + 1
PITCH = 2 * FRAMES - 1
SLOTS = HEADS
SCALE = 1.0 / math.sqrt(DK)
COLS = {"wq": (0, HEADS * DK), "wk": (HEADS * DK, 2 * HEADS * DK), "wv": (2 * HEADS * DK, 2 * HEADS * DK + D),
        "w1": (2 * HEADS * DK + D, 2 * HEADS * DK + D + DFF)}
ALL_COLS = 2 * HEADS * DK + D + DFF
SROW = 2 * 128 + EXPERTS


EXP_SET = "exp_and_others"


def dft_table():
    n = np.arange(FRAME_LEN, dtype=np.float64)
    window = 0.54 - 0.46 * np.cos(2.0 * np.pi * n / (FRAME_LEN - 1))
    angle = 2.0 * np.pi * np.outer(n, np.arange(BINS)) / FRAME_LEN
    return (np.concatenate([np.cos(angle), np.sin(angle)], 1) * window[:, None]).astype(np.float32)


def basis_table():
    half = N_POS // 2
    rate = np.exp(np.log(np.float32((FRAMES + 1) / 2.0)) / np.float32(half)).astype(np.float32)
    widths = rate ** np.arange(1, half + 1, dtype=np.float32)
    assert widths[-1] < RANGE + 1
    dist = np.arange(-RANGE, RANGE + 1).astype(np.float32)
    inside = (np.abs(dist)[None, :] <= widths[:, None]).astype(np.float32)
    return np.concatenate([inside, np.sign(dist)[None, :] * inside], 0)


PARTS = ((0, 0, 0), (1, 0, 0), (0, 1, 0), (2, 0, 1), (2, 1, 1))


def apart(eng, ready, *waits):
    waits = [(s, v if isinstance(v, int) else eng.to_reg(v)) for s, v in waits]
    eng.wait_ge(*ready)
    for s, v in waits:
        if not isinstance(v, int) or v > 0:
            eng.wait_ge(s, v)


def tower(nc, w, hx_d, bias_d, h1_d, xs_d, xnT_d, scT_d, sem, n_batch=BATCH):
    ctx = ExitStack()

    def sb(name, shape, dt=F32):
        return ctx.enter_context(nc.sbuf_tensor("sb_" + name, shape, dt))

    def pb(name, shape):
        return ctx.enter_context(nc.psum_tensor("ps_" + name, shape, F32))

    with ctx:
        ident = sb("ident", [128, 128])
        dft = sb("dft", [FRAME_LEN, 2 * BINS])
        mel = sb("mel", [2 * BINS, MELS])
        dct = sb("dct", [MELS, MFCC])
        wproj = sb("wproj", [MFCC + 1, D])
        wraw = sb("wraw", [128, 2, ALL_COLS])
        wsp = sb("wsp", [128, 3, ALL_COLS], F32R)
        wo = sb("wo", [KD, NK, D])
        w2 = sb("w2", [128, DFF // 128, D])
        gate = sb("gate", [KD, NK, EXPERTS])
        n1w = sb("n1w", [128, 2])
        n2w = sb("n2w", [128, 2])
        b1 = sb("b1", [128, DFF // 128])
        ucol = sb("ucol", [128, PAIRS])
        vcol = sb("vcol", [128, PAIRS])
        vmu = sb("vmu", [128, PAIRS])
        wpz = sb("wpz", [128, PAIRS, 2, 2, N_POS])
        cq = sb("cq", [128, PAIRS])
        braw = sb("braw", [128, 2, NDE])
        bz = sb("bz", [128, 2, NDE], F32R)
        bb = sb("bb", [TP, NT, 2 * D])
        tiny = sb("tiny", [MELS, 1])
        power = sb("power", [TP, 2 * NT])
        zeros = sb("zeros", [TP, PITCH])
        frames = sb("frames", [FRAME_LEN, FRAMES])
        sq = sb("sq", [2 * BINS, FRAMES])
        logmel = sb("logmel", [MELS, FRAMES])
        mfcc = sb("mfcc", [MFCC + 1, FRAMES])
        hx = sb("hx", [TP, NT, 2 * D])
        t_stats = sb("t_stats", [TP, NT, 6])
        t_mv = sb("t_mv", [TP, NT, 2])
        t_inv = sb("t_inv", [TP, NT])
        t_v = sb("t_v", [TP, 2 * NT])
        t_y = sb("t_y", [TP, 2 * NT])
        h1n = sb("h1n", [TP, NT, 256])
        hsp = sb("hsp", [128, 2, 2, FRAMES], F32R)
        qu = sb("qu", [128, PAIRS, FRAMES])
        qw = sb("qw", [128, FRAMES], F32R)
        kz = sb("kz", [128, HEADS, FRAMES])
        vz = sb("vz", [TP, NT, HEADS, KD])
        vtmp = sb("vtmp", [TP, NT, D])
        rsb = sb("rsb", [TP, 2, NT, ND])
        bsk = sb("bsk", [TP, 4, NT, FRAMES])
        ssb = sb("ssb", [TP, 2, NT, FRAMES])
        prob = sb("prob", [TP, 2, NT, FRAMES])
        mx = sb("mx", [TP, 2, NT])
        rs = sb("rs", [TP, 2, NT])
        rinv = sb("rinv", [TP, 2, NT])
        ptsb = sb("ptsb", [TP, 2, NT, FRAMES])
        otsb = sb("otsb", [KD, NK, FRAMES])
        hxl = sb("hxl", [TP, NT, 2 * D])
        x1 = sb("x1", [TP, NT, D])
        xb = sb("xb", [TP, NT, D])
        junk = sb("junk", [TP, D])
        ss = sb("ss", [TP, NT])
        c_v = sb("c_v", [TP, NT])
        c_y = sb("c_y", [TP, NT])
        h2n = sb("h2n", [TP, NT, 256])
        h2sp = sb("h2sp", [128, 2, 2, FRAMES], F32R)
        gT = sb("gT", [128, DFF // 128, FRAMES])
        h1 = sb("h1", [TP, NT, D])
        c_stats = sb("c_stats", [TP, NT, 6])
        c_mv = sb("c_mv", [TP, NT, 2])
        d_v = sb("d_v", [TP, NT])
        d_y = sb("d_y", [TP, NT])
        xs = sb("xs", [TP, NT, SROW])
        xnT = sb("xnT", [KD, NK, FRAMES])
        sige = sb("sige", [TP, NT, EXPERTS])
        scT = sb("scT", [EXPERTS, FRAMES])
        sps = [pb(f"sps{i}", [TP, NT, FRAMES]) for i in range(2)]
        ptps = pb("ptps", [TP, NT, FRAMES])
        otps = pb("otps", [KD, NK, FRAMES])
        qps = [pb(f"qps{i}", [128, 512]) for i in range(2)]
        tps = pb("tps", [128, 512])
        cps = pb("cps", [128, 512])

        w_ld = sem("w_ld")
        READY = (w_ld, W_LOADS)
        z_set = sem("z_set")
        zero_st = sem("zero_st")
        cq_mm = sem("cq_mm")
        ini = sem("ini")
        w_hi = sem("w_hi")
        t_hi = sem("t_hi")
        c_hi = sem("c_hi")
        fr_ld = sem("fr_ld")
        t_mm = sem("t_mm")
        t_ev = sem("t_ev")
        t_ch = sem("t_ch")
        hx_st = sem("hx_st")
        q_mm = sem("q_mm")
        q_ev = [sem(f"q_ev{i}") for i in range(2)]
        r_st = [sem(f"r_st{i}") for i in range(2)]
        bsk_ld = [sem(f"bsk_ld{i}") for i in range(4)]
        s_mm = sem("s_mm")
        s_add = sem("s_add")
        p_exp = sem("p_exp")
        r_inv = sem("r_inv")
        p_nrm = sem("p_nrm")
        pt_mm = sem("pt_mm")
        pt_ev = sem("pt_ev")
        pv_mm = sem("pv_mm")
        ot_ev = sem("ot_ev")
        hxl_ld = sem("hxl_ld")
        c_hb = sem("c_hb")
        c_mm = sem("c_mm")
        c_ev = sem("c_ev")
        c_ch = sem("c_ch")
        c_xb = sem("c_xb")
        d_ch = sem("d_ch")
        c_sg = sem("c_sg")
        x_dup = sem("x_dup")
        d_mm = sem("d_mm")
        d_ev = sem("d_ev")
        vz_in = sem("vz_in")
        c_st = sem("c_st")
        scT_st = sem("scT_st")

        T_USES, C_USES, D_USES, Q_USES = 5, 5, 3, 18
        T_CHAIN, C_CHAIN, D_CHAIN = 13, 6, 8
        QK_SLOT = {0: 0, 2: 1, 4: 2, 6: 3}
        T_SLOT = {1: 0, 2: 1, 4: 2, 5: 3}
        QK_USE = [0, 4, 10, 14]
        QW_USE = [1, 5, 11, 15]
        V_USE = [6, 7]
        R_USE = [2, 3, 8, 9, 12, 13, 16, 17]

        def biases(s, bq, b):
            return {0: (b, 3), 2: (bq, 0), 4: (bq, 1), 6: (bq, 2)}.get(s, (None, 0))

        def wait(eng, s, value):
            if not isinstance(value, int) or value > 0:
                eng.wait_ge(s, value)

        def q_freed(eng, b, use):
            wait(eng, q_ev[use % 2], 2 * (Q_USES // 2 * b + use // 2))

        def q_count(b, use):
            return 2 * (Q_USES // 2 * b + use // 2 + 1)

        def q_evacuated(eng, b, use):
            wait(eng, q_ev[use % 2], q_count(b, use))

        def rounds(eng, body):
            last = n_batch - 1

            def at(i):
                return [(i - j) if 0 <= i - j <= last else None for j in range(5)]

            head = min(5, n_batch + 4)
            for i in range(head):
                body(*at(i))
            if n_batch > 5:
                with eng.Fori(5, n_batch) as i:
                    body(i, i - 1, i - 2, i - 3, i - 4)
            for i in range(max(head, n_batch), n_batch + 4):
                body(*at(i))

        def bank2(ps, n, rows):
            return ps[0:rows, 0:2 * n].rearrange("p (t n) -> p t n", t=2)

        block = ctx.enter_context(nc.Block())

        @block.sync
        def _(sp):
            loads = [
                (ident[:], w["ident"]), (dft[:], w["dft"]), (mel[0:BINS], w["melT"]),
                (mel[BINS:2 * BINS], w["melT"]), (dct[:], w["dctT"]),
                (wproj[0:MFCC], w["w_proj"]), (wproj[MFCC:MFCC + 1], w["b_proj"]),
                (wo[:], w["wo"].rearrange("(k p) n -> p k n", p=KD)),
                (w2[:], w["w2"].rearrange("(k p) n -> p k n", p=128)),
                (gate[:], w["gateT"].rearrange("(k p) n -> p k n", p=KD)),
                (n1w[:], w["n1w"]), (n2w[:], w["n2w"]), (b1[:], w["b1"]),
                (ucol[:], w["u"]), (vcol[:], w["v"]),
            ]
            for t in range(NT):
                loads += [(bb[:, t, 0:D], w["b2"].partition_broadcast(TP)),
                          (bb[:, t, D:2 * D], w["bo"].partition_broadcast(TP))]
            for i in range(2):
                for r in range(2):
                    loads += [(wpz[64 * i:64 * i + 64, :, r, i], w["w_pos"].rearrange("(p i d) n -> i d p n", i=2, d=DK)[i]),
                              (braw[64 * r + 32 * i:64 * r + 32 * i + 32, i, 0:ND], w["basis"])]
            for name, (first, end) in COLS.items():
                cols = slice(first, end)
                loads += [(wraw[:, 0, cols], w[name][0:128])]
                loads += [(wraw[64 * i:64 * i + 64, 1, cols], w[name][128:D]) for i in range(2)]
            sp.wait_ge(z_set, 3)
            for dst, src in loads:
                sp.dma_start(dst, src).then_inc(w_ld, 16)
            for h in range(HEADS):
                for t in range(NT):
                    sp.dma_start(bias_d[h, t * TP:(t + 1) * TP, :], zeros[:]).then_inc(zero_st, 16)

            def body(bt, bq, bb_, bc, bd):
                for s in range(SLOTS):
                    if bt is not None and s == 0:
                        wait(sp, t_mm, T_USES * bt - 4)
                        sp.dma_start(frames[:], w["frames"][:, bass.ds(bt * FRAMES, FRAMES)]).then_inc(fr_ld, 16)
                    if bb_ is not None and s + 2 < HEADS:
                        load_bias(bb_, s + 2)
                    br, pair = biases(s, bq, bb_)
                    if br is not None:
                        for h in (2 * pair, 2 * pair + 1):
                            q_evacuated(sp, br, R_USE[h])
                            wait(sp, bsk_ld[h % 4], 16 * (2 * (br - 1) + h // 4 + 1))
                            if isinstance(br, int) and br == 0 and h == 0:
                                sp.wait_ge(zero_st, 16 * HEADS * NT)
                            dst = bias_d[h, :, FRAMES - 1 - RANGE:FRAMES + RANGE].rearrange("(t p) n -> p t n", p=TP)
                            sp.dma_start(dst, rsb[:, h % 2]).then_inc(r_st[h % 2], 16)
                    if bd is not None and s == 4:
                        sl = bass.ds(bd * FRAMES, FRAMES)
                        apart(sp, READY, (d_ev, D_USES * bd + 2), (c_sg, 2 * bd + 2), (x_dup, bd + 1))
                        sp.dma_start(h1_d[sl, :].rearrange("(t p) n -> p t n", p=TP), h1[:]).then_inc(c_st, 16)
                        sp.dma_start(xnT_d[:, sl].rearrange("(k p) n -> p k n", p=KD), xnT[:]).then_inc(c_st, 16)
                        sp.dma_start(xs_d[sl, :].rearrange("(t p) n -> p t n", p=TP), xs[:]).then_inc(c_st, 16)
                    if bb_ is not None and s == 5:
                        apart(sp, READY, (hx_st, 16 * (bb_ + 1)), (c_xb, bb_))
                        sp.dma_start(hxl[:], hx_d[bass.ds(bb_ * FRAMES, FRAMES), :].rearrange("(t p) n -> p t n", p=TP)).then_inc(hxl_ld, 16)
                    if bq is not None and s >= 6:
                        load_bias(bq, s - 6)
                    if bt is not None and s == 7:
                        wait(sp, t_ch, T_CHAIN * bt + 11)
                        sp.dma_start(hx_d[bass.ds(bt * FRAMES, FRAMES), :].rearrange("(t p) n -> p t n", p=TP), hx[:]).then_inc(hx_st, 16)

            def load_bias(b, h):
                wait(sp, r_st[h % 2], 16 * (4 * b + h // 2 + 1))
                wait(sp, s_add, 2 * (HEADS * b + h - 4) + 2)
                base = bias_d[h, 0:1, FRAMES - 1:FRAMES]
                src = bass.AP(base.tensor, base.offset, [[PITCH - 1, TP], [(PITCH - 1) * TP, NT], [1, FRAMES]])
                sp.dma_start(bsk[:, h % 4], src).then_inc(bsk_ld[h % 4], 16)

            rounds(sp, body)
            sp.wait_ge(c_st, 48 * n_batch)
            sp.wait_ge(hx_st, 16 * n_batch)

        @block.gpsimd
        def _(pool):
            g = nc.gpsimd
            g.memset(zeros[:], 0.0).then_inc(z_set, 1)
            g.memset(wpz[:], 0.0).then_inc(z_set, 1)
            g.memset(braw[:], 0.0).then_inc(z_set, 1)
            g.memset(mfcc[:], 1.0).then_inc(z_set, 1)
            g.memset(kz[:], 0.0).then_inc(z_set, 1)
            g.memset(vz[:], 0.0).then_inc(z_set, 1)
            g.memset(tiny[:], 1e-6).then_inc(z_set, 1)
            g.memset(power[:], -0.5).then_inc(z_set, 1)
            pool.wait_ge(w_ld, W_LOADS)
            pool.wait_ge(z_set, 8)

            def vz_copy(b, i):
                base = vz[:, 0, i * 4, 0:DV]
                dst = bass.AP(base.tensor, base.offset, [base.ap[0], [HEADS * KD, NT], [KD + DV, 4], [1, DV]])
                apart(pool, READY, (q_ev[0], q_count(b, V_USE[0])), (q_ev[1], q_count(b, V_USE[1])),
                      (pv_mm, HEADS * (b - 1) + 4 * i + 4))
                g.tensor_copy(dst, vtmp[:, :, i * KD:(i + 1) * KD].rearrange("p t (h n) -> p t h n", h=4)).then_inc(vz_in, 1)

            def body(bt, bq, bb_, bc, bd):
                for s in range(SLOTS):
                    if bb_ is not None and s == 1:
                        vz_copy(bb_, 1)
                    if bc is not None and s == 1:
                        pool.wait_ge(hxl_ld, 16 * (bc + 1))
                        g.tensor_tensor(hxl[:], hxl[:], bb[:], ALU.add).then_inc(c_hb, 1)
                    if bc is not None and s == 3:
                        pool.wait_ge(c_ch, C_CHAIN * bc + 3)
                        g.tensor_tensor(c_y[:], c_v[:], power[:, 0:NT], ALU.pow).then_inc(c_ch, 1)
                        g.tensor_tensor(xb[:], x1[:], hxl[:, :, 0:D], ALU.add).then_inc(c_xb, 1)
                    if bc is not None and s == 7:
                        pool.wait_ge(d_ch, D_CHAIN * bc + 5)
                        g.tensor_tensor(d_y[:], d_v[:], power[:, 0:NT], ALU.pow).then_inc(d_ch, 1)
                        apart(pool, READY, (d_ch, D_CHAIN * bc + D_CHAIN))
                        g.tensor_copy(xs[:, :, D:256], xs[:, :, 128:D]).then_inc(x_dup, 1)
                    if bq is not None and s == 5:
                        vz_copy(bq, 0)
                    if bd is not None and s == 6:
                        pool.wait_ge(d_ev, D_USES * bd + 3)
                        g.dma_start(scT_d[:, bass.ds(bd * FRAMES, FRAMES)], scT[:]).then_inc(scT_st, 16)
                    if bt is not None and s == 5:
                        pool.wait_ge(t_ch, T_CHAIN * bt + 8)
                        g.tensor_tensor(t_y[:], t_v[:], power[:], ALU.pow).then_inc(t_ch, 1)

            rounds(pool, body)
            pool.wait_ge(scT_st, 16 * n_batch)

        @block.scalar
        def _(act):
            a = nc.scalar
            a.preload_act_table_set(EXP_SET)
            act.wait_ge(w_ld, W_LOADS)
            act.wait_ge(z_set, 8)

            for k in range(2):
                a.activation(wsp[:, 2 * k], wraw[:, k], ACT.Copy).then_inc(w_hi, 1)

            def body(bt, bq, bb_, bc, bd):
                for s in range(SLOTS):
                    if bq is not None and s - 1 in QK_SLOT:
                        p = QK_SLOT[s - 1]
                        act.wait_ge(q_mm, Q_USES * bq + QK_USE[p] + 1)
                        ps = bank2(qps[QK_USE[p] % 2], FRAMES, 128)
                        wait(act, s_mm, HEADS * (bq - 1) + 2 * p + 2)
                        a.activation(qu[:, p], ps[:, 0], ACT.Identity, bias=ucol[:, p:p + 1]).then_inc(q_ev[QK_USE[p] % 2], 1)
                        a.activation(kz[0:64, 2 * p], ps[0:64, 1], ACT.Copy)
                        a.activation(kz[64:128, 2 * p + 1], ps[64:128, 1], ACT.Copy).then_inc(q_ev[QK_USE[p] % 2], 1)
                    br, pair = biases(s, bq, bb_)
                    if br is not None:
                        for h in (2 * pair, 2 * pair + 1):
                            act.wait_ge(q_mm, Q_USES * br + R_USE[h] + 1)
                            wait(act, r_st[h % 2], 16 * (4 * br + h // 2))
                            a.activation(rsb[:, h % 2], bank2(qps[R_USE[h] % 2], NDE, TP)[:, :, 0:ND], ACT.Copy).then_inc(q_ev[R_USE[h] % 2], 2)
                    if bb_ is not None and s < HEADS:
                        n = HEADS * bb_ + s
                        for t in range(NT):
                            act.wait_ge(s_add, 2 * n + t + 1)
                            if t == 0:
                                wait(act, pt_mm, n - 1)
                            a.activation(prob[:, s % 2, t], ssb[:, s % 2, t], ACT.Exp, bias=mx[:, s % 2, t:t + 1],
                                         scale=-1.0, accum_out=rs[:, s % 2, t:t + 1]).then_inc(p_exp, 1)
                    if bt is not None and s == 3:
                        act.wait_ge(t_mm, T_USES * bt + 2)
                        a.activation(logmel[:], tps[0:MELS, 0:FRAMES], ACT.Ln, bias=tiny[:, 0:1]).then_inc(t_ev, 1)
                        a.preload_act_table_set(EXP_SET)
                    if bc is not None and s == 2:
                        b0 = C_CHAIN * bc
                        act.wait_ge(c_ev, C_USES * bc + 1)
                        a.activation(junk[:], x1[:, 0], ACT.Square, accum_out=ss[:, 0:1]).then_inc(c_ch, 1)
                        act.wait_ge(c_ch, b0 + 1)
                        a.activation(junk[:], x1[:, 1], ACT.Square, accum_out=ss[:, 1:2]).then_inc(c_ch, 1)
                    if bd is not None and s == 1:
                        act.wait_ge(d_mm, D_USES * bd + 2)
                        a.activation(sige[:], cps[0:TP, 0:NT * EXPERTS].rearrange("p (t n) -> p t n", t=NT), ACT.Exp, scale=-1.0).then_inc(d_ev, 1)
                    if bc is not None and s == 4:
                        act.wait_ge(c_mm, C_USES * bc + 2)
                        ps = bank2(cps, FRAMES, 128)
                        for k in range(2):
                            a.activation(h2sp[:, 0, k], ps[:, k], ACT.Copy, scale=n2w[:, k:k + 1]).then_inc(c_hi, 1)
                    if bc is not None and s == 5:
                        act.wait_ge(c_mm, C_USES * bc + 3)
                        ps = bank2(cps, FRAMES, 128)
                        a.activation(gT[:, 0], ps[:, 0], ACT.Gelu, bias=b1[:, 0:1])
                        a.activation(gT[:, 1], ps[:, 1], ACT.Gelu, bias=b1[:, 1:2]).then_inc(c_ev, 1)
                    if bt is not None and s == 1:
                        act.wait_ge(t_mm, T_USES * bt + 1)
                        a.activation(sq[:], tps[0:2 * BINS, 0:FRAMES], ACT.Square).then_inc(t_ev, 1)
                    if bt is not None and s == 4:
                        act.wait_ge(t_mm, T_USES * bt + 3)
                        a.activation(mfcc[0:MFCC], tps[0:MFCC, 0:FRAMES], ACT.Copy).then_inc(t_ev, 1)
                    if bt is not None and s == 5:
                        act.wait_ge(t_mm, T_USES * bt + 4)
                        wait(act, hx_st, 16 * bt)
                        a.activation(hx[:, :, 0:D], bank2(tps, D, TP), ACT.Copy).then_inc(t_ev, 1)
                    if bc is not None and s == 5:
                        act.wait_ge(c_mm, C_USES * bc + 4)
                        a.activation(gT[:, 2], bank2(cps, FRAMES, 128)[:, 0], ACT.Gelu, bias=b1[:, 2:3]).then_inc(c_ev, 1)
                        a.preload_act_table_set(EXP_SET)
                    if bq is not None and s == 3:
                        for t in range(NT):
                            act.wait_ge(q_mm, Q_USES * bq + V_USE[t] + 1)
                            if t == 0:
                                wait(act, vz_in, 2 * bq)
                            a.activation(vtmp[:, t], qps[V_USE[t] % 2][0:TP, 0:D], ACT.Copy).then_inc(q_ev[V_USE[t] % 2], 2)
                    if bt is not None and s == 7:
                        act.wait_ge(t_mm, T_USES * bt + 5)
                        if bq is not None:
                            act.wait_ge(q_mm, Q_USES * bq + QK_USE[-1] + 1)
                        ps = bank2(tps, FRAMES, 128)
                        for k in range(2):
                            a.activation(hsp[:, 0, k], ps[:, k], ACT.Copy, scale=n1w[:, k:k + 1]).then_inc(t_hi, 1)

            rounds(act, body)

        @block.vector
        def _(dve):
            v = nc.vector
            dve.wait_ge(w_ld, W_LOADS)
            dve.wait_ge(z_set, 8)
            v.tensor_tensor(vmu[:], vcol[:], ucol[:], ALU.subtract).then_inc(ini, 1)
            v.tensor_copy(bz[:], braw[:]).then_inc(ini, 1)
            for k, half in ((0, slice(0, 128)), (1, slice(64, 128))):
                dve.wait_ge(w_hi, k + 1)
                v.tensor_tensor(wsp[half, 1 + k], wraw[half, k], wsp[half, 2 * k].bitcast(F32), ALU.subtract).then_inc(ini, 1)
            dve.wait_ge(cq_mm, 1)
            v.tensor_copy(cq[:], tps[:, 0:PAIRS]).then_inc(ini, 1)

            def pt_copy(b, h):
                if b is not None:
                    n = HEADS * b + h
                    dve.wait_ge(pt_mm, n + 1)
                    wait(dve, pv_mm, n - 1)
                    v.tensor_copy(ptsb[:, h % 2], ptps[:]).then_inc(pt_ev, 1)

            def body(bt, bq, bb_, bc, bd):
                for s in range(SLOTS):
                    if bb_ is not None and s < HEADS:
                        n = HEADS * bb_ + s
                        apart(dve, READY, (s_mm, n + 1), (bsk_ld[s % 4], 16 * (2 * bb_ + s // 4 + 1)),
                              (p_exp, 2 * (n - 1)))
                        for t in range(NT):
                            v.tensor_tensor_reduce(out=ssb[:, s % 2, t], in0=sps[s % 2][:, t], in1=bsk[:, s % 4, t],
                                                   scale=-SCALE, scalar=3.0e38, op0=ALU.add, op1=ALU.min,
                                                   accum_out=mx[:, s % 2, t:t + 1]).then_inc(s_add, 1)
                    if s == 0:
                        pt_copy(bc, HEADS - 1)
                    if s > 0:
                        pt_copy(bb_, s - 1)
                    if bc is not None and s == 1:
                        dve.wait_ge(pv_mm, HEADS * (bc + 1))
                        wait(dve, c_mm, C_USES * (bc - 1) + 1)
                        v.tensor_copy(otsb[:], otps[:]).then_inc(ot_ev, 1)
                    if bb_ is not None and s < HEADS:
                        n = HEADS * bb_ + s
                        dve.wait_ge(p_exp, 2 * n + 2)
                        v.reciprocal(rinv[:, s % 2], rs[:, s % 2]).then_inc(r_inv, 1)
                        dve.wait_ge(r_inv, n + 1)
                        for t in range(NT):
                            v.tensor_scalar(prob[:, s % 2, t], prob[:, s % 2, t], rinv[:, s % 2, t:t + 1], None, ALU.mult).then_inc(p_nrm, 1)
                    if bq is not None and s - 1 in QK_SLOT:
                        p = QK_SLOT[s - 1]
                        use = QW_USE[p]
                        dve.wait_ge(q_mm, Q_USES * bq + use + 1)
                        v.tensor_scalar(qw[:], qps[use % 2][:, 0:FRAMES], cq[:, p:p + 1], None, ALU.add).then_inc(q_ev[use % 2], 1)
                        dve.wait_ge(q_ev[use % 2], q_count(bq, use) - 1)
                        v.scalar_tensor_tensor(out=qw[64:128], in0=qps[use % 2][64:128, 0:FRAMES], scalar=cq[64:128, p:p + 1],
                                               in1=qw[64:128].bitcast(F32), op0=ALU.add, op1=ALU.subtract).then_inc(q_ev[use % 2], 1)
                    if bc is not None and s == 2:
                        dve.wait_ge(c_mm, C_USES * bc + 1)
                        dve.wait_ge(c_hb, bc + 1)
                        v.tensor_tensor(x1[:], bank2(cps, D, TP), hxl[:, :, D:2 * D], ALU.add).then_inc(c_ev, 1)
                    if bc is not None and s == 4:
                        ps = bank2(cps, FRAMES, 128)
                        dve.wait_ge(c_hi, 2 * (bc + 1))
                        for k in range(2):
                            ins = v.scalar_tensor_tensor(out=h2sp[:, 1, k], in0=ps[:, k], scalar=n2w[:, k:k + 1], in1=h2sp[:, 0, k].bitcast(F32),
                                                         op0=ALU.mult, op1=ALU.subtract)
                        ins.then_inc(c_ev, 1)
                    if bd is not None and s == 0:
                        dve.wait_ge(d_mm, D_USES * bd + 1)
                        wait(dve, c_st, 48 * bd)
                        v.tensor_copy(xnT[:], bank2(cps, FRAMES, KD)).then_inc(d_ev, 1)
                    if bc is not None and s == 3:
                        dve.wait_ge(c_ch, C_CHAIN * bc + 2)
                        v.tensor_scalar(c_v[:], ss[:], 1.0 / D, EPS, ALU.mult, ALU.add).then_inc(c_ch, 1)
                        dve.wait_ge(c_ch, C_CHAIN * bc + 4)
                        for t in range(NT):
                            v.tensor_scalar(h2n[:, t, 0:D], x1[:, t], c_y[:, t:t + 1], None, ALU.mult)
                            v.tensor_scalar(h2n[:, t, D:256], x1[:, t, 128:D], c_y[:, t:t + 1], None, ALU.mult).then_inc(c_ch, 1)
                    if bd is not None and s == 1:
                        dve.wait_ge(d_ev, D_USES * bd + 2)
                        v.tensor_scalar(sige[:], sige[:], 1.0, None, ALU.add).then_inc(c_sg, 1)
                        dve.wait_ge(c_sg, 2 * bd + 1)
                        v.reciprocal(xs[:, :, 256:SROW], sige[:]).then_inc(c_sg, 1)
                    if bd is not None and s == 6:
                        dve.wait_ge(d_mm, D_USES * bd + 3)
                        wait(dve, scT_st, 16 * bd)
                        v.tensor_copy(scT[:], tps[0:EXPERTS, 0:FRAMES]).then_inc(d_ev, 1)
                    if bc is not None and s == 7:
                        b0 = D_CHAIN * bc
                        wait(dve, c_st, 48 * bc)
                        dve.wait_ge(d_ch, b0 + 6)
                        for t in range(NT):
                            v.tensor_scalar(xs[:, t, 0:D], h1[:, t], c_mv[:, t, 0:1], d_y[:, t:t + 1], ALU.subtract, ALU.mult).then_inc(d_ch, 1)
                    if bt is not None and s == 5:
                        b0 = T_CHAIN * bt
                        dve.wait_ge(t_ev, T_USES * bt + 4)
                        for t in range(NT):
                            v.bn_stats(t_stats[:, t], hx[:, t, 0:D]).then_inc(t_ch, 1)
                        apart(dve, READY, (t_ch, b0 + 2))
                        for t in range(NT):
                            v.bn_aggr(t_mv[:, t], t_stats[:, t]).then_inc(t_ch, 1)
                        dve.wait_ge(t_ch, b0 + 4)
                        v.tensor_scalar(t_v[:, 0:NT], t_mv[:, :, 1], EPS, None, ALU.add).then_inc(t_ch, 1)
                        dve.wait_ge(t_ch, b0 + 5)
                        v.reciprocal(t_inv[:], t_v[:, 0:NT]).then_inc(t_ch, 1)
                        dve.wait_ge(t_ch, b0 + 6)
                        v.tensor_tensor(t_inv[:], t_inv[:], t_mv[:, :, 1], ALU.mult).then_inc(t_ch, 1)
                        dve.wait_ge(t_ch, b0 + 7)
                        v.tensor_scalar(t_v[:, NT:2 * NT], t_inv[:], EPS, None, ALU.add).then_inc(t_ch, 1)
                    if bt is not None and s == 6:
                        b0 = T_CHAIN * bt
                        wait(dve, hx_st, 16 * bt)
                        dve.wait_ge(t_ch, b0 + 9)
                        for t in range(NT):
                            v.tensor_scalar(hx[:, t, D:2 * D], hx[:, t, 0:D], t_mv[:, t, 0:1], t_y[:, t:t + 1], ALU.subtract, ALU.mult).then_inc(t_ch, 1)
                        for t in range(NT):
                            dve.wait_ge(t_ch, b0 + 10 + t)
                            v.tensor_scalar(h1n[:, t, 0:D], hx[:, t, D:2 * D], t_y[:, NT + t:NT + t + 1], None, ALU.mult)
                            v.tensor_scalar(h1n[:, t, D:256], hx[:, t, D + 128:2 * D], t_y[:, NT + t:NT + t + 1], None, ALU.mult).then_inc(t_ch, 1)
                    if bc is not None and s == 6:
                        b0 = D_CHAIN * bc
                        dve.wait_ge(c_mm, C_USES * bc + 5)
                        dve.wait_ge(c_xb, bc + 1)
                        wait(dve, c_st, 48 * bc)
                        v.tensor_tensor(h1[:], bank2(cps, D, TP), xb[:], ALU.add).then_inc(c_ev, 1)
                        dve.wait_ge(c_ev, C_USES * bc + 5)
                        for t in range(NT):
                            v.bn_stats(c_stats[:, t], h1[:, t]).then_inc(d_ch, 1)
                        apart(dve, READY, (d_ch, b0 + 2))
                        for t in range(NT):
                            v.bn_aggr(c_mv[:, t], c_stats[:, t]).then_inc(d_ch, 1)
                        dve.wait_ge(d_ch, b0 + 4)
                        v.tensor_scalar(d_v[:], c_mv[:, :, 1], EPS, None, ALU.add).then_inc(d_ch, 1)
                    if bt is not None and s == 7:
                        ps = bank2(tps, FRAMES, 128)
                        dve.wait_ge(t_hi, 2 * (bt + 1))
                        for k in range(2):
                            ins = v.scalar_tensor_tensor(out=hsp[:, 1, k], in0=ps[:, k], scalar=n1w[:, k:k + 1], in1=hsp[:, 0, k].bitcast(F32),
                                                         op0=ALU.mult, op1=ALU.subtract)
                        ins.then_inc(t_ev, 1)

            rounds(dve, body)

        @block.tensor
        def _(pe):
            m = nc.tensor.matmul
            pe.wait_ge(w_ld, W_LOADS)
            pe.wait_ge(ini, 1)
            for p in range(PAIRS):
                ins = m(tps[:, p:p + 1], wpz[:, p].rearrange("d r i n -> d (r i n)"), vmu[:, p:p + 1], start=True, stop=True)
            ins.then_inc(cq_mm, 1)
            pe.wait_ge(ini, 5)
            pe.wait_ge(z_set, 8)

            def transposes(ps, src, s):
                rows = ps.shape[0]
                for k in range(NK):
                    for t in range(NT):
                        ins = nc.tensor.transpose(ps[:, k, t * TP:(t + 1) * TP], src[:, t, k * rows:(k + 1) * rows], ident[0:TP, 0:TP])
                ins.then_inc(s, 1)

            def natural(ps, lhsT, rhs, s):
                nk = rhs.shape[1]
                for t in range(NT):
                    for k in range(nk):
                        ins = m(ps[:, t], lhsT[:, k, t * TP:(t + 1) * TP], rhs[:, k], start=k == 0, stop=k == nk - 1)
                ins.then_inc(s, 1)

            def probs_T(b, h):
                if b is not None:
                    n = HEADS * b + h
                    pe.wait_ge(p_nrm, 2 * n + 2)
                    wait(pe, pt_ev, n)
                    for j in range(NT):
                        for t in range(NT):
                            ins = nc.tensor.transpose(ptps[:, j, t * TP:(t + 1) * TP], prob[:, h % 2, t, j * TP:(j + 1) * TP], ident[0:TP, 0:TP])
                    ins.then_inc(pt_mm, 1)

            def values(b, h):
                if b is not None:
                    n = HEADS * b + h
                    if h % 4 == 0:
                        pe.wait_ge(vz_in, 2 * b + 1 + h // 4)
                    if h == 0:
                        wait(pe, ot_ev, b)
                    pe.wait_ge(pt_ev, n + 1)
                    for j in range(NT):
                        ins = m(otps[:, h // 4], vz[:, j, h], ptsb[:, h % 2, j], start=h % 4 == 0 and j == 0, stop=h % 4 == 3 and j == NT - 1)
                    ins.then_inc(pv_mm, 1)

            def body(bt, bq, bb_, bc, bd):
                for s in range(SLOTS):
                    if bb_ is not None and s < HEADS:
                        n = HEADS * bb_ + s
                        if s % 2 == 0:
                            q_evacuated(pe, bb_, QK_USE[s // 2])
                        wait(pe, s_add, 2 * (n - 1))
                        for t in range(NT):
                            ins = m(sps[s % 2][:, t], qu[:, s // 2, t * TP:(t + 1) * TP], kz[:, s], start=True, stop=True)
                        ins.then_inc(s_mm, 1)
                    br, pair = biases(s, bq, bb_)
                    if br is not None:
                        for h in (2 * pair, 2 * pair + 1):
                            q_freed(pe, br, R_USE[h])
                            if h % 2 == 0:
                                q_evacuated(pe, br, QW_USE[pair])
                            ps = bank2(qps[R_USE[h] % 2], NDE, TP)
                            for t in range(NT):
                                ins = m(ps[:, t], qw[:, t * TP:(t + 1) * TP], bz[:, h % 2], start=True, stop=True)
                            ins.then_inc(q_mm, 1)
                    if s == 0:
                        probs_T(bc, HEADS - 1)
                    if s > 0:
                        probs_T(bb_, s - 1)
                    if bd is not None and s == 0:
                        pe.wait_ge(d_ch, D_CHAIN * bd + D_CHAIN)
                        pe.wait_ge(c_ev, C_USES * bd + 5)
                        transposes(bank2(cps, FRAMES, KD), xs[:, :, 0:D], d_mm)
                    if bd is not None and s == 1:
                        pe.wait_ge(d_ev, D_USES * bd + 1)
                        natural(cps[0:TP, 0:NT * EXPERTS].rearrange("p (t n) -> p t n", t=NT), xnT, gate, d_mm)
                    if bc is not None and s == 2:
                        if bd is not None:
                            pe.wait_ge(d_ev, D_USES * bd + 2)
                        pe.wait_ge(ot_ev, bc + 1)
                        natural(bank2(cps, D, TP), otsb, wo, c_mm)
                    if bc is not None and s == 4:
                        pe.wait_ge(c_ch, C_CHAIN * bc + C_CHAIN)
                        pe.wait_ge(c_ev, C_USES * bc + 1)
                        transposes(bank2(cps, FRAMES, 128), h2n, c_mm)
                    if bd is not None and s == 6:
                        pe.wait_ge(c_sg, 2 * bd + 2)
                        if bt is not None:
                            pe.wait_ge(t_ev, T_USES * bt + 4)
                        for t in range(NT):
                            ins = nc.tensor.transpose(tps[0:EXPERTS, t * TP:(t + 1) * TP], xs[:, t, 256:SROW], ident[0:TP, 0:TP])
                        ins.then_inc(d_mm, 1)
                    if bc is not None and s == 5:
                        pe.wait_ge(c_ev, C_USES * bc + 2)
                        ps = bank2(cps, FRAMES, 128)
                        for j in range(2):
                            col = COLS["w1"][0] + j * 128
                            for k, (wk, xp, xk) in enumerate(PARTS):
                                ins = m(ps[:, j], wsp[:, wk, col:col + 128], h2sp[:, xp, xk], start=k == 0, stop=k == len(PARTS) - 1)
                        ins.then_inc(c_mm, 1)
                    if bc is not None and s == 6:
                        pe.wait_ge(c_ev, C_USES * bc + 4)
                        natural(bank2(cps, D, TP), gT, w2, c_mm)
                    if bt is not None and s in T_SLOT:
                        apart(pe, READY, (t_ev, T_USES * bt + T_SLOT[s]))
                        if T_SLOT[s] == 0:
                            pe.wait_ge(fr_ld, 16 * (bt + 1))
                            m(tps[0:2 * BINS, 0:FRAMES], dft[:], frames[:], start=True, stop=True).then_inc(t_mm, 1)
                        if T_SLOT[s] == 1:
                            m(tps[0:MELS, 0:FRAMES], mel[:], sq[:], start=True, stop=True).then_inc(t_mm, 1)
                        if T_SLOT[s] == 2:
                            m(tps[0:MFCC, 0:FRAMES], dct[:], logmel[:], start=True, stop=True).then_inc(t_mm, 1)
                        if T_SLOT[s] == 3:
                            ps = bank2(tps, D, TP)
                            for t in range(NT):
                                ins = m(ps[:, t], mfcc[:, t * TP:(t + 1) * TP], wproj[:], start=True, stop=True)
                            ins.then_inc(t_mm, 1)
                    if bq is not None and s - 1 in QK_SLOT:
                        p = QK_SLOT[s - 1]
                        use = QW_USE[p]
                        q_freed(pe, bq, use)
                        wait(pe, q_ev[QK_USE[p] % 2], q_count(bq, QK_USE[p]) - 1)
                        m(qps[use % 2][:, 0:FRAMES], wpz[:, p].rearrange("d r i n -> d (r i n)"), qu[:, p], start=True, stop=True).then_inc(q_mm, 1)
                    if bt is not None and s == 7:
                        pe.wait_ge(t_ch, T_CHAIN * bt + T_CHAIN)
                        if bd is not None:
                            pe.wait_ge(d_ev, D_USES * bd + 3)
                        pe.wait_ge(t_ev, T_USES * bt + 4)
                        transposes(bank2(tps, FRAMES, 128), h1n, t_mm)
                    if bq is not None and s in QK_SLOT:
                        p = QK_SLOT[s]
                        q_freed(pe, bq, QK_USE[p])
                        if p == 0:
                            pe.wait_ge(t_ev, T_USES * (bq + 1))
                        ps = bank2(qps[QK_USE[p] % 2], FRAMES, 128)
                        for i in range(2):
                            col = i * HEADS * DK + p * 128
                            for k, (wk, xp, xk) in enumerate(PARTS):
                                ins = m(ps[:, i], wsp[:, wk, col:col + 128], hsp[:, xp, xk], start=k == 0, stop=k == len(PARTS) - 1)
                        ins.then_inc(q_mm, 1)
                    if s == 0:
                        values(bc, HEADS - 1)
                    if s > 0:
                        values(bb_, s - 1)
                    if bc is not None and s == 5:
                        pe.wait_ge(c_ev, C_USES * bc + 3)
                        ps = bank2(cps, FRAMES, 128)
                        col = COLS["w1"][0] + 2 * 128
                        for k, (wk, xp, xk) in enumerate(PARTS):
                            ins = m(ps[:, 0], wsp[:, wk, col:col + 128], h2sp[:, xp, xk], start=k == 0, stop=k == len(PARTS) - 1)
                        ins.then_inc(c_mm, 1)
                    if bq is not None and s == 3:
                        for t in range(NT):
                            q_freed(pe, bq, V_USE[t])
                            for k, (wk, xp, xk) in enumerate(PARTS):
                                ins = m(qps[V_USE[t] % 2][0:TP, 0:D], hsp[:, xp, xk, t * TP:(t + 1) * TP], wsp[:, wk, slice(*COLS["wv"])], start=k == 0, stop=k == len(PARTS) - 1)
                            ins.then_inc(q_mm, 1)

            rounds(pe, body)


W_LOADS = 16 * (15 + 8 + 12 + 2 * NT)

BF16 = mybir.dt.bfloat16
I32 = mybir.dt.int32
U32 = mybir.dt.uint32

CHUNK = 500
CHUNKS = TOKENS // CHUNK
CT = CHUNK // TP
MS = F_SH // 128
SPLIT = 128 // EXPERTS
SPAN = TOKENS // SPLIT
BLOCKS = SPAN // TP
SCORE_BITS = 30
LO = 32


def expert_blocks():
    p = np.arange(128)
    return (p[:, None] // SPLIT == p[None, :] // SPLIT).astype(np.float32)


def expert_before():
    p = np.arange(128)
    return expert_blocks() * (p[:, None] < p[None, :]).astype(np.float32)


def shared_and_route(nc, w, h1_d, xnT_d, scT_d, out_d, hi_all, lo_all, sem):
    ctx = ExitStack()

    def sb(name, shape, dt=F32):
        return ctx.enter_context(nc.sbuf_tensor("sh_" + name, shape, dt))

    def pb(name, shape):
        return ctx.enter_context(nc.psum_tensor("shp_" + name, shape, F32))

    with ctx:
        ident = sb("ident", [128, 128])
        wraw = sb("wraw", [128, 2, 2, F_SH])
        wsp = sb("wsp", [128, 2, 3, F_SH], F32R)
        wd = sb("wd", [128, MS, D])
        blocks = sb("blocks", [128, 128])
        before = sb("before", [128, 128])
        xraw = sb("xraw", [128, 2, 2, CHUNK])
        xsp = sb("xsp", [128, 2, 2, 2, CHUNK], F32R)
        res = sb("res", [TP, 2, CT, D])
        sg = sb("sg", [128, 2, CHUNK])
        hT = sb("hT", [128, MS, CHUNK])
        y = sb("y", [TP, 2, CT, D])
        sc = sb("sc", [128, SPAN])
        hit = sb("hit", [128, SPAN])
        eq = sb("eq", [128, SPAN])
        run = sb("run", [128, SPAN])
        zero = sb("zero", [128, SPAN])
        thr = sb("thr", [128, 1], I32)
        bit = sb("bit", [128, 1], I32)
        cand = sb("cand", [128, 1], I32)
        take = sb("take", [128, 1], I32)
        cnt = sb("cnt", [128, 1])
        need = sb("need", [128, 1])
        off = sb("off", [128, 1])
        posi = sb("posi", [TP, BLOCKS, 128], I32)
        gps = [pb(f"g{i}", [128, CHUNK]) for i in range(2)]
        ups = [pb(f"u{i}", [128, CHUNK]) for i in range(2)]
        dps = [pb(f"d{i}", [TP, 2, D]) for i in range(2)]
        kps = pb("k", [128, 1])
        pps = pb("p", [TP, BLOCKS // 2, 128])

        w_ld = sem("sh_w_ld")
        sc_ld = sem("sh_sc_ld")
        ini = sem("sh_ini")
        x_ld = [sem(f"sh_x_ld{i}") for i in range(2)]
        r_ld = [sem(f"sh_r_ld{i}") for i in range(2)]
        w_hi = sem("sh_w_hi")
        w_lo = sem("sh_w_lo")
        x_hi = sem("sh_x_hi")
        x_lo = sem("sh_x_lo")
        gu_mm = sem("sh_gu_mm")
        g_ev = sem("sh_g_ev")
        h_ev = sem("sh_h_ev")
        d_mm = sem("sh_d_mm")
        y_ev = sem("sh_y_ev")
        y_st = [sem(f"sh_y_st{i}") for i in range(2)]
        k_cnt = sem("sh_k_cnt")
        k_mm = sem("sh_k_mm")
        k_ch = sem("sh_k_ch")
        r_ch = sem("sh_r_ch")
        r_mm = sem("sh_r_mm")
        K_CHAIN = 3

        def wait(eng, s, value):
            if not isinstance(value, int) or value > 0:
                eng.wait_ge(s, value)

        def chunks(eng, body):
            for i in range(2):
                body(i, i, True)
            with eng.Fori(1, CHUNKS // 2 - 1) as j:
                for i in range(2):
                    body(2 * j + i, i, True)
            for i in range(2):
                body(CHUNKS - 2 + i, i, i == 0)

        block = ctx.enter_context(nc.Block())

        @block.sync
        def _(sp):
            sp.dma_start(sc[:], scT_d.rearrange("e (c n) -> (e c) n", n=SPAN)).then_inc(sc_ld, 16)
            for i, src in enumerate((w["WsgT"], w["WsuT"])):
                sp.dma_start(wraw[:, i, 0], src[0:128]).then_inc(w_ld, 16)
                for half in range(2):
                    sp.dma_start(wraw[half * 64:half * 64 + 64, i, 1], src[128:D]).then_inc(w_ld, 16)
            for dst, src in ((wd[:], w["WsdT"].rearrange("(k p) n -> p k n", p=128)),
                             (ident[:], w["ident"]), (blocks[:], w["blocks"]), (before[:], w["before"])):
                sp.dma_start(dst, src).then_inc(w_ld, 16)

            def body(c, par, more):
                own = bass.ds(c * CHUNK, CHUNK)
                wait(sp, x_lo, 2 * (c - 1))
                sp.dma_start(xraw[:, par, 0], xnT_d[0:128, own]).then_inc(x_ld[par], 16)
                for half in range(2):
                    sp.dma_start(xraw[half * 64:half * 64 + 64, par, 1], xnT_d[128:D, own]).then_inc(x_ld[par], 16)
                wait(sp, y_ev, 2 * (c - 1))
                sp.dma_start(res[:, par], h1_d[own, :].rearrange("(t p) n -> p t n", p=TP)).then_inc(r_ld[par], 16)

            chunks(sp, body)

        @block.scalar
        def _(act):
            a = nc.scalar

            def high(c, par):
                act.wait_ge(x_ld[par], 24 * (c - par) + 48)
                wait(act, h_ev, MS * (c - 1))
                for k in range(2):
                    a.activation(xsp[:, par, 0, k], xraw[:, par, k], ACT.Copy).then_inc(x_hi, 1)

            act.wait_ge(w_ld, 16 * 10)
            for i in range(2):
                a.activation(wsp[:, i, 0], wraw[:, i, 0], ACT.Copy).then_inc(w_hi, 1)
                a.activation(wsp[:, i, 2], wraw[:, i, 1], ACT.Copy).then_inc(w_hi, 1)
            high(0, 0)

            def body(c, par, more):
                for m in range(MS):
                    n = MS * c + m
                    act.wait_ge(gu_mm, 2 * n + 1)
                    wait(act, h_ev, n - 1)
                    a.activation(sg[:, (MS * par + m) % 2], gps[(MS * par + m) % 2][:], ACT.Silu).then_inc(g_ev, 1)
                if more:
                    high(c + 1, 1 - par)
                act.wait_ge(y_ev, 2 * c + 2)
                act.dma_start(out_d[bass.ds(c * CHUNK, CHUNK), :].rearrange("(t p) n -> p t n", p=TP), y[:, par]).then_inc(y_st[par], 16)

            chunks(act, body)
            for i in range(2):
                act.wait_ge(y_st[i], 16 * (CHUNKS // 2))

        @block.vector
        def _(dve):
            v = nc.vector
            v.memset(thr[:], 0).then_inc(ini, 1)
            v.memset(bit[:], 1 << (SCORE_BITS - 1)).then_inc(ini, 1)
            v.memset(zero[:], 0.0).then_inc(ini, 1)
            dve.wait_ge(ini, 3)
            dve.wait_ge(sc_ld, 16)

            def count(k):
                wait(dve, k_ch, K_CHAIN * k)
                v.tensor_tensor(cand[:], thr[:], bit[:], ALU.bitwise_or).then_inc(k_ch, 1)
                dve.wait_ge(k_ch, K_CHAIN * k + 1)
                v.tensor_scalar(hit[:], sc[:], cand[:].bitcast(F32), 0.0, ALU.is_ge, ALU.add, accum_out=cnt[:]).then_inc(k_cnt, 1)

            def update(k):
                dve.wait_ge(k_mm, k + 1)
                v.tensor_scalar(take[:], kps[:], float(CAPACITY), None, ALU.is_ge).then_inc(k_ch, 1)
                dve.wait_ge(k_ch, K_CHAIN * k + 2)
                v.tensor_single_scalar(bit[:], bit[:], 1, ALU.logical_shift_right)
                v.copy_predicated(thr[:], take[:], cand[:]).then_inc(k_ch, 1)

            def gated(c, par, m):
                n = MS * c + m
                dve.wait_ge(gu_mm, 2 * n + 2)
                dve.wait_ge(g_ev, n + 1)
                wait(dve, d_mm, 2 * c)
                v.tensor_tensor(hT[:, m], sg[:, (MS * par + m) % 2], ups[(MS * par + m) % 2][:], ALU.mult).then_inc(h_ev, 1)

            def low(c, par):
                for k in range(2):
                    dve.wait_ge(x_hi, 2 * c + k + 1)
                    v.tensor_tensor(xsp[:, par, 1, k], xraw[:, par, k], xsp[:, par, 0, k].bitcast(F32), ALU.subtract).then_inc(x_lo, 1)

            for i in range(2):
                for k, half in ((0, slice(0, 128)), (1, slice(64, 128))):
                    dve.wait_ge(w_hi, 2 * i + k + 1)
                    v.tensor_tensor(wsp[half, i, 1 + k], wraw[half, i, k], wsp[half, i, 2 * k].bitcast(F32), ALU.subtract).then_inc(w_lo, 1)
            low(0, 0)

            def body(c, par, more):
                count(2 * c)
                gated(c, par, 0)
                update(2 * c)
                count(2 * c + 1)
                gated(c, par, 1)
                gated(c, par, 2)
                update(2 * c + 1)
                if more:
                    low(c + 1, 1 - par)
                dve.wait_ge(r_ld[par], 8 * (c - par) + 16)
                wait(dve, y_st[par], 16 * (c // 2) if isinstance(c, int) else 8 * (c - par))
                for i in range(2):
                    dve.wait_ge(d_mm, 2 * c + i + 1)
                    v.tensor_tensor(y[:, par, 2 * i:2 * i + 2], dps[i][:], res[:, par, 2 * i:2 * i + 2], ALU.add).then_inc(y_ev, 1)

            assert 2 * CHUNKS >= SCORE_BITS
            chunks(dve, body)

            step = [0]

            def then(ins):
                step[0] += 1
                ins.then_inc(r_ch, 1)
                dve.wait_ge(r_ch, step[0])

            dve.wait_ge(k_ch, K_CHAIN * 2 * CHUNKS)
            t = thr[:].bitcast(F32)
            then(v.tensor_scalar(hit[:], sc[:], t, 0.0, ALU.is_gt, ALU.add, accum_out=cnt[:]))
            then(v.tensor_scalar(eq[:], sc[:], t, None, ALU.is_equal))
            then(v.tensor_tensor_scan(run[:], eq[:], zero[:], 0.0, ALU.add, ALU.add))
            dve.wait_ge(r_mm, 1)
            then(v.tensor_scalar(need[:], kps[:], -1.0, float(CAPACITY), ALU.mult, ALU.add))
            dve.wait_ge(r_mm, 2)
            then(v.tensor_tensor(need[:], need[:], kps[:], ALU.subtract))
            then(v.scalar_tensor_tensor(out=eq[:], in0=run[:], scalar=need[:], in1=eq[:], op0=ALU.is_le, op1=ALU.mult))
            then(v.tensor_tensor(hit[:], hit[:], eq[:], ALU.add))
            then(v.tensor_tensor_scan(run[:], hit[:], zero[:], 0.0, ALU.add, ALU.add))
            dve.wait_ge(r_mm, 3)
            then(v.tensor_copy(off[:], kps[:]))
            then(v.scalar_tensor_tensor(out=run[:], in0=run[:], scalar=off[:], in1=hit[:], op0=ALU.add, op1=ALU.mult))
            then(v.tensor_scalar(run[:], run[:], -1.0, None, ALU.add))
            half = BLOCKS // 2
            for i in range(2):
                dve.wait_ge(r_mm, 4 + i)
                then(v.tensor_copy(posi[:, i * half:(i + 1) * half], pps[:]))
            then(v.tensor_single_scalar(hi_all[:], posi[:], 5, ALU.arith_shift_right))
            then(v.tensor_single_scalar(lo_all[:], posi[:], LO - 1, ALU.bitwise_and))

        @block.tensor
        def _(pe):
            m_ = nc.tensor.matmul
            pe.wait_ge(w_ld, 16 * 10)
            pe.wait_ge(w_lo, 4)

            def tally(k):
                pe.wait_ge(k_cnt, k + 1)
                m_(kps[:], blocks[:], cnt[:], start=True, stop=True).then_inc(k_mm, 1)

            def body(c, par, more):
                pe.wait_ge(x_lo, 2 * (c + 1))
                for m in range(MS):
                    n = MS * c + m
                    b = (MS * par + m) % 2
                    for i, (ps, s) in enumerate(((gps[b], g_ev), (ups[b], h_ev))):
                        wait(pe, s, n - 1)
                        for k, (wk, xp, xk) in enumerate(PARTS):
                            ins = m_(ps[:], wsp[:, i, wk, m * 128:(m + 1) * 128], xsp[:, par, xp, xk], start=k == 0, stop=k == 4)
                        ins.then_inc(gu_mm, 1)
                    if m == 0:
                        tally(2 * c)
                tally(2 * c + 1)
                pe.wait_ge(h_ev, MS * (c + 1))
                for i in range(2):
                    wait(pe, y_ev, 2 * (c - 1) + i + 1)
                    for t in range(2):
                        for m in range(MS):
                            ins = m_(dps[i][:, t], hT[:, m, (2 * i + t) * TP:(2 * i + t + 1) * TP], wd[:, m], start=m == 0, stop=m == MS - 1)
                    ins.then_inc(d_mm, 1)

            chunks(pe, body)
            pe.wait_ge(r_ch, 1)
            m_(kps[:], blocks[:], cnt[:], start=True, stop=True).then_inc(r_mm, 1)
            pe.wait_ge(r_ch, 4)
            m_(kps[:], before[:], run[:, SPAN - 1:SPAN], start=True, stop=True).then_inc(r_mm, 1)
            pe.wait_ge(r_ch, 8)
            m_(kps[:], before[:], run[:, SPAN - 1:SPAN], start=True, stop=True).then_inc(r_mm, 1)
            for i in range(2):
                pe.wait_ge(r_ch, 11 + i)
                for j in range(BLOCKS // 2):
                    b = i * (BLOCKS // 2) + j
                    ins = nc.tensor.transpose(pps[:, j], run[:, b * TP:(b + 1) * TP], ident[:])
                ins.then_inc(r_mm, 1)


def experts(nc, w, xs_d, idx_d, out_d, hi_all, lo_all, sem, n_exp=EXPERTS):
    ctx = ExitStack()

    def sb(name, shape, dt=F32):
        return ctx.enter_context(nc.sbuf_tensor("ex_" + name, shape, dt))

    def pb(name, shape):
        return ctx.enter_context(nc.psum_tensor("exp_" + name, shape, F32))

    CAP_T = CAPACITY // TP
    ME = F_EXP // 128
    HALF = CAPACITY // 2
    HT = HALF // TP

    with ctx:
        ident = sb("ident", [128, 128])
        iota = sb("iota", [TP, LO])
        row = sb("row", [TP, 1])
        tile = sb("tile", [TP, BLOCKS * SPLIT])
        wraw = sb("wraw", [128, 2, 2, F_EXP])
        wsp = sb("wsp", [128, 2, 3, F_EXP], F32R)
        wd = sb("wd", [128, ME, D])
        one_hi = sb("one_hi", [TP, BLOCKS, SPLIT, LO], BF16)
        one_lo = sb("one_lo", [TP, BLOCKS, SPLIT, LO], BF16)
        val = sb("val", [TP, BLOCKS * SPLIT, 2, LO], BF16)
        lst = sb("lst", [LO, LO])
        lsti = sb("lsti", [LO, LO], U32)
        idxg = sb("idxg", [TP, CAP_T], U32)
        idxs = sb("idxs", [TP, CAP_T], U32)
        xg = sb("xg", [TP, CAP_T, SROW])
        gsc = sb("gsc", [TP, CAP_T])
        xsp = sb("xsp", [128, 2, 2, CAPACITY], F32R)
        sg = sb("sg", [128, 2, HALF])
        hT = sb("hT", [128, ME, CAPACITY])
        y = sb("y", [TP, CAP_T, D])
        gps = [pb(f"g{i}", [128, HALF]) for i in range(2)]
        ups = [pb(f"u{i}", [128, HALF]) for i in range(2)]
        dps = [pb(f"d{i}", [TP, 2, D]) for i in range(2)]
        tps = pb("t", [128, HT, TP])
        lps = pb("l", [LO, 2 * LO])

        c_ld = sem("ex_c_ld")
        wgu_ld = sem("ex_wgu_ld")
        w_hi = sem("ex_w_hi")
        w_lo = sem("ex_w_lo")
        t_hi = sem("ex_t_hi")
        wd_ld = sem("ex_wd_ld")
        hot = sem("ex_hot")
        l_mm = sem("ex_l_mm")
        l_ev = sem("ex_l_ev")
        l_st = sem("ex_l_st")
        ig_ld = sem("ex_ig_ld")
        is_ld = sem("ex_is_ld")
        gat = sem("ex_gat")
        t_mm = sem("ex_t_mm")
        t_ev = sem("ex_t_ev")
        sc_ev = sem("ex_sc_ev")
        gu_mm = sem("ex_gu_mm")
        g_ev = sem("ex_g_ev")
        h_ev = sem("ex_h_ev")
        d_mm = sem("ex_d_mm")
        y_ev = sem("ex_y_ev")
        sca = sem("ex_sca")
        UNITS = 2 * ME
        TR = 2 * 2
        WSP = 2 * 2
        DN = CAP_T // 2
        HOT = 4

        def wait(eng, s, value):
            if not isinstance(value, int) or value > 0:
                eng.wait_ge(s, value)

        def turns(eng, body):
            body(0, True, True)
            with eng.Fori(1, n_exp - 2) as e:
                body(e, True, True)
            body(n_exp - 2, True, False)
            body(n_exp - 1, False, False)

        block = ctx.enter_context(nc.Block())

        @block.sync
        def _(sp):
            for dst, src in ((ident[:], w["ident"]), (iota[:], w["iota"]), (row[:], w["row"]), (tile[:], w["tile"])):
                sp.dma_start(dst, src).then_inc(c_ld, 16)

            def load_gu(e):
                wait(sp, w_lo, WSP * e)
                for i, src in enumerate((w["WgT"], w["WuT"])):
                    one = src[bass.ds(e, 1)].rearrange("a d n -> d (a n)")
                    sp.dma_start(wraw[:, i, 0], one[0:128]).then_inc(wgu_ld, 16)
                    for half in range(2):
                        sp.dma_start(wraw[half * 64:half * 64 + 64, i, 1], one[128:D]).then_inc(wgu_ld, 16)

            def load_d(e):
                wait(sp, d_mm, DN * e)
                sp.dma_start(wd[:], w["WdT"][bass.ds(e, 1)].rearrange("a (k p) n -> p (a k) n", p=128)).then_inc(wd_ld, 16)

            def store_list(e):
                wait(sp, l_ev, 2 * e + 2)
                sp.dma_start(idx_d[bass.ds(e, 1), :].rearrange("a (p n) -> p (a n)", n=LO), lsti[:]).then_inc(l_st, 16)

            def load_idx(dst, s, e):
                wait(sp, l_st, 16 * (e + 1))
                sp.dma_start(dst[:], idx_d[bass.ds(e, 1), 0:CAPACITY].rearrange("a (p t) -> p (a t)", t=CAP_T)).then_inc(s, 16)

            load_gu(0)
            load_d(0)
            store_list(0)
            load_idx(idxg, ig_ld, 0)
            store_list(1)

            def body(e, more, lists):
                if more:
                    wait(sp, gat, 16 * CAP_T * (e + 1))
                    load_idx(idxg, ig_ld, e + 1)
                apart(sp, (c_ld, 64), (l_st, 16 * (e + 1)), (sca, 16 * CAP_T * e))
                load_idx(idxs, is_ld, e)
                if more:
                    load_gu(e + 1)
                if lists:
                    store_list(e + 2)
                if more:
                    load_d(e + 1)

            turns(sp, body)

        @block.gpsimd
        def _(pool):
            g = nc.gpsimd
            last = pool.to_reg(TOKENS - 1)

            def gather(e):
                apart(pool, (c_ld, 64), (ig_ld, 16 * (e + 1)), (t_mm, TR * e), (sc_ev, e))
                for t in range(CAP_T):
                    g.indirect_dma_start(xg[:, t], None, xs_d[:, :], bass.IndirectOffsetOnAxis(idxg[:, t:t + 1], 0),
                                         bounds_check=last).then_inc(gat, 16)

            gather(0)

            def body(e, more, lists):
                if more:
                    gather(e + 1)
                for t in range(CAP_T):
                    apart(pool, (c_ld, 64), *[(is_ld, 16 * (e + 1))] * (t == 0), *[(y_ev, DN * e + t // 2 + 1)] * (t % 2 == 0),
                               (sca, 16 * (CAP_T * e + t)))
                    g.indirect_dma_start(out_d[:, :], bass.IndirectOffsetOnAxis(idxs[:, t:t + 1], 0), y[:, t], None,
                                         bounds_check=last, compute_op=ALU.add).then_inc(sca, 16)

            turns(pool, body)
            pool.wait_ge(sca, 16 * CAP_T * n_exp)

        @block.scalar
        def _(act):
            a = nc.scalar

            def weights_high(e):
                act.wait_ge(wgu_ld, 96 * (e + 1))
                wait(act, gu_mm, 2 * UNITS * e)
                for i in range(2):
                    a.activation(wsp[:, i, 0], wraw[:, i, 0], ACT.Copy).then_inc(w_hi, 1)
                    a.activation(wsp[:, i, 2], wraw[:, i, 1], ACT.Copy).then_inc(w_hi, 1)

            def rows_high(e, j):
                act.wait_ge(t_mm, TR * e + j + 1)
                k, half = j % 2, j // 2
                a.activation(xsp[:, 0, k, half * HALF:(half + 1) * HALF], tps[:].rearrange("p t n -> p (t n)"), ACT.Copy).then_inc(t_hi, 1)

            weights_high(0)
            for j in range(TR):
                rows_high(0, j)

            def body(e, more, lists):
                for n in range(UNITS):
                    act.wait_ge(gu_mm, 2 * (UNITS * e + n) + 1)
                    wait(act, h_ev, UNITS * e + n - 1)
                    a.activation(sg[:, n % 2], gps[n % 2][:], ACT.Silu).then_inc(g_ev, 1)
                if more:
                    for j in range(TR):
                        rows_high(e + 1, j)
                        if j == 0:
                            weights_high(e + 1)

            turns(act, body)

        @block.vector
        def _(dve):
            v = nc.vector
            dve.wait_ge(c_ld, 64)

            def one_hots(e, step):
                shape = [TP, BLOCKS, SPLIT, LO]
                own = bass.ds(e * SPLIT, SPLIT)
                io = iota[:].rearrange("p (a b n) -> p a b n", a=1, b=1).to_broadcast(shape)
                flat = one_lo[:].rearrange("p a b n -> p (a b) n")
                if step == 0:
                    wait(dve, l_mm, e)
                    v.tensor_tensor(one_hi[:], hi_all[:, :, own].rearrange("p a (b n) -> p a b n", n=1).to_broadcast(shape), io, ALU.is_equal).then_inc(hot, 1)
                if step == 1:
                    v.tensor_tensor(one_lo[:], lo_all[:, :, own].rearrange("p a (b n) -> p a b n", n=1).to_broadcast(shape), io, ALU.is_equal).then_inc(hot, 1)
                if step == 2:
                    dve.wait_ge(hot, HOT * e + 2)
                    v.tensor_scalar(val[:, :, 0], flat, row[:, 0:1], None, ALU.mult).then_inc(hot, 1)
                if step == 3:
                    v.tensor_tensor(val[:, :, 1], flat, tile[:].rearrange("p (a n) -> p a n", n=1).to_broadcast([TP, BLOCKS * SPLIT, LO]), ALU.mult).then_inc(hot, 1)

            def list_out(e):
                dve.wait_ge(l_mm, e + 1)
                wait(dve, l_st, 16 * e)
                v.tensor_copy(lst[:], lps[:, 0:LO]).then_inc(l_ev, 1)
                dve.wait_ge(l_ev, 2 * e + 1)
                v.scalar_tensor_tensor(out=lsti[:], in0=lps[:, LO:2 * LO], scalar=float(TP), in1=lst[:], op0=ALU.mult, op1=ALU.add).then_inc(l_ev, 1)

            def rows_in(e, j):
                dve.wait_ge(t_mm, TR * e + j + 1)
                k, half = j % 2, j // 2
                dve.wait_ge(t_hi, TR * e + j + 1)
                part = slice(half * HALF, (half + 1) * HALF)
                v.tensor_tensor(xsp[:, 1, k, part], tps[:].rearrange("p t n -> p (t n)"), xsp[:, 0, k, part].bitcast(F32), ALU.subtract).then_inc(t_ev, 1)

            def weights_low(e, j):
                i, k = j // 2, j % 2
                dve.wait_ge(w_hi, WSP * e + j + 1)
                half = slice(0, 128) if k == 0 else slice(64, 128)
                v.tensor_tensor(wsp[half, i, 1 + k], wraw[half, i, k], wsp[half, i, 2 * k].bitcast(F32), ALU.subtract).then_inc(w_lo, 1)

            def scores_in(e):
                dve.wait_ge(gat, 16 * CAP_T * (e + 1))
                wait(dve, y_ev, DN * e)
                v.tensor_copy(gsc[:], xg[:, :, bass.ds(2 * 128 + e, 1)].rearrange("p t n -> p (t n)")).then_inc(sc_ev, 1)

            for step in range(HOT):
                one_hots(0, step)
            list_out(0)
            for step in range(HOT):
                one_hots(1, step)
            list_out(1)
            for j in range(TR):
                weights_low(0, j)
                rows_in(0, j)
            scores_in(0)

            def body(e, more, lists):
                for n in range(UNITS):
                    dve.wait_ge(gu_mm, 2 * (UNITS * e + n) + 2)
                    dve.wait_ge(g_ev, UNITS * e + n + 1)
                    wait(dve, d_mm, DN * e)
                    m, half = n % ME, n // ME
                    v.tensor_tensor(hT[:, m, half * HALF:(half + 1) * HALF], sg[:, n % 2], ups[n % 2][:], ALU.mult).then_inc(h_ev, 1)
                    if lists and n >= UNITS - 2 * HOT and n % 2 == 0:
                        one_hots(e + 2, (n - UNITS + 2 * HOT) // 2)
                for j in range(DN):
                    if more:
                        rows_in(e + 1, j)
                        weights_low(e + 1, j)
                    if j == 0:
                        dve.wait_ge(sc_ev, e + 1)
                        wait(dve, sca, 16 * CAP_T * e)
                    dve.wait_ge(d_mm, DN * e + j + 1)
                    for i in range(2):
                        t = 2 * j + i
                        ins = v.tensor_scalar(y[:, t], dps[j % 2][:, i], gsc[:, t:t + 1], None, ALU.mult)
                    ins.then_inc(y_ev, 1)
                if more:
                    dve.wait_ge(y_ev, DN * (e + 1))
                    scores_in(e + 1)
                if lists:
                    list_out(e + 2)

            turns(dve, body)

        @block.tensor
        def _(pe):
            m_ = nc.tensor.matmul
            pe.wait_ge(c_ld, 64)

            def list_mm(e):
                pe.wait_ge(hot, HOT * (e + 1))
                wait(pe, l_ev, 2 * e)
                for b in range(BLOCKS):
                    for c in range(SPLIT):
                        n = b * SPLIT + c
                        ins = m_(lps[:], one_hi[:, b, c], val[:, n].rearrange("p a n -> p (a n)"), start=n == 0, stop=n == BLOCKS * SPLIT - 1)
                ins.then_inc(l_mm, 1)

            def rows_T(e, j):
                k, half = j % 2, j // 2
                if j == 0:
                    pe.wait_ge(gat, 16 * CAP_T * (e + 1))
                wait(pe, t_ev, TR * e + j)
                for t in range(HT):
                    ins = nc.tensor.transpose(tps[:, t], xg[:, half * HT + t, k * 128:(k + 1) * 128], ident[0:TP, 0:TP])
                ins.then_inc(t_mm, 1)

            list_mm(0)
            list_mm(1)
            for j in range(TR):
                rows_T(0, j)

            def body(e, more, lists):
                pe.wait_ge(w_lo, WSP * (e + 1))
                pe.wait_ge(t_ev, TR * (e + 1))
                for n in range(UNITS):
                    m, half = n % ME, n // ME
                    for i, (ps, s) in enumerate(((gps, g_ev), (ups, h_ev))):
                        wait(pe, s, UNITS * e + n - 1)
                        for k, (wk, xp, xk) in enumerate(PARTS):
                            ins = m_(ps[n % 2][:], wsp[:, i, wk, m * 128:(m + 1) * 128], xsp[:, xp, xk, half * HALF:(half + 1) * HALF], start=k == 0, stop=k == 4)
                        ins.then_inc(gu_mm, 1)
                pe.wait_ge(wd_ld, 16 * (e + 1))
                for j in range(DN):
                    if more:
                        rows_T(e + 1, j)
                    if j == 0:
                        pe.wait_ge(h_ev, UNITS * (e + 1))
                    wait(pe, y_ev, DN * e + j - 1)
                    for i in range(2):
                        t = 2 * j + i
                        for m in range(ME):
                            ins = m_(dps[j % 2][:, i], hT[:, m, t * TP:(t + 1) * TP], wd[:, m], start=m == 0, stop=m == ME - 1)
                    ins.then_inc(d_mm, 1)
                if lists:
                    list_mm(e + 2)

            turns(pe, body)


def audio_tower(nc, w, out_d):
    def scratch(name, shape, dt=F32):
        return nc.dram_tensor(name, shape, dt, kind="Internal").ap()

    hx_d = scratch("hx_d", (TOKENS, 2 * D))
    bias_d = scratch("bias_d", (HEADS, FRAMES, PITCH))
    h1_d = scratch("h1_d", (TOKENS, D))
    xs_d = scratch("xs_d", (TOKENS, SROW))
    xnT_d = scratch("xnT_d", (D, TOKENS))
    scT_d = scratch("scT_d", (EXPERTS, TOKENS))
    idx_d = scratch("idx_d", (EXPERTS, LO * LO), U32)
    with ExitStack() as ctx:
        def sem(name):
            return ctx.enter_context(nc.semaphore(name))

        tower(nc, w, hx_d, bias_d, h1_d, xs_d, xnT_d, scT_d, sem)
        hi_all = ctx.enter_context(nc.sbuf_tensor("hi_all", [TP, BLOCKS, 128], I32))
        lo_all = ctx.enter_context(nc.sbuf_tensor("lo_all", [TP, BLOCKS, 128], I32))
        shared_and_route(nc, w, h1_d, xnT_d, scT_d, out_d, hi_all, lo_all, sem)
        experts(nc, w, xs_d, idx_d, out_d, hi_all, lo_all, sem)


def constants():
    block, part = np.divmod(np.arange(BLOCKS * SPLIT), SPLIT)
    return {
        "ident": np.eye(128, dtype=np.float32), "dft": dft_table(), "basis": basis_table(),
        "blocks": expert_blocks(), "before": expert_before(),
        "iota": np.tile(np.arange(LO, dtype=np.float32), (TP, 1)),
        "row": np.arange(TP, dtype=np.float32)[:, None],
        "tile": np.tile((part * BLOCKS + block).astype(np.float32), (TP, 1)),
    }


def layout(i):
    a, f, t = "L0_attn_", "L0_ffn_", "L0_tok_"
    framed = i["x"][:, :FRAMES * FRAME_STEP].reshape(BATCH, FRAMES, FRAME_STEP)[:, :, :FRAME_LEN]
    return {
        "frames": framed.transpose(2, 0, 1).reshape(FRAME_LEN, TOKENS),
        "melT": i[t + "mel_filters"].T, "dctT": i[t + "dct"].T,
        "w_proj": i[t + "w_proj"], "b_proj": i[t + "b_proj"].reshape(1, D),
        "wq": i[a + "wq"], "wk": i[a + "wk"], "wv": i[a + "wv"], "wo": i[a + "wo"],
        "w1": i[a + "w1"], "w2": i[a + "w2"], "b2": i[a + "b2"], "bo": i[a + "bo"],
        "n1w": np.stack([i[a + "norm1_w"][:128], np.tile(i[a + "norm1_w"][128:], 2)], 1), "n2w": np.stack([i[a + "norm2_w"][:128], np.tile(i[a + "norm2_w"][128:], 2)], 1),
        "b1": i[a + "b1"].reshape(DFF // 128, 128).T,
        "u": i[a + "u_param"].reshape(PAIRS, 128).T, "v": i[a + "v_param"].reshape(PAIRS, 128).T,
        "w_pos": i[a + "w_pos"].reshape(HEADS * DK, N_POS),
        "gateT": i[f + "gate_weight"].T,
        "WsgT": i[f + "Ws_g"].T, "WsuT": i[f + "Ws_u"].T, "WsdT": i[f + "Ws_d"].T,
        "WgT": i[f + "Wg"].transpose(0, 2, 1), "WuT": i[f + "Wu"].transpose(0, 2, 1),
        "WdT": i[f + "Wd"].transpose(0, 2, 1),
    }


def kernel(**inputs):
    import concourse.bacc as bacc
    from concourse.bass_utils import run_bass_kernel_spmd

    nc = bacc.Bacc("TRN2", target_bir_lowering=False, num_devices=1)
    arrays = {k: np.ascontiguousarray(v) for k, v in {**layout(inputs), **constants()}.items()}
    w = {k: nc.dram_tensor(k, v.shape, mybir.dt.from_np(v.dtype), kind="ExternalInput").ap() for k, v in arrays.items()}
    out_d = nc.dram_tensor("out", (TOKENS, D), F32, kind="ExternalOutput").ap()
    audio_tower(nc, w, out_d)
    r = run_bass_kernel_spmd(nc, [arrays], core_ids=[0])
    return r.results[0]["out"].reshape(BATCH, FRAMES, D)
```
